# Optimizing a Trainium2 kernel written in Bass

```python
import numpy as np
import jax
import jax.numpy as jnp

def _softmax(x, axis=-1):
    return jax.nn.softmax(x, axis=axis)

def _gelu(x):
    return jax.nn.gelu(x, approximate=True)

def _silu(x):
    return jax.nn.silu(x)

def _sigmoid(x):
    return jax.nn.sigmoid(x)

def _layernorm(x, axis=-1, eps=1e-05):
    m = jnp.mean(x, axis=axis, keepdims=True)
    v = jnp.var(x, axis=axis, keepdims=True)
    return (x - m) / jnp.sqrt(v + eps)

def _scatter_add(tgt, idx, src, axis=0):
    return tgt.at[idx].add(src)

def _segment_sum(src, seg, n):
    return jax.ops.segment_sum(src, seg, n)
kernel_name = 'mk_decoder_postln_d4_seqx_r4_c3a37c'

def setup_inputs(seed: int=0):
    np.random.seed(seed)
    _w = jnp.asarray

    def _rec_inputs():
        import jax
        import jax.numpy as jnp
        _rk = jax.random.key(seed)
        x = 7.22e-05 + 1 * jax.random.normal(jax.random.fold_in(_rk, 1), (8, 256, 256), jnp.float32)
        _lenS = 256 - jax.random.randint(jax.random.fold_in(_rk, 7), (8,), 0, max(1, 256 // 4) + 1, jnp.int32)
        _lenS2 = 120 - jax.random.randint(jax.random.fold_in(_rk, 8), (8,), 0, max(1, 120 // 4) + 1, jnp.int32)
        _ctx_1024P = jax.random.normal(jax.random.fold_in(_rk, 11), (8, 16, 256), jnp.float32)
        _ctx_1024c = jax.random.dirichlet(jax.random.fold_in(_rk, 511), 0.3 * jnp.ones((16,), jnp.float32), (8, 120))
        _ctx_1024t = jnp.einsum('bsk,bkd->bsd', _ctx_1024c, _ctx_1024P)
        _ctx_1024t = _ctx_1024t * jax.lax.rsqrt(jnp.mean(jnp.square(_ctx_1024t)) + 1e-12) * 0.953939
        ctx_1024 = -0.000514642 + 1.00011 * (_ctx_1024t + 0.3 * jax.random.normal(jax.random.fold_in(_rk, 611), (8, 120, 256), jnp.float32))
        _validS = jnp.arange(256)[None, :] < _lenS[:, None]
        _validS2 = jnp.arange(120)[None, :] < _lenS2[:, None]
        _causal = jnp.tril(jnp.ones((256, 256), dtype=bool))
        mask_Bx16xSxS2_bk1 = jnp.broadcast_to(_validS2[:, None, None, :], (8, 16, 256, 120))
        mask_SxS2_bk0 = jnp.logical_not(jnp.broadcast_to(_validS2[0:1, :], (256, 120)))
        return (x, ctx_1024, mask_Bx16xSxS2_bk1, mask_SxS2_bk0)
    x, ctx_1024, mask_Bx16xSxS2_bk1, mask_SxS2_bk0 = _rec_inputs()

    def _L0_attn_setup():
        import jax, jax.numpy as jnp
        import numpy as np
        T, B, D = (256, 32, 256)
        N_STATE, BLOCK = (256, 8)
        NB = N_STATE // BLOCK

        def _xavier(key, shape):
            fan_out, fan_in = shape
            a = (6.0 / (fan_in + fan_out)) ** 0.5
            return jax.random.uniform(key, shape, jnp.float32, -a, a)
        key = jax.random.key(seed)
        kx, kk, kv, kq = jax.random.split(key, 4)
        return {'x': jax.random.normal(kx, (T, B, D), jnp.float32), 'W_k': _xavier(kk, (N_STATE, D)), 'W_v': _xavier(kv, (N_STATE, D)), 'W_q': _xavier(kq, (N_STATE, D))}
    _L0_attn_all = _L0_attn_setup()
    _L0_attn_in = {k: v for k, v in _L0_attn_all.items() if k in ('W_k', 'W_v', 'W_q')}
    del _L0_attn_all

    def _L0_xattn_setup():
        import jax, jax.numpy as jnp
        import numpy as np
        B, L_ENC, L_DEC, D = (16, 128, 128, 256)
        key = jax.random.key(seed)
        k1, k2, k3, k4, k5, k6 = jax.random.split(key, 6)
        encoder_hc = jax.random.normal(k1, (B, L_ENC, D), dtype=jnp.float32)
        decoder_hq = jax.random.normal(k2, (B, L_DEC, D), dtype=jnp.float32)
        w_sim = jax.random.normal(k3, (3 * D,), dtype=jnp.float32) * 0.02
        b_sim = jax.random.normal(k4, (1,), dtype=jnp.float32) * 0.02
        W_qv = jax.random.normal(k5, (4 * D, D), dtype=jnp.float32) * 0.02
        b_qv = jax.random.normal(k6, (D,), dtype=jnp.float32) * 0.02
        return {'encoder_hc': encoder_hc, 'decoder_hq': decoder_hq, 'w_sim': w_sim, 'b_sim': b_sim, 'W_qv': W_qv, 'b_qv': b_qv}
    _L0_xattn_all = _L0_xattn_setup()
    _L0_xattn_in = {k: v for k, v in _L0_xattn_all.items() if k in ('w_sim', 'b_sim', 'W_qv', 'b_qv')}
    del _L0_xattn_all

    def _L0_ffn_setup():
        import jax, jax.numpy as jnp
        import numpy as np
        ALPHA = 1.0
        key = jax.random.key(seed)
        ks = jax.random.split(key, 7)
        B, S, IN, OUT = (8, 2048, 256, 256)
        RANK, DDIM, UDIM = (4, 100, 50)
        return {'hidden_states': jax.random.normal(ks[0], (B, S, IN), dtype=jnp.float32), 'W': jax.random.normal(ks[1], (OUT, IN), dtype=jnp.float32) * 0.02, 'b': jax.random.normal(ks[2], (OUT,), dtype=jnp.float32) * 0.02, 'lora_down': jax.random.normal(ks[3], (RANK, DDIM), dtype=jnp.float32) * 0.1, 'lora_up': jax.random.normal(ks[4], (UDIM, RANK), dtype=jnp.float32) * 0.1, 'down_aux': jax.random.normal(ks[5], (DDIM, IN), dtype=jnp.float32) * 0.03, 'up_aux': jax.random.normal(ks[6], (OUT, UDIM), dtype=jnp.float32) * 0.03}
    _L0_ffn_all = _L0_ffn_setup()
    _L0_ffn_in = {k: v for k, v in _L0_ffn_all.items() if k in ('W', 'b', 'lora_down', 'lora_up', 'down_aux', 'up_aux')}
    del _L0_ffn_all

    def _L1_attn_setup():
        import jax, jax.numpy as jnp
        import numpy as np
        B, S, E, H, BS = (4, 1024, 256, 256, 128)
        key = jax.random.key(seed)
        k1, k2, k3, k4 = jax.random.split(key, 4)
        x = jax.random.normal(k1, (B, S, E), dtype=jnp.float32)
        W_qkv = jax.random.normal(k2, (E, 3 * H), dtype=jnp.float32) * E ** (-0.5)
        W_out = jax.random.normal(k3, (H, H), dtype=jnp.float32) * H ** (-0.5)
        b_out = jax.random.normal(k4, (H,), dtype=jnp.float32) * 0.01
        return {'x': x, 'W_qkv': W_qkv, 'W_out': W_out, 'b_out': b_out}
    _L1_attn_all = _L1_attn_setup()
    _L1_attn_in = {k: v for k, v in _L1_attn_all.items() if k in ('W_qkv', 'W_out', 'b_out')}
    del _L1_attn_all

    def _L1_xattn_setup():
        import jax, jax.numpy as jnp
        import numpy as np
        import math
        B, S, D, H = (2, 512, 256, 16)
        DH = D // H
        key = jax.random.key(seed)
        ks = jax.random.split(key, 13)
        sc = 1.0 / math.sqrt(D)
        return {'q': jax.random.normal(ks[0], (B, S, D), jnp.float32), 'k': jax.random.normal(ks[1], (B, S, D), jnp.float32), 'v': jax.random.normal(ks[2], (B, S, D), jnp.float32), 'mask': jax.random.randint(ks[3], (B, H, S, S), 0, 2) == 1, 'Wq': jax.random.normal(ks[4], (D, D), jnp.float32) * sc, 'bq': jnp.zeros((D,), jnp.float32), 'Wk': jax.random.normal(ks[5], (D, D), jnp.float32) * sc, 'bk': jnp.zeros((D,), jnp.float32), 'Wv': jax.random.normal(ks[6], (D, D), jnp.float32) * sc, 'bv': jnp.zeros((D,), jnp.float32), 'Wo': jax.random.normal(ks[7], (D, D), jnp.float32) * sc, 'bo': jnp.zeros((D,), jnp.float32)}
    _L1_xattn_all = _L1_xattn_setup()
    _L1_xattn_in = {k: v for k, v in _L1_xattn_all.items() if k in ('Wq', 'bq', 'Wk', 'bk', 'Wv', 'bv', 'Wo', 'bo')}
    del _L1_xattn_all

    def _L1_ffn_setup():
        import jax, jax.numpy as jnp
        import numpy as np
        BLOCK = 32
        W_BITS = 4
        ACT_BITS = 16

        def act_qdq(x):
            qmax = 2.0 ** (ACT_BITS - 1) - 1.0
            scale = jnp.maximum(jnp.max(jnp.abs(x)) / qmax, 1e-12)
            return jnp.clip(jnp.round(x / scale), -qmax - 1.0, qmax) * scale

        def fixed_qdq_u16(x):
            scale = 1.0 / 65536.0
            return jnp.clip(jnp.round(x / scale), 0.0, 65535.0) * scale

        def lpbq_dequant(w):
            O, I = w.shape
            qmax = 2.0 ** (W_BITS - 1) - 1.0
            wb = w.reshape(O, I // BLOCK, BLOCK)
            s = jnp.maximum(jnp.max(jnp.abs(wb), axis=-1, keepdims=True) / qmax, 1e-12)
            wq = jnp.clip(jnp.round(wb / s), -qmax - 1.0, qmax) * s
            return wq.reshape(O, I)
        key = jax.random.key(seed)
        k1, k2, k3, k4 = jax.random.split(key, 4)
        B, S, H, I = (2, 1024, 256, 768)
        x = jax.random.normal(k1, (B, S, H), jnp.float32)
        w_gate = jax.random.normal(k2, (I, H), jnp.float32) * 0.02
        w_up = jax.random.normal(k3, (I, H), jnp.float32) * 0.02
        w_down = jax.random.normal(k4, (H, I), jnp.float32) * 0.02
        return {'x': x, 'w_gate': w_gate, 'w_up': w_up, 'w_down': w_down}
    _L1_ffn_all = _L1_ffn_setup()
    _L1_ffn_in = {k: v for k, v in _L1_ffn_all.items() if k in ('w_gate', 'w_up', 'w_down')}
    del _L1_ffn_all

    def _L2_attn_setup():
        import jax, jax.numpy as jnp
        import numpy as np
        HEADS, D_MODEL, D_V = (16, 256, 64)
        D_K = D_MODEL // HEADS
        key = jax.random.key(seed)
        k1, k2, k3, k4, k5 = jax.random.split(key, 5)
        B, T = (2, 512)
        s = 1.0 / np.sqrt(D_MODEL)
        return {'x': jax.random.normal(k1, (B, T, D_MODEL), dtype=jnp.float32), 'Wq': jax.random.normal(k2, (D_MODEL, HEADS * D_K), dtype=jnp.float32) * s, 'Wk': jax.random.normal(k3, (D_MODEL, HEADS * D_K), dtype=jnp.float32) * s, 'Wv': jax.random.normal(k4, (D_MODEL, HEADS * D_V), dtype=jnp.float32) * s, 'Wo': jax.random.normal(k5, (HEADS * D_V, D_MODEL), dtype=jnp.float32) * (1.0 / np.sqrt(HEADS * D_V))}
    _L2_attn_all = _L2_attn_setup()
    _L2_attn_in = {k: v for k, v in _L2_attn_all.items() if k in ('Wq', 'Wk', 'Wv', 'Wo')}
    del _L2_attn_all

    def _L2_xattn_setup():
        import jax, jax.numpy as jnp
        import numpy as np
        B, S, DIM, H = (4, 512, 256, 16)
        HD = DIM // H
        SCALE = HD ** (-0.5)

        def _heads(x):
            b, s, _ = x.shape
            return x.reshape(b, s, H, HD).transpose(0, 2, 1, 3)
        key = jax.random.key(seed)
        ks = jax.random.split(key, 7)
        init = 0.02
        return {'query': jax.random.normal(ks[0], (B, S, DIM), dtype=jnp.float32), 'key': jax.random.normal(ks[1], (B, S, DIM), dtype=jnp.float32), 'value': jax.random.normal(ks[2], (B, S, DIM), dtype=jnp.float32), 'attn_mask': jnp.tril(jnp.ones((S, S), dtype=bool)), 'Wq': jax.random.normal(ks[3], (DIM, DIM), dtype=jnp.float32) * init, 'Wk': jax.random.normal(ks[4], (DIM, DIM), dtype=jnp.float32) * init, 'Wv': jax.random.normal(ks[5], (DIM, DIM), dtype=jnp.float32) * init, 'Wo': jax.random.normal(ks[6], (DIM, DIM), dtype=jnp.float32) * init}
    _L2_xattn_all = _L2_xattn_setup()
    _L2_xattn_in = {k: v for k, v in _L2_xattn_all.items() if k in ('Wq', 'Wk', 'Wv', 'Wo')}
    del _L2_xattn_all

    def _L2_ffn_setup():
        import jax, jax.numpy as jnp
        import numpy as np
        EPS = 1e-05

        def _quantize(W):
            gamma = jnp.mean(jnp.abs(W))
            return jnp.clip(jnp.round(W / (gamma + EPS)), -1.0, 1.0)
        key = jax.random.key(seed)
        k_x, k_w1, k_b1, k_w2, k_b2 = jax.random.split(key, 5)
        n_embd = 256
        d_ff = 4 * n_embd
        B, S = (4, 1024)
        bound1 = 1.0 / np.sqrt(n_embd)
        bound2 = 1.0 / np.sqrt(d_ff)
        x = jax.random.normal(k_x, (B, S, n_embd), dtype=jnp.float32)
        W1 = jax.random.uniform(k_w1, (d_ff, n_embd), jnp.float32, -bound1, bound1)
        b1 = jax.random.uniform(k_b1, (d_ff,), jnp.float32, -bound1, bound1)
        W2 = jax.random.uniform(k_w2, (n_embd, d_ff), jnp.float32, -bound2, bound2)
        b2 = jax.random.uniform(k_b2, (n_embd,), jnp.float32, -bound2, bound2)
        return {'x': x, 'W1': W1, 'b1': b1, 'W2': W2, 'b2': b2}
    _L2_ffn_all = _L2_ffn_setup()
    _L2_ffn_in = {k: v for k, v in _L2_ffn_all.items() if k in ('W1', 'b1', 'W2', 'b2')}
    del _L2_ffn_all

    def _L3_attn_setup():
        import jax, jax.numpy as jnp
        import numpy as np
        EMBED_DIM = 256
        NUM_HEADS = 16
        HEAD_DIM = EMBED_DIM // NUM_HEADS
        ROPE_BASE = 10000.0

        def rotate_half(x):
            d = x.shape[-1] // 2
            x1, x2 = (x[..., :d], x[..., d:])
            return jnp.concatenate((-x2, x1), axis=-1)
        key = jax.random.key(seed)
        k_x, k_wqkv, k_bqkv, k_wo, k_bo = jax.random.split(key, 5)
        C = EMBED_DIM
        x = jax.random.normal(k_x, (4, 512, C), dtype=jnp.float32)
        s = 1.0 / np.sqrt(C)
        W_qkv = jax.random.uniform(k_wqkv, (C, 3 * C), minval=-s, maxval=s, dtype=jnp.float32)
        b_qkv = jax.random.uniform(k_bqkv, (3 * C,), minval=-s, maxval=s, dtype=jnp.float32)
        W_out = jax.random.uniform(k_wo, (C, C), minval=-s, maxval=s, dtype=jnp.float32)
        b_out = jax.random.uniform(k_bo, (C,), minval=-s, maxval=s, dtype=jnp.float32)
        return {'x': x, 'W_qkv': W_qkv, 'b_qkv': b_qkv, 'W_out': W_out, 'b_out': b_out}
    _L3_attn_all = _L3_attn_setup()
    _L3_attn_in = {k: v for k, v in _L3_attn_all.items() if k in ('W_qkv', 'b_qkv', 'W_out', 'b_out')}
    del _L3_attn_all

    def _L3_xattn_setup():
        import jax, jax.numpy as jnp
        import numpy as np
        key = jax.random.key(seed)
        kq, kk, kv = jax.random.split(key, 3)
        bs, s, d = (16, 512, 256)
        return {'query': jax.random.normal(kq, (bs, s, d), dtype=jnp.float32), 'key': jax.random.normal(kk, (bs, s, d), dtype=jnp.float32), 'value': jax.random.normal(kv, (bs, s, d), dtype=jnp.float32)}
    _L3_xattn_all = _L3_xattn_setup()
    _L3_xattn_in = {k: v for k, v in _L3_xattn_all.items() if k in ()}
    del _L3_xattn_all

    def _L3_ffn_setup():
        import jax, jax.numpy as jnp
        import numpy as np
        B, S, D = (4, 512, 256)
        DFF = 128
        E = 16
        TOP_K = 2
        N_SHARED = 2
        FUSED_DFF = DFF * N_SHARED
        key = jax.random.key(seed)
        ks = jax.random.split(key, 16)
        sc_d = 1.0 / np.sqrt(D)
        sc_f = 1.0 / np.sqrt(DFF)
        sc_sf = 1.0 / np.sqrt(FUSED_DFF)
        inp = {'x': jax.random.normal(ks[0], (B, S, D), dtype=jnp.float32), 'gate_w': jax.random.uniform(ks[1], (E, D), dtype=jnp.float32, minval=-sc_d, maxval=sc_d), 'expert_bias': jnp.zeros((E,), dtype=jnp.float32), 'w1': jax.random.uniform(ks[2], (E, DFF, D), dtype=jnp.float32, minval=-sc_d, maxval=sc_d), 'b1': jax.random.uniform(ks[3], (E, DFF), dtype=jnp.float32, minval=-sc_d, maxval=sc_d), 'w3': jax.random.uniform(ks[4], (E, DFF, D), dtype=jnp.float32, minval=-sc_d, maxval=sc_d), 'b3': jax.random.uniform(ks[5], (E, DFF), dtype=jnp.float32, minval=-sc_d, maxval=sc_d), 'w2': jax.random.uniform(ks[6], (E, D, DFF), dtype=jnp.float32, minval=-sc_f, maxval=sc_f), 'b2': jax.random.uniform(ks[7], (E, D), dtype=jnp.float32, minval=-sc_f, maxval=sc_f), 'sw1': jax.random.uniform(ks[8], (FUSED_DFF, D), dtype=jnp.float32, minval=-sc_d, maxval=sc_d), 'sb1': jax.random.uniform(ks[9], (FUSED_DFF,), dtype=jnp.float32, minval=-sc_d, maxval=sc_d), 'sw3': jax.random.uniform(ks[10], (FUSED_DFF, D), dtype=jnp.float32, minval=-sc_d, maxval=sc_d), 'sb3': jax.random.uniform(ks[11], (FUSED_DFF,), dtype=jnp.float32, minval=-sc_d, maxval=sc_d), 'sw2': jax.random.uniform(ks[12], (D, FUSED_DFF), dtype=jnp.float32, minval=-sc_sf, maxval=sc_sf), 'sb2': jax.random.uniform(ks[13], (D,), dtype=jnp.float32, minval=-sc_sf, maxval=sc_sf)}
        return inp
    _L3_ffn_all = _L3_ffn_setup()
    _L3_ffn_in = {k: v for k, v in _L3_ffn_all.items() if k in ('gate_w', 'expert_bias', 'w1', 'b1', 'w2', 'b2', 'w3', 'b3', 'sw1', 'sb1', 'sw2', 'sb2', 'sw3', 'sb3')}
    del _L3_ffn_all
    return {'x': x, 'ctx_1024': ctx_1024, 'mask_Bx16xSxS2_bk1': mask_Bx16xSxS2_bk1, 'mask_SxS2_bk0': mask_SxS2_bk0, 'L0_attn_W_k': _L0_attn_in['W_k'], 'L0_attn_W_v': _L0_attn_in['W_v'], 'L0_attn_W_q': _L0_attn_in['W_q'], 'L0_xattn_w_sim': _L0_xattn_in['w_sim'], 'L0_xattn_b_sim': _L0_xattn_in['b_sim'], 'L0_xattn_W_qv': _L0_xattn_in['W_qv'], 'L0_xattn_b_qv': _L0_xattn_in['b_qv'], 'L0_ffn_W': _L0_ffn_in['W'], 'L0_ffn_b': _L0_ffn_in['b'], 'L0_ffn_lora_down': _L0_ffn_in['lora_down'], 'L0_ffn_lora_up': _L0_ffn_in['lora_up'], 'L0_ffn_down_aux': _L0_ffn_in['down_aux'], 'L0_ffn_up_aux': _L0_ffn_in['up_aux'], 'L1_attn_W_qkv': _L1_attn_in['W_qkv'], 'L1_attn_W_out': _L1_attn_in['W_out'], 'L1_attn_b_out': _L1_attn_in['b_out'], 'L1_xattn_Wq': _L1_xattn_in['Wq'], 'L1_xattn_bq': _L1_xattn_in['bq'], 'L1_xattn_Wk': _L1_xattn_in['Wk'], 'L1_xattn_bk': _L1_xattn_in['bk'], 'L1_xattn_Wv': _L1_xattn_in['Wv'], 'L1_xattn_bv': _L1_xattn_in['bv'], 'L1_xattn_Wo': _L1_xattn_in['Wo'], 'L1_xattn_bo': _L1_xattn_in['bo'], 'L1_ffn_w_gate': _L1_ffn_in['w_gate'], 'L1_ffn_w_up': _L1_ffn_in['w_up'], 'L1_ffn_w_down': _L1_ffn_in['w_down'], 'L2_attn_Wq': _L2_attn_in['Wq'], 'L2_attn_Wk': _L2_attn_in['Wk'], 'L2_attn_Wv': _L2_attn_in['Wv'], 'L2_attn_Wo': _L2_attn_in['Wo'], 'L2_xattn_Wq': _L2_xattn_in['Wq'], 'L2_xattn_Wk': _L2_xattn_in['Wk'], 'L2_xattn_Wv': _L2_xattn_in['Wv'], 'L2_xattn_Wo': _L2_xattn_in['Wo'], 'L2_ffn_W1': _L2_ffn_in['W1'], 'L2_ffn_b1': _L2_ffn_in['b1'], 'L2_ffn_W2': _L2_ffn_in['W2'], 'L2_ffn_b2': _L2_ffn_in['b2'], 'L3_attn_W_qkv': _L3_attn_in['W_qkv'], 'L3_attn_b_qkv': _L3_attn_in['b_qkv'], 'L3_attn_W_out': _L3_attn_in['W_out'], 'L3_attn_b_out': _L3_attn_in['b_out'], 'L3_ffn_gate_w': _L3_ffn_in['gate_w'], 'L3_ffn_expert_bias': _L3_ffn_in['expert_bias'], 'L3_ffn_w1': _L3_ffn_in['w1'], 'L3_ffn_b1': _L3_ffn_in['b1'], 'L3_ffn_w2': _L3_ffn_in['w2'], 'L3_ffn_b2': _L3_ffn_in['b2'], 'L3_ffn_w3': _L3_ffn_in['w3'], 'L3_ffn_b3': _L3_ffn_in['b3'], 'L3_ffn_sw1': _L3_ffn_in['sw1'], 'L3_ffn_sb1': _L3_ffn_in['sb1'], 'L3_ffn_sw2': _L3_ffn_in['sw2'], 'L3_ffn_sb2': _L3_ffn_in['sb2'], 'L3_ffn_sw3': _L3_ffn_in['sw3'], 'L3_ffn_sb3': _L3_ffn_in['sb3']}

def reference(x, ctx_1024, mask_Bx16xSxS2_bk1, mask_SxS2_bk0, L0_attn_W_k, L0_attn_W_v, L0_attn_W_q, L0_xattn_w_sim, L0_xattn_b_sim, L0_xattn_W_qv, L0_xattn_b_qv, L0_ffn_W, L0_ffn_b, L0_ffn_lora_down, L0_ffn_lora_up, L0_ffn_down_aux, L0_ffn_up_aux, L1_attn_W_qkv, L1_attn_W_out, L1_attn_b_out, L1_xattn_Wq, L1_xattn_bq, L1_xattn_Wk, L1_xattn_bk, L1_xattn_Wv, L1_xattn_bv, L1_xattn_Wo, L1_xattn_bo, L1_ffn_w_gate, L1_ffn_w_up, L1_ffn_w_down, L2_attn_Wq, L2_attn_Wk, L2_attn_Wv, L2_attn_Wo, L2_xattn_Wq, L2_xattn_Wk, L2_xattn_Wv, L2_xattn_Wo, L2_ffn_W1, L2_ffn_b1, L2_ffn_W2, L2_ffn_b2, L3_attn_W_qkv, L3_attn_b_qkv, L3_attn_W_out, L3_attn_b_out, L3_ffn_gate_w, L3_ffn_expert_bias, L3_ffn_w1, L3_ffn_b1, L3_ffn_w2, L3_ffn_b2, L3_ffn_w3, L3_ffn_b3, L3_ffn_sw1, L3_ffn_sb1, L3_ffn_sw2, L3_ffn_sb2, L3_ffn_sw3, L3_ffn_sb3):
    import jax
    import jax.numpy as jnp

    def _L0_attn_ref(x, W_k, W_v, W_q):
        import jax, jax.numpy as jnp
        import numpy as np
        T, B, D = (256, 32, 256)
        N_STATE, BLOCK = (256, 8)
        NB = N_STATE // BLOCK

        def _xavier(key, shape):
            fan_out, fan_in = shape
            a = (6.0 / (fan_in + fan_out)) ** 0.5
            return jax.random.uniform(key, shape, jnp.float32, -a, a)
        T_, B_, D_ = x.shape
        n = W_k.shape[0]
        b = BLOCK
        nb = n // b
        k = jnp.einsum('tbd,nd->tbn', x, W_k).reshape(T_, B_, nb, b)
        v = jnp.einsum('tbd,nd->tbn', x, W_v).reshape(T_, B_, nb, b)
        q = jnp.einsum('tbd,nd->tbn', x, W_q).reshape(T_, B_, nb, b)

        def step(S, kvq):
            k_t, v_t, q_t = kvq
            k_norm = k_t / (jnp.linalg.norm(k_t, axis=-1, keepdims=True) + 1e-06)
            retrieved = jnp.einsum('bnij,bnj->bni', S, k_norm)
            delta = v_t - retrieved
            S_new = jnp.tanh(S + jnp.einsum('bni,bnj->bnij', delta, k_norm))
            Sq = jnp.einsum('bnij,bnj->bni', S_new, q_t).reshape(B_, n)
            out = Sq * jax.nn.silu(Sq)
            return (S_new, out)
        S0 = jnp.zeros((B_, nb, b, b), x.dtype)
        _, outputs = jax.lax.scan(step, S0, (k, v, q))
        return outputs

    def _L0_xattn_ref(encoder_hc, decoder_hq, w_sim, b_sim, W_qv, b_qv):
        import jax, jax.numpy as jnp
        import numpy as np
        B, L_ENC, L_DEC, D = (16, 128, 128, 256)
        d = encoder_hc.shape[-1]
        w1, w2, w3 = (w_sim[:d], w_sim[d:2 * d], w_sim[2 * d:])
        Sim = (encoder_hc @ w1)[:, :, None] + (decoder_hq @ w2)[:, None, :] + jnp.einsum('bid,bjd->bij', encoder_hc * w3, decoder_hq) + b_sim[0]
        A = jax.nn.softmax(Sim, axis=2)
        hq_hat = jnp.einsum('bij,bjd->bid', A, decoder_hq)
        Batt = jax.nn.softmax(jnp.max(Sim, axis=2), axis=1)
        hc_bar = jnp.einsum('bi,bid->bd', Batt, encoder_hc)[:, None, :]
        hc_hat = jnp.broadcast_to(hc_bar, encoder_hc.shape)
        feats = jnp.concatenate([encoder_hc, hq_hat, encoder_hc * hq_hat, encoder_hc * hc_hat], axis=-1)
        hcq = feats @ W_qv + b_qv
        return hcq

    def _L0_ffn_ref(hidden_states, W, b, lora_down, lora_up, down_aux, up_aux):
        import jax, jax.numpy as jnp
        import numpy as np
        ALPHA = 1.0
        lilora_weight = up_aux @ (lora_up @ (lora_down @ down_aux))
        base = jnp.einsum('bsi,oi->bso', hidden_states, W) + b
        delta = jnp.einsum('bsi,oi->bso', hidden_states, lilora_weight)
        return base + ALPHA * delta

    def _L1_attn_ref(x, W_qkv, W_out, b_out):
        import jax, jax.numpy as jnp
        import numpy as np
        B, S, E, H, BS = (4, 1024, 256, 256, 128)
        b, s, e = x.shape
        h = W_out.shape[1]
        nb = s // BS
        qkv = x @ W_qkv
        q, k, v = jnp.split(qkv, 3, axis=-1)

        def blk(t):
            return t.reshape(b, nb, BS, h)
        scale = h ** (-0.5)
        scores = jnp.einsum('bnqd,bnkd->bnqk', blk(q), blk(k)) * scale
        causal = jnp.tril(jnp.ones((BS, BS), dtype=bool))
        scores = jnp.where(causal, scores, -jnp.inf)
        scores = scores - jnp.max(scores, axis=-1, keepdims=True)
        p = jnp.exp(scores)
        p = p / (jnp.sum(p, axis=-1, keepdims=True) + 1e-06)
        out = jnp.einsum('bnqk,bnkd->bnqd', p, blk(v)).reshape(b, s, h)
        return out @ W_out.T + b_out

    def _L1_xattn_ref(q, k, v, mask, Wq, bq, Wk, bk, Wv, bv, Wo, bo):
        import jax, jax.numpy as jnp
        import numpy as np
        import math
        B, S, D, H = (2, 512, 256, 16)
        DH = D // H
        b = q.shape[0]

        def proj(x, W, bias):
            return (x @ W + bias).reshape(b, -1, H, DH).transpose(0, 2, 1, 3)
        qh, kh, vh = (proj(q, Wq, bq), proj(k, Wk, bk), proj(v, Wv, bv))
        scores = jnp.einsum('bhqd,bhkd->bhqk', qh, kh) / math.sqrt(DH)
        scores = jnp.where(mask, -jnp.inf, scores)
        attn = jax.nn.softmax(scores, axis=-1)
        out = jnp.einsum('bhqk,bhkd->bhqd', attn, vh)
        out = out.transpose(0, 2, 1, 3).reshape(b, -1, D)
        return out @ Wo + bo

    def _L1_ffn_ref(x, w_gate, w_up, w_down):
        import jax, jax.numpy as jnp
        import numpy as np
        BLOCK = 32
        W_BITS = 4
        ACT_BITS = 16

        def act_qdq(x):
            qmax = 2.0 ** (ACT_BITS - 1) - 1.0
            scale = jnp.maximum(jnp.max(jnp.abs(x)) / qmax, 1e-12)
            return jnp.clip(jnp.round(x / scale), -qmax - 1.0, qmax) * scale

        def fixed_qdq_u16(x):
            scale = 1.0 / 65536.0
            return jnp.clip(jnp.round(x / scale), 0.0, 65535.0) * scale

        def lpbq_dequant(w):
            O, I = w.shape
            qmax = 2.0 ** (W_BITS - 1) - 1.0
            wb = w.reshape(O, I // BLOCK, BLOCK)
            s = jnp.maximum(jnp.max(jnp.abs(wb), axis=-1, keepdims=True) / qmax, 1e-12)
            wq = jnp.clip(jnp.round(wb / s), -qmax - 1.0, qmax) * s
            return wq.reshape(O, I)
        x = act_qdq(x)
        up = act_qdq(x @ lpbq_dequant(w_up).T)
        gate = act_qdq(x @ lpbq_dequant(w_gate).T)
        sig = fixed_qdq_u16(jax.nn.sigmoid(gate))
        gate = act_qdq(gate * sig)
        o = act_qdq(gate * up)
        return o @ lpbq_dequant(w_down).T

    def _L2_attn_ref(x, Wq, Wk, Wv, Wo):
        import jax, jax.numpy as jnp
        import numpy as np
        HEADS, D_MODEL, D_V = (16, 256, 64)
        D_K = D_MODEL // HEADS
        B, T, _ = x.shape
        scale = jnp.asarray(np.sqrt(D_K), x.dtype)
        q = (x @ Wq).reshape(B, T, HEADS, D_K).transpose(0, 2, 1, 3)
        k = (x @ Wk).reshape(B, T, HEADS, D_K).transpose(0, 2, 1, 3)
        v = (x @ Wv).reshape(B, T, HEADS, D_V).transpose(0, 2, 1, 3)
        scores = jnp.einsum('bhqd,bhkd->bhqk', q, k) / scale
        causal = jnp.triu(jnp.ones((T, T), dtype=bool), k=1)
        scores = jnp.where(causal, jnp.asarray(-jnp.inf, scores.dtype), scores)
        attn = jax.nn.softmax(scores, axis=-1)
        ctx = jnp.einsum('bhqk,bhkd->bhqd', attn, v)
        out = ctx.transpose(0, 2, 1, 3).reshape(B, T, HEADS * D_V)
        return out @ Wo

    def _L2_xattn_ref(query, key, value, attn_mask, Wq, Wk, Wv, Wo):
        import jax, jax.numpy as jnp
        import numpy as np
        B, S, DIM, H = (4, 512, 256, 16)
        HD = DIM // H
        SCALE = HD ** (-0.5)

        def _heads(x):
            b, s, _ = x.shape
            return x.reshape(b, s, H, HD).transpose(0, 2, 1, 3)
        q = _heads(query @ Wq.T)
        k = _heads(key @ Wk.T)
        v = _heads(value @ Wv.T)
        logits = jnp.einsum('bhqd,bhkd->bhqk', q, k) * SCALE
        mask = attn_mask[None, None, :, :]
        masked = jnp.where(mask, logits, -1000000000.0)
        weights = jax.nn.softmax(masked, axis=-1)
        weights = weights * mask.astype(weights.dtype)
        denom = jnp.maximum(weights.sum(axis=-1, keepdims=True), 1e-09)
        weights = weights / denom
        out = jnp.einsum('bhqk,bhkd->bhqd', weights, v)
        out = out.transpose(0, 2, 1, 3).reshape(query.shape[0], query.shape[1], -1)
        return out @ Wo.T

    def _L2_ffn_ref(x, W1, b1, W2, b2):
        import jax, jax.numpy as jnp
        import numpy as np
        EPS = 1e-05

        def _quantize(W):
            gamma = jnp.mean(jnp.abs(W))
            return jnp.clip(jnp.round(W / (gamma + EPS)), -1.0, 1.0)
        Wq1 = _quantize(W1)
        Wq2 = _quantize(W2)
        h = jax.nn.relu(jnp.einsum('bsd,fd->bsf', x, Wq1) + b1)
        out = jnp.einsum('bsf,df->bsd', h, Wq2) + b2
        return out

    def _L3_attn_ref(x, W_qkv, b_qkv, W_out, b_out):
        import jax, jax.numpy as jnp
        import numpy as np
        EMBED_DIM = 256
        NUM_HEADS = 16
        HEAD_DIM = EMBED_DIM // NUM_HEADS
        ROPE_BASE = 10000.0

        def rotate_half(x):
            d = x.shape[-1] // 2
            x1, x2 = (x[..., :d], x[..., d:])
            return jnp.concatenate((-x2, x1), axis=-1)
        B, T, C = x.shape
        H, Dh = (NUM_HEADS, HEAD_DIM)
        qkv = (x @ W_qkv + b_qkv).reshape(B, T, 3, H, Dh).transpose(2, 0, 3, 1, 4)
        q, k, v = (qkv[0], qkv[1], qkv[2])
        inv_freq = 1.0 / ROPE_BASE ** (jnp.arange(0, Dh, 2, dtype=jnp.float32) / Dh)
        freqs = jnp.arange(T, dtype=jnp.float32)[:, None] * inv_freq[None, :]
        emb = jnp.concatenate((freqs, freqs), axis=-1)
        cos, sin = (jnp.cos(emb), jnp.sin(emb))
        q = q * cos + rotate_half(q) * sin
        k = k * cos + rotate_half(k) * sin
        scale = 1.0 / np.sqrt(Dh)
        attn = jax.nn.softmax(jnp.einsum('bhqd,bhkd->bhqk', q, k) * scale, axis=-1)
        out = jnp.einsum('bhqk,bhkd->bhqd', attn, v)
        out = out.transpose(0, 2, 1, 3).reshape(B, T, C)
        return out @ W_out + b_out

    def _L3_xattn_ref(query, key, value):
        import jax, jax.numpy as jnp
        import numpy as np
        scale = jnp.asarray(query.shape[-1], query.dtype) ** 0.5
        scores = jnp.einsum('bqd,bkd->bqk', query, key) / scale
        attn = jax.nn.softmax(scores, axis=-1)
        return jnp.einsum('bqk,bkd->bqd', attn, value)

    def _L3_ffn_ref(x, gate_w, expert_bias, w1, b1, w2, b2, w3, b3, sw1, sb1, sw2, sb2, sw3, sb3):
        import jax, jax.numpy as jnp
        import numpy as np
        B, S, D = (4, 512, 256)
        DFF = 128
        E = 16
        TOP_K = 2
        N_SHARED = 2
        FUSED_DFF = DFF * N_SHARED
        Bv, Sv, Dv = x.shape
        xf = x.reshape(-1, Dv)
        logits = xf @ gate_w.T
        scores = jax.nn.sigmoid(logits)
        biased = logits + expert_bias.astype(logits.dtype)[None, :]
        _, topk_idx = jax.lax.top_k(biased, TOP_K)
        topk_w = jnp.take_along_axis(scores, topk_idx, axis=-1)
        topk_w = topk_w / (topk_w.sum(-1, keepdims=True) + 1e-10)
        gatew = (jax.nn.one_hot(topk_idx, E, dtype=xf.dtype) * topk_w[..., None]).sum(1)
        y = jnp.zeros_like(xf)
        for e in range(E):
            h = jax.nn.silu(xf @ w1[e].T + b1[e]) * (xf @ w3[e].T + b3[e])
            y = y + gatew[:, e:e + 1] * (h @ w2[e].T + b2[e])
        hs = jax.nn.silu(xf @ sw1.T + sb1) * (xf @ sw3.T + sb3)
        y = y + hs @ sw2.T + sb2
        return y.reshape(Bv, Sv, Dv)
    x = _layernorm(x + _L0_attn_ref(x, L0_attn_W_k, L0_attn_W_v, L0_attn_W_q), axis=-1)
    x = _layernorm(x + _L0_xattn_ref(x, ctx_1024, L0_xattn_w_sim, L0_xattn_b_sim, L0_xattn_W_qv, L0_xattn_b_qv), axis=-1)
    x = _layernorm(x + _L0_ffn_ref(x, L0_ffn_W, L0_ffn_b, L0_ffn_lora_down, L0_ffn_lora_up, L0_ffn_down_aux, L0_ffn_up_aux), axis=-1)
    x = _layernorm(x + _L1_attn_ref(x, L1_attn_W_qkv, L1_attn_W_out, L1_attn_b_out), axis=-1)
    x = _layernorm(x + _L1_xattn_ref(x, ctx_1024, ctx_1024, mask_Bx16xSxS2_bk1, L1_xattn_Wq, L1_xattn_bq, L1_xattn_Wk, L1_xattn_bk, L1_xattn_Wv, L1_xattn_bv, L1_xattn_Wo, L1_xattn_bo), axis=-1)
    x = _layernorm(x + _L1_ffn_ref(x, L1_ffn_w_gate, L1_ffn_w_up, L1_ffn_w_down), axis=-1)
    x = _layernorm(x + _L2_attn_ref(x, L2_attn_Wq, L2_attn_Wk, L2_attn_Wv, L2_attn_Wo), axis=-1)
    x = _layernorm(x + _L2_xattn_ref(x, ctx_1024, ctx_1024, mask_SxS2_bk0, L2_xattn_Wq, L2_xattn_Wk, L2_xattn_Wv, L2_xattn_Wo), axis=-1)
    x = _layernorm(x + _L2_ffn_ref(x, L2_ffn_W1, L2_ffn_b1, L2_ffn_W2, L2_ffn_b2), axis=-1)
    x = _layernorm(x + _L3_attn_ref(x, L3_attn_W_qkv, L3_attn_b_qkv, L3_attn_W_out, L3_attn_b_out), axis=-1)
    x = _layernorm(x + _L3_xattn_ref(x, ctx_1024, ctx_1024), axis=-1)
    x = _layernorm(x + _L3_ffn_ref(x, L3_ffn_gate_w, L3_ffn_expert_bias, L3_ffn_w1, L3_ffn_b1, L3_ffn_w2, L3_ffn_b2, L3_ffn_w3, L3_ffn_b3, L3_ffn_sw1, L3_ffn_sb1, L3_ffn_sw2, L3_ffn_sb2, L3_ffn_sw3, L3_ffn_sb3), axis=-1)
    return x

_drawn_inputs = setup_inputs


def setup_inputs(seed=0):
    import zlib

    import numpy as np

    out = dict(_drawn_inputs(seed))
    spreads = {'L1_xattn_bq': (0.0, 0.1),
     'L1_xattn_bk': (0.0, 2.0),
     'L1_xattn_bv': (0.0, 0.1),
     'L1_xattn_bo': (0.0, 0.1),
     'L3_ffn_expert_bias': (0.0, 0.1)}
    factors = {'L0_ffn_lora_down': 3.495,
     'L0_ffn_lora_up': 3.667,
     'L0_ffn_down_aux': 3.642,
     'L0_ffn_up_aux': 3.608,
     'L1_attn_b_out': 5.673,
     'L2_xattn_Wq': 8.0,
     'L2_xattn_Wk': 8.0,
     'L2_ffn_b1': 8.0,
     'L2_ffn_b2': 64.0,
     'L3_ffn_b1': 8.0,
     'L3_ffn_b3': 8.0,
     'L3_ffn_sb1': 8.0,
     'L3_ffn_sb3': 8.0,
     'L0_ffn_b': 4.472}
    for name, (base, spread) in spreads.items():
        noise = np.random.default_rng([zlib.crc32(name.encode()), seed]).standard_normal(out[name].shape)
        drawn = base * np.exp(spread * noise) if base else spread * noise
        out[name] = jnp.asarray(drawn.astype(out[name].dtype))
    for name, factor in factors.items():
        out[name] = (out[name] * factor).astype(out[name].dtype)
    return out
```

```python
from contextlib import ExitStack

import numpy as np

import concourse.bass as bass
from concourse import mybir

ALU = mybir.AluOpType
ACT = mybir.ActivationFunctionType
F32 = mybir.dt.float32
BF16 = mybir.dt.bfloat16
U8 = mybir.dt.uint8
U32 = mybir.dt.uint32
X = mybir.AxisListType.X
XY = mybir.AxisListType.XY

P = 128
NB, SEQ, D = 8, 256, 256
SK = 120
TILES = SEQ // P
DC = D // P
NH, DH = 16, 16
HC = 4
SLOT = 32
ONE_ROW = DH
EPS = 1e-5
NEG = -1.0e30
BLK = 8
TOKENS = NB * SEQ
FF1, FF2, FF3, NE = 768, 1024, 128, 16
ROUND = 12582912.0
QMAX = 32767.0
SB = 2
DV2 = 64


class Signals:

    def __init__(self, nc, ctx):
        self.nc, self.ctx, self.by_name = nc, ctx, {}

    def __call__(self, name, s=""):
        key = f"{name}_{s}" if s != "" else name
        if key not in self.by_name:
            self.by_name[key] = self.ctx.enter_context(self.nc.semaphore(key))
        return self.by_name[key]

    def runs(self):
        nums, found = sorted(h.num for h in self.by_name.values()), []
        for n in nums:
            if found and found[-1].stop == n:
                found[-1] = range(found[-1].start, n + 1)
            else:
                found.append(range(n, n + 1))
        return found


class Chain:

    def __init__(self, eng, sem):
        self.eng, self.sem, self.n = eng, sem, 0

    def __call__(self, *instructions):
        for ins in instructions:
            self.n += 1
            ins.then_inc(self.sem, 1)
        self.eng.wait_ge(self.sem, self.n)


def side_by_side(programs):
    live = list(programs)
    while live:
        for p in list(live):
            if next(p, "end") == "end":
                live.remove(p)


def norm_pe(pe, g, b, s, L, bank):
    pe.wait_ge(g(L + "_x", s), TILES)
    for t in range(TILES):
        for c in range(DC):
            last = pe.transpose(b.ps[s][:, bank, c * SEQ + t * P:c * SEQ + (t + 1) * P],
                                b.x[s][:, t, c * P:(c + 1) * P], b.ident[:, :])
    last.then_inc(g(L + "_xt", s), 1)


def norm_act(act, g, b, s, L, bank):
    act.wait_ge(g(L + "_xt", s), 1)
    act.activation(b.xT[s][:, :, :].rearrange("p c n -> p (c n)"), b.ps[s][:, bank, :], ACT.Copy)\
       .then_inc(g(L + "_xT", s), 1)


def norm_dve(dve, link, g, b, s, L, bank, bias=None, half=False):
    r, x, st, mv, rstd = b.r[s], b.x[s], b.st[s], b.mv[s], b.rstd[s]
    out = b.ps[s][:, bank, :].rearrange("p (t n) -> p t n", t=TILES)
    dve.wait_ge(g(L + "_out", s), 1)
    if half:
        link(dve.scalar_tensor_tensor(r[:, :, :], out, 0.5, x[:, :, :], ALU.mult, ALU.add))
    else:
        link(dve.tensor_tensor(r[:, :, :], out, x[:, :, :], ALU.add))
    if bias is not None:
        link(dve.tensor_tensor(r[:, :, :], r[:, :, :], bias.unsqueeze(1).to_broadcast([P, TILES, D]), ALU.add))
    link(*[dve.bn_stats(st[:, t, :], r[:, t, :]) for t in range(TILES)])
    link(*[dve.bn_aggr(mv[:, t, :], st[:, t, :]) for t in range(TILES)])
    dve.tensor_scalar(mv[:, :, 1], mv[:, :, 1], EPS, None, ALU.add).then_inc(g(L + "_var", s), 1)
    dve.wait_ge(g(L + "_rstd", s), 1)
    for t in range(TILES):
        dve.tensor_scalar(x[:, t, :], r[:, t, :], mv[:, t, 0:1], rstd[:, t:t + 1],
                          ALU.subtract, ALU.mult).then_inc(g(L + "_x", s), 1)


def norm_pool(pool, g, b, s, L):
    pool.wait_ge(g(L + "_var", s), 1)
    pool.tensor_tensor(b.rstd[s][:, :], b.mv[s][:, :, 1], b.minus_half[:, :], ALU.pow)\
        .then_inc(g(L + "_rstd", s), 1)


class Heads:

    def __init__(self, L, keys, dv, parts, mask=None, ob=1):
        self.L, self.keys, self.dv, self.mask, self.ob = L, keys, dv, mask, ob
        self.parts = parts
        self.scale = DH ** -0.5
        self.per = 2 if len(keys) == 1 else 1
        self.units = HC // self.per
        self.chunks = [range(u * self.per, (u + 1) * self.per) for u in range(self.units)]
        self.narrow = dv == DH

    def sees(self, t, k):
        return self.mask != "causal" or k <= t


def masked(h, b, s, pe, out, t, c, j, flipped):
    if h.mask == "causal":
        add = b.causalT[:, :] if flipped else b.causal[:, :]
    elif h.mask == "per_head":
        add = b.maskT[s][:, c * 4 + j, t * P:(t + 1) * P] if flipped else b.mask[s][:, t, c * 4 + j, :]
    else:
        add = b.smaskT[:, t * P:(t + 1) * P] if flipped else b.smask[:, t, :]
    n = add.shape[0]
    return pe.matmul(out, lhsT=b.identb[0:n, 0:n], rhs=add, start=False, stop=True, skip_group_check=True)


def heads_pe(pe, g, b, s, h):
    L, ps, qT, kT, v = h.L, b.ps[s], b.qT[s], b.kT[s], (b.vn if h.narrow else b.vw)[s]
    slot = lambda j: slice(SLOT * j, SLOT * (j + 1))
    two = len(h.keys) == 2
    if h.parts[0]:
        pe.wait_ge(g(L + "_q", s), h.parts[0])
        pe.wait_ge(g(L + "_k", s), h.parts[1])
    pe.wait_ge(g(L + "_v", s), h.parts[2])
    if h.mask == "per_head":
        pe.wait_ge(g(L + "_mask", s), 2)
    for u, chunks in enumerate(h.chunks):
        if u >= 1:
            pe.wait_ge(g(L + "_mx", s), TILES * u)
        for n, c in enumerate(chunks):
            for t in range(TILES):
                col = (n * TILES + t) * P * len(h.keys)
                width = sum(ks for k, (o, ks) in enumerate(h.keys) if h.sees(t, k))
                for j in range(4):
                    last = pe.matmul(ps[:, j, col:col + width], lhsT=qT[slot(j), c, t * P:(t + 1) * P],
                                     rhs=kT[slot(j), c, 0:width], start=True, stop=True, skip_group_check=True)
                if h.mask:
                    o = t * P if h.mask == "causal" else 0
                    ks = h.keys[0][1]
                    for j in range(4):
                        last = masked(h, b, s, pe, ps[:, j, col + o:col + o + ks], t, c, j, False)
        last.then_inc(g(L + "_s", s), 1)
        yield
    pe.wait_ge(g(L + "_mx", s), TILES * h.units)
    for c in range(HC):
        for t in range(TILES):
            last = pe.transpose(ps[:, c // 2, (c % 2) * SEQ + t * P:(c % 2) * SEQ + (t + 1) * P],
                                b.mneg[s][:, t, c * P:(c + 1) * P], b.ident[:, :])
    last.then_inc(g(L + "_mT", s), 1)
    yield
    pe.wait_ge(g(L + "_qa", s), 1)
    w = h.dv + 1
    for u, chunks in enumerate(h.chunks):
        if u >= 1:
            pe.wait_ge(g(L + "_o", s), u)
        for n, c in enumerate(chunks):
            for k, (o, ks) in enumerate(h.keys):
                col = (n + k) * SEQ
                first = min(t for t in range(TILES) if h.sees(t, k)) * P
                for j in range(4):
                    last = pe.matmul(ps[0:ks, j, col + first:col + SEQ], lhsT=kT[slot(j), c, o:o + ks],
                                     rhs=qT[slot(j), c, first:SEQ], start=True, stop=True, skip_group_check=True)
                for t in range(TILES):
                    if h.mask and (h.mask != "causal" or t == k):
                        for j in range(4):
                            last = masked(h, b, s, pe, ps[0:ks, j, col + t * P:col + (t + 1) * P], t, c, j, True)
        last.then_inc(g(L + "_st", s), 1)
        yield
        pe.wait_ge(g(L + "_e", s), len(h.keys) * (u + 1))
        for n, c in enumerate(chunks):
            for t in range(TILES):
                seen = [k for k in range(len(h.keys)) if h.sees(t, k)]
                for j in range(4):
                    at, head = (n * 4 + j) * w, c * 4 + j
                    for m, k in enumerate(seen):
                        ks = h.keys[k][1]
                        last = pe.matmul(ps[:, 2 + t, at:at + w],
                                         lhsT=b.PT[s][0:ks, j, (n + k) * SEQ + t * P:(n + k) * SEQ + (t + 1) * P],
                                         rhs=v[0:ks, k, head * w:(head + 1) * w], start=(m == 0),
                                         stop=(m == len(seen) - 1), skip_group_check=True)
        last.then_inc(g(L + "_pv", s), 1)
        yield
    nC = NH * h.dv // P
    pe.wait_ge(g(L + "_o", s), h.units)
    for t in range(TILES):
        for c in range(nC):
            last = pe.transpose(ps[:, c // 2, (c % 2) * SEQ + t * P:(c % 2) * SEQ + (t + 1) * P],
                                b.O[s][:, t, c * P:(c + 1) * P], b.ident[:, :])
    last.then_inc(g(L + "_ot", s), 1)
    yield
    pe.wait_ge(g(L + "_oT", s), max(1, nC // 4))
    for t in range(TILES):
        for c in range(nC):
            last = pe.matmul(ps[:, h.ob, t * D:(t + 1) * D], lhsT=b.oT[s][:, c, t * P:(t + 1) * P],
                             rhs=b.wo[L][:, c, :], start=(c == 0), stop=(c == nC - 1), skip_group_check=True)
    last.then_inc(g(L + "_out", s), 1)
    yield


def heads_act(act, g, b, s, h):
    L, ps = h.L, b.ps[s]
    for u in range(h.units):
        act.wait_ge(g(L + "_st", s), u + 1)
        if u >= 1:
            act.wait_ge(g(L + "_pv", s), u)
        if len(h.keys) == 1:
            ks = h.keys[0][1]
            act.activation(b.PT[s][0:ks, :, :], ps[0:ks, :, :], ACT.Exp, scale=h.scale).then_inc(g(L + "_e", s), 1)
        else:
            for k in range(2):
                lo = k * SEQ + min(t for t in range(TILES) if h.sees(t, k)) * P
                act.activation(b.PT[s][:, :, lo:(k + 1) * SEQ], ps[:, :, lo:(k + 1) * SEQ], ACT.Exp,
                               scale=h.scale).then_inc(g(L + "_e", s), 1)
        yield
    nC = NH * h.dv // P
    act.wait_ge(g(L + "_ot", s), 1)
    for i in range(max(1, nC // 4)):
        nb = min(nC // 2, 2)
        act.activation(b.oT[s][:, 4 * i:4 * i + 2 * nb, :].rearrange("p (a c) n -> p a (c n)", a=nb),
                       ps[:, 2 * i:2 * i + nb, :], ACT.Copy).then_inc(g(L + "_oT", s), 1)
    yield


def heads_dve(dve, link, g, b, s, h, valid=None):
    L, ps, w = h.L, b.ps[s], h.dv + 1
    spare = b.mneg[s][:, :, :].rearrange("p t (c j r) -> p t c j r", c=HC, j=4)
    for u, chunks in enumerate(h.chunks):
        dve.wait_ge(g(L + "_s", s), u + 1)
        for t in range(TILES):
            width = sum(ks for k, (o, ks) in enumerate(h.keys) if h.sees(t, k))
            if h.per == 2:
                src = ps[:, :, :].rearrange("p j (c t k) -> p t c j k", c=2, t=TILES)[:, t, :, :, 0:width]
                dst = spare[:, t, chunks.start:chunks.stop, :, ONE_ROW]
            else:
                src = ps[:, :, t * SEQ:t * SEQ + width]
                dst = spare[:, t, chunks.start, :, ONE_ROW]
            dve.tensor_reduce(dst, src, X, ALU.max, negate=True).then_inc(g(L + "_mx", s), 1)
        yield
    dve.wait_ge(g(L + "_mT", s), 1)
    q = b.qT[s][:, :, :].rearrange("p (a c) n -> p a (c n)", a=2)
    dve.tensor_tensor(q, q, ps[:, 0:2, :], ALU.add).then_inc(g(L + "_qa", s), 1)
    yield
    nh = 4 * h.per
    for u in range(h.units):
        dve.wait_ge(g(L + "_pv", s), u + 1)
        view = ps[:, 2:4, 0:nh * w].rearrange("p t (j w) -> p t j w", w=w)
        ri = b.ri[s][:, 0:TILES * nh].rearrange("p (t j) -> p t j", t=TILES)
        dst = b.O[s][:, :, u * nh * h.dv:(u + 1) * nh * h.dv].rearrange("p t (j w) -> p t j w", w=h.dv)
        if valid is not None:
            link(dve.tensor_scalar(ri, view[:, :, :, h.dv], 1e-9, None, ALU.max))
            link(dve.reciprocal(ri, ri))
            link(dve.tensor_tensor(ri, ri, valid[:, :].unsqueeze(2).to_broadcast([P, TILES, nh]), ALU.mult))
        else:
            link(dve.reciprocal(ri, view[:, :, :, h.dv]))
        dve.tensor_tensor(dst, view[:, :, :, 0:h.dv], ri.unsqueeze(3).to_broadcast([P, TILES, nh, h.dv]), ALU.mult)\
           .then_inc(g(L + "_o", s), 1)
        yield


def cross_pe(pe, g, b, s, L, prev):
    ps, w = b.ps[s], b.w[L]
    pe.wait_ge(g("ctx", s), 32)
    pe.wait_ge(g(prev + "_xT", s), 1)
    for c in range(HC):
        for i in range(DC):
            last = pe.matmul(ps[:, 2, c * P:c * P + SK], lhsT=w["k"][:, i, c * P:(c + 1) * P],
                             rhs=b.ctxT[s][:, i, :], start=(i == 0), stop=(i == DC - 1), skip_group_check=True)
    last.then_inc(g(L + "_pk", s), 1)
    for i in range(DC):
        last = pe.matmul(ps[0:SK, 0, 0:D], lhsT=b.ctxT[s][:, i, :], rhs=w["v"][:, i, :],
                         start=(i == 0), stop=(i == DC - 1), skip_group_check=True)
    last.then_inc(g(L + "_pvv", s), 1)
    yield
    for c in range(HC):
        bank = 1 + 2 * (c // 2)
        for i in range(DC):
            last = pe.matmul(ps[:, bank, (c % 2) * SEQ:(c % 2 + 1) * SEQ], lhsT=w["q"][:, i, c * P:(c + 1) * P],
                             rhs=b.xT[s][:, i, :], start=(i == 0), stop=(i == DC - 1), skip_group_check=True)
        if c % 2 == 1:
            last.then_inc(g(L + "_pq", s), 1)
    yield


def cross_act(act, g, b, s, L, q_bias=None):
    act.wait_ge(g(L + "_pk", s), 1)
    for c in range(HC):
        act.activation(b.kT[s][:, c, 0:SK], b.ps[s][:, 2, c * P:c * P + SK], ACT.Identity,
                       bias=b.k_bias[L][:, c:c + 1]).then_inc(g(L + "_k", s), 1)
    yield
    for i in range(2):
        act.wait_ge(g(L + "_pq", s), i + 1)
        for c in range(2):
            kw = {"bias": q_bias[:, 2 * i + c:2 * i + c + 1]} if q_bias is not None else {}
            act.activation(b.qT[s][:, 2 * i + c, :], b.ps[s][:, 1 + 2 * i, c * SEQ:(c + 1) * SEQ],
                           ACT.Identity, **kw).then_inc(g(L + "_q", s), 1)
    yield


def cross_dve(dve, g, b, s, L, v_bias=None):
    dve.wait_ge(g(L + "_pvv", s), 1)
    dst = b.vn[s][0:SK, 0, :].rearrange("p (h w) -> p h w", w=DH + 1)[:, :, 0:DH]
    src = b.ps[s][0:SK, 0, 0:D].rearrange("p (h w) -> p h w", w=DH)
    if v_bias is not None:
        ins = dve.tensor_tensor(dst, src, v_bias[0:SK, :].rearrange("p (h w) -> p h w", w=DH), ALU.add)
    else:
        ins = dve.tensor_copy(dst, src)
    ins.then_inc(g(L + "_v", s), 1)
    yield


def project_T(pe, out, w, c, xT):
    for i in range(DC):
        last = pe.matmul(out, lhsT=w[:, i, c * P:(c + 1) * P], rhs=xT[:, i, :],
                         start=(i == 0), stop=(i == DC - 1), skip_group_check=True)
    return last


def project(pe, ps, bank, xT, w, n=D):
    for t in range(TILES):
        for i in range(DC):
            last = pe.matmul(ps[:, bank, t * n:(t + 1) * n], lhsT=xT[:, i, t * P:(t + 1) * P],
                             rhs=w[:, i, :], start=(i == 0), stop=(i == DC - 1), skip_group_check=True)
    return last


def causal_pe(pe, g, b, s, prev):
    ps, w, xT = b.ps[s], b.w["L2a"], b.xT[s]
    pe.wait_ge(g(prev + "_xT", s), 1)
    for n, c in enumerate(range(HC)):
        last = project_T(pe, ps[:, c // 2, (c % 2) * SEQ:(c % 2 + 1) * SEQ], w["q"], c, xT)
    last.then_inc(g("L2a_pq", s), 1)
    for c in range(HC):
        last = project_T(pe, ps[:, 2 + c // 2, (c % 2) * SEQ:(c % 2 + 1) * SEQ], w["k"], c, xT)
    last.then_inc(g("L2a_pk", s), 1)
    yield
    for t in range(TILES):
        if t == 0:
            pe.wait_ge(g("L2a_q", s), 1)
        else:
            pe.wait_ge(g("L2a_k", s), HC)
        for half in range(2):
            for i in range(DC):
                last = pe.matmul(ps[:, 2 * t + half, :], lhsT=xT[:, i, t * P:(t + 1) * P],
                                 rhs=w["v"][:, i, half * 512:(half + 1) * 512],
                                 start=(i == 0), stop=(i == DC - 1), skip_group_check=True)
        last.then_inc(g("L2a_pvv", s), 1)
    yield
    pe.wait_ge(g("L2a_v", s), 2)
    yield from heads_pe(pe, g, b, s, b.heads["L2a"])


def causal_act(act, g, b, s):
    ps = b.ps[s]
    act.wait_ge(g("L2a_pq", s), 1)
    act.activation(b.qT[s][:, :, :].rearrange("p (a c) n -> p a (c n)", a=2), ps[:, 0:2, :], ACT.Copy)\
       .then_inc(g("L2a_q", s), 1)
    act.wait_ge(g("L2a_pk", s), 1)
    for c in range(HC):
        act.activation(b.kT[s][:, c, :], ps[:, 2 + c // 2, (c % 2) * SEQ:(c % 2 + 1) * SEQ], ACT.Identity,
                       bias=b.k_bias["L2a"][:, c:c + 1]).then_inc(g("L2a_k", s), 1)
    yield
    yield
    yield from heads_act(act, g, b, s, b.heads["L2a"])


def causal_dve(dve, link, g, b, s):
    for t in range(TILES):
        dve.wait_ge(g("L2a_pvv", s), t + 1)
        dve.tensor_copy(b.vw[s][:, t, :].rearrange("p (h w) -> p h w", w=DV2 + 1)[:, :, 0:DV2],
                        b.ps[s][:, 2 * t:2 * t + 2, :].rearrange("p a (h w) -> p (a h) w", w=DV2))\
           .then_inc(g("L2a_v", s), 1)
    yield
    yield from heads_dve(dve, link, g, b, s, b.heads["L2a"])


def rotary_pe(pe, g, b, s, prev):
    ps, w, xT = b.ps[s], b.w["L3a"], b.xT[s]
    pe.wait_ge(g(prev + "_xT", s), 1)
    n = 0
    for name in ("q", "k"):
        for pair in range(2):
            bank = 2 * (n % 2)
            if n >= 2:
                pe.wait_ge(g("L3a_rope", s), n - 1)
            for rot in range(2):
                for c in range(2):
                    last = project_T(pe, ps[:, bank + rot, c * SEQ:(c + 1) * SEQ],
                                     w[name + ("_rot" if rot else "")], 2 * pair + c, xT)
            last.then_inc(g("L3a_pqk", s), 1)
            n += 1
            yield
    pe.wait_ge(g("L3a_rope", s), 4)
    project(pe, ps, 0, xT, w["v"]).then_inc(g("L3a_pvv", s), 1)
    yield
    pe.wait_ge(g("L3a_v", s), 1)
    yield from heads_pe(pe, g, b, s, b.heads["L3a"])


def rotary_dve(dve, link, g, b, s):
    ps = b.ps[s]
    n = 0
    for name, dst in (("q", b.qT[s]), ("k", b.kT[s])):
        for pair in range(2):
            bank = 2 * (n % 2)
            dve.wait_ge(g("L3a_pqk", s), n + 1)
            for c in range(2):
                dve.scalar_tensor_tensor(b.rc[s][:, c, :], ps[:, bank, c * SEQ:(c + 1) * SEQ],
                                         b.rope_bias[name][:, 2 * pair + c:2 * pair + c + 1],
                                         b.cos[:, :], ALU.add, ALU.mult)
                link(dve.scalar_tensor_tensor(b.rs[s][:, c, :], ps[:, bank + 1, c * SEQ:(c + 1) * SEQ],
                                         b.rope_bias[name + "_rot"][:, 2 * pair + c:2 * pair + c + 1],
                                         b.sin[:, :], ALU.add, ALU.mult))
            dve.tensor_tensor(dst[:, 2 * pair:2 * pair + 2, :], b.rc[s][:, :, :], b.rs[s][:, :, :], ALU.add)\
               .then_inc(g("L3a_rope", s), 1)
            n += 1
            yield
    dve.wait_ge(g("L3a_pvv", s), 1)
    dve.tensor_tensor(b.vn[s][:, :, :].rearrange("p t (h w) -> p t h w", w=DH + 1)[:, :, :, 0:DH],
                      ps[:, 0, :].rearrange("p (t h w) -> p t h w", t=TILES, w=DH),
                      b.v_bias["L3a"][:, :].rearrange("p (h w) -> p h w", w=DH).unsqueeze(1)
                       .to_broadcast([P, TILES, NH, DH]), ALU.add).then_inc(g("L3a_v", s), 1)
    yield
    yield from heads_dve(dve, link, g, b, s, b.heads["L3a"])


def flow_pe(pe, g, b, s, prev):
    ps, xT, x = b.ps[s], b.xT[s], b.x[s]
    pe.wait_ge(g(prev + "_xT", s), 1)
    pe.wait_ge(g("ctx", s), 32)
    pe.wait_ge(g("L0x_m", s), DC)
    for t in range(TILES):
        out = ps[:, 2, t * P:t * P + SK]
        for i in range(DC):
            pe.matmul(out, lhsT=xT[:, i, t * P:(t + 1) * P], rhs=b.flow_m[s][:, i, :],
                      start=(i == 0), stop=False, skip_group_check=True)
        for i in range(DC):
            last = pe.matmul(out, lhsT=b.w2_wide[:, i, :], rhs=b.ctxT[s][:, i, :],
                             start=False, stop=(i == DC - 1), skip_group_check=True)
    last.then_inc(g("L0x_sim", s), 1)
    yield
    pe.wait_ge(g("L0x_A", s), 1)
    for t in range(TILES):
        pe.transpose(ps[0:SK, 3, t * P:(t + 1) * P], b.A[s][:, t, :], b.ident[:, :])
    for t in range(TILES):
        last = pe.transpose(ps[0:1, 1, t * P:(t + 1) * P], b.nm[s][:, t:t + 1], b.ident[:, :])
    last.then_inc(g("L0x_At", s), 1)
    yield
    pe.wait_ge(g("L0x_nM", s), 1)
    pe.matmul(ps[:, 2, 2 * P:2 * P + 1], lhsT=b.ones[0:1, :], rhs=b.nM[s][0:1, 0:1], start=True, stop=True,
              skip_group_check=True).then_inc(g("L0x_nMb", s), 1)
    pe.wait_ge(g("L0x_AT", s), 1)
    for i in range(DC):
        pe.matmul(ps[:, 1, i * SEQ:(i + 1) * SEQ], lhsT=b.ctx[s][:, i * P:(i + 1) * P], rhs=b.AT[s][:, :],
                  start=True, stop=True, skip_group_check=True)
    pe.wait_ge(g("L0x_e", s), 1)
    for t in range(TILES):
        pe.matmul(ps[:, 2, 2 * P + 8:2 * P + 9], lhsT=b.ones[:, :], rhs=b.ecol[s][:, t:t + 1],
                  start=(t == 0), stop=(t == TILES - 1), skip_group_check=True)
    for i in range(DC):
        for t in range(TILES):
            last = pe.matmul(ps[:, 2, 2 * P + 16 + i:2 * P + 17 + i], lhsT=x[:, t, i * P:(i + 1) * P],
                             rhs=b.ecol[s][:, t:t + 1], start=(t == 0), stop=(t == TILES - 1),
                             skip_group_check=True)
    last.then_inc(g("L0x_hq", s), 1)
    yield
    pe.wait_ge(g("L0x_f", s), 2)
    pe.wait_ge(g("L0x_hqT", s), 1)
    for t in range(TILES):
        for f, feat in enumerate((xT, b.hqT[s], b.xhq[s], b.xhc[s])):
            for i in range(DC):
                last = pe.matmul(ps[:, 0, t * D:(t + 1) * D], lhsT=feat[:, i, t * P:(t + 1) * P],
                                 rhs=b.w["L0x"][:, 2 * f + i, :], start=(f + i == 0), stop=(f == 3 and i == 1),
                                 skip_group_check=True)
    last.then_inc(g("L0x_out", s), 1)
    yield


def flow_act(act, g, b, s):
    ps = b.ps[s]
    act.wait_ge(g("L0x_nm", s), 1)
    for t in range(TILES):
        act.activation(b.A[s][:, t, :], b.sim[s][:, t, :], ACT.Exp, bias=b.nm[s][:, t:t + 1],
                       accum_out=b.ssum[s][:, t:t + 1]).then_inc(g("L0x_exp", s), 1)
    yield
    act.wait_ge(g("L0x_At", s), 1)
    act.activation(b.AT[s][:, :], ps[0:SK, 3, 0:SEQ], ACT.Copy).then_inc(g("L0x_AT", s), 1)
    yield
    act.wait_ge(g("L0x_nMs", s), 1)
    act.activation(b.ecol[s][:, :], b.nm[s][:, :], ACT.Exp, scale=-1.0, bias=b.nMb[s][:, 0:1])\
       .then_inc(g("L0x_e", s), 1)
    act.wait_ge(g("L0x_hq", s), 1)
    act.activation(b.hqT[s][:, :, :].rearrange("p c n -> p (c n)"), ps[:, 1, :], ACT.Copy)\
       .then_inc(g("L0x_hqT", s), 1)
    yield


def flow_dve(dve, link, g, b, s):
    ps = b.ps[s]
    dve.wait_ge(g("ctx", s), 32)
    for i in range(DC):
        dve.tensor_scalar(b.flow_m[s][:, i, :], b.ctxT[s][:, i, :], b.w3[:, i:i + 1], b.w1[:, i:i + 1],
                          ALU.mult, ALU.add).then_inc(g("L0x_m", s), 1)
    yield
    dve.wait_ge(g("L0x_sim", s), 1)
    sim = ps[:, 2, 0:2 * P].rearrange("p (t n) -> p t n", t=TILES)[:, :, 0:SK]
    link(dve.tensor_scalar(b.sim[s][:, :, :], sim, b.b_sim[:, 0:1], None, ALU.add))
    dve.tensor_reduce(b.nm[s][:, :], b.sim[s][:, :, :], X, ALU.max, negate=True).then_inc(g("L0x_nm", s), 1)
    yield
    dve.wait_ge(g("L0x_exp", s), TILES)
    link(dve.reciprocal(b.ssum[s][:, :], b.ssum[s][:, :]))
    dve.tensor_tensor(b.A[s][:, :, :], b.A[s][:, :, :],
                      b.ssum[s][:, :].unsqueeze(2).to_broadcast([P, TILES, SK]), ALU.mult)\
       .then_inc(g("L0x_A", s), 1)
    yield
    dve.wait_ge(g("L0x_At", s), 1)
    dve.tensor_reduce(b.nM[s][0:1, 0:1], ps[0:1, 1, 0:SEQ], X, ALU.min).then_inc(g("L0x_nM", s), 1)
    dve.wait_ge(g("L0x_nMb", s), 1)
    dve.tensor_copy(b.nMb[s][:, :], ps[:, 2, 2 * P:2 * P + 1]).then_inc(g("L0x_nMs", s), 1)
    yield
    dve.wait_ge(g("L0x_hq", s), 1)
    link(dve.reciprocal(b.nMb[s][:, :], ps[:, 2, 2 * P + 8:2 * P + 9]))
    link(dve.tensor_scalar(b.hc[s][:, :], ps[:, 2, 2 * P + 16:2 * P + 16 + DC], b.nMb[s][:, 0:1], None, ALU.mult))
    dve.wait_ge(g("L0x_hqT", s), 1)
    dve.tensor_tensor(b.xhq[s][:, :, :], b.xT[s][:, :, :], b.hqT[s][:, :, :], ALU.mult).then_inc(g("L0x_f", s), 1)
    dve.tensor_tensor(b.xhc[s][:, :, :], b.xT[s][:, :, :],
                      b.hc[s][:, :].unsqueeze(2).to_broadcast([P, DC, SEQ]), ALU.mult)\
       .then_inc(g("L0x_f", s), 1)
    yield


def block_pe(pe, g, b, s, prev):
    ps, xT, w = b.ps[s], b.xT[s], b.w["L1a"]
    pe.wait_ge(g(prev + "_xT", s), 1)
    for n, bank in enumerate((0, 2)):
        for c in range(DC):
            last = project_T(pe, ps[:, bank, c * SEQ:(c + 1) * SEQ], w[:, :, n * D:(n + 1) * D], c, xT)
        last.then_inc(g("L1a_pqk", s), 1)
    project(pe, ps, 3, xT, w[:, :, 2 * D:3 * D]).then_inc(g("L1a_pvv", s), 1)
    yield
    pe.wait_ge(g("L1a_qk", s), 2)
    for t in range(TILES):
        for c in range(DC):
            last = pe.matmul(ps[:, 1, t * P:(t + 1) * P], lhsT=b.bq[s][:, c, t * P:(t + 1) * P],
                             rhs=b.bk[s][:, c, t * P:(t + 1) * P], start=(c == 0), stop=(c == DC - 1),
                             skip_group_check=True)
    last.then_inc(g("L1a_s", s), 1)
    yield
    pe.wait_ge(g("L1a_p", s), 1)
    for t in range(TILES):
        last = pe.transpose(ps[:, 2, t * P:(t + 1) * P], b.pb[s][:, t, :], b.ident[:, :])
    last.then_inc(g("L1a_pt", s), 1)
    yield
    pe.wait_ge(g("L1a_pT", s), 1)
    pe.wait_ge(g("L1a_v", s), 1)
    for c in range(DC):
        for t in range(TILES):
            last = pe.matmul(ps[:, 3, c * SEQ + t * P:c * SEQ + (t + 1) * P], lhsT=b.bv[s][:, t, c * P:(c + 1) * P],
                             rhs=b.pbT[s][:, t * P:(t + 1) * P], start=True, stop=True, skip_group_check=True)
    last.then_inc(g("L1a_ot", s), 1)
    yield
    pe.wait_ge(g("L1a_oT", s), 1)
    project(pe, ps, 0, b.oT[s], b.wo["L1a"]).then_inc(g("L1a_out", s), 1)
    yield


def block_act(act, g, b, s):
    ps = b.ps[s]
    flat = lambda a: a[:, :, :].rearrange("p c n -> p (c n)")
    for n, (bank, dst) in enumerate(((0, b.bq[s]), (2, b.bk[s]))):
        act.wait_ge(g("L1a_pqk", s), n + 1)
        act.activation(flat(dst), ps[:, bank, :], ACT.Copy).then_inc(g("L1a_qk", s), 1)
    yield
    act.wait_ge(g("L1a_nm", s), 1)
    for t in range(TILES):
        act.activation(b.pb[s][:, t, :], b.sc[s][:, t, :], ACT.Exp, bias=b.nm[s][:, t:t + 1],
                       accum_out=b.ssum[s][:, t:t + 1]).then_inc(g("L1a_exp", s), 1)
    yield
    act.wait_ge(g("L1a_pt", s), 1)
    act.activation(b.pbT[s][:, :], ps[:, 2, 0:SEQ], ACT.Copy).then_inc(g("L1a_pT", s), 1)
    yield
    act.wait_ge(g("L1a_ot", s), 1)
    act.activation(flat(b.oT[s]), ps[:, 3, :], ACT.Copy).then_inc(g("L1a_oT", s), 1)
    yield


def block_dve(dve, link, g, b, s):
    ps = b.ps[s]
    dve.wait_ge(g("L1a_pvv", s), 1)
    dve.tensor_copy(b.bv[s][:, :, :].rearrange("p t n -> p (t n)"), ps[:, 3, :]).then_inc(g("L1a_v", s), 1)
    yield
    dve.wait_ge(g("L1a_s", s), 1)
    link(dve.scalar_tensor_tensor(b.sc[s][:, :, :], ps[:, 1, 0:SEQ].rearrange("p (t n) -> p t n", t=TILES),
                                  float(D) ** -0.5, b.causal32[:, :].unsqueeze(1).to_broadcast([P, TILES, P]),
                                  ALU.mult, ALU.add))
    dve.tensor_reduce(b.nm[s][:, :], b.sc[s][:, :, :], X, ALU.max, negate=True).then_inc(g("L1a_nm", s), 1)
    yield
    dve.wait_ge(g("L1a_exp", s), TILES)
    link(dve.tensor_scalar(b.ssum[s][:, :], b.ssum[s][:, :], 1e-6, None, ALU.add))
    link(dve.reciprocal(b.ssum[s][:, :], b.ssum[s][:, :]))
    dve.tensor_tensor(b.pb[s][:, :, :], b.pb[s][:, :, :],
                      b.ssum[s][:, :].unsqueeze(2).to_broadcast([P, TILES, P]), ALU.mult)\
       .then_inc(g("L1a_p", s), 1)
    yield


def ternary_pe(pe, g, b, s, prev):
    ps, xT = b.ps[s], b.xT[s]
    pe.wait_ge(g(prev + "_xT", s), 1)
    for f in range(FF2 // P):
        last = project_T(pe, ps[:, f // 2, (f % 2) * SEQ:(f % 2 + 1) * SEQ], b.w["L2f1"], f, xT)
        if f % 2 == 1:
            last.then_inc(g("L2f_h", s), 1)
    yield
    pe.wait_ge(g("L2f_r", s), FF2 // P)
    for t in range(TILES):
        for f in range(FF2 // P):
            last = pe.matmul(ps[:, 0, t * D:(t + 1) * D], lhsT=b.hT[s][:, f, t * P:(t + 1) * P],
                             rhs=b.w["L2f2"][:, f, :], start=(f == 0), stop=(f == FF2 // P - 1),
                             skip_group_check=True)
    last.then_inc(g("L2f_out", s), 1)
    yield


def ternary_act(act, g, b, s):
    for f in range(FF2 // P):
        if f % 2 == 0:
            act.wait_ge(g("L2f_h", s), f // 2 + 1)
        act.activation(b.hT[s][:, f, :], b.ps[s][:, f // 2, (f % 2) * SEQ:(f % 2 + 1) * SEQ], ACT.Relu,
                       bias=b.b1[:, f:f + 1]).then_inc(g("L2f_r", s), 1)
    yield


def wide_pe(pe, g, b, s, prev):
    ps, xT = b.ps[s], b.xT[s]
    pe.wait_ge(g(prev + "_xT", s), 1)
    for t in range(TILES):
        for i in range(DC):
            last = pe.matmul(ps[:, 0, t * P:t * P + SK], lhsT=xT[:, i, t * P:(t + 1) * P], rhs=b.ctxT[s][:, i, :],
                             start=(i == 0), stop=(i == DC - 1), skip_group_check=True)
    last.then_inc(g("L3x_s", s), 1)
    yield
    pe.wait_ge(g("L3x_A", s), 1)
    for t in range(TILES):
        last = pe.transpose(ps[0:SK, 2, t * P:(t + 1) * P], b.A[s][:, t, :], b.ident[:, :])
    last.then_inc(g("L3x_At", s), 1)
    yield
    pe.wait_ge(g("L3x_AT", s), 1)
    for t in range(TILES):
        last = pe.matmul(ps[:, 1, t * D:(t + 1) * D], lhsT=b.AT[s][:, t * P:(t + 1) * P], rhs=b.ctx[s][:, :],
                         start=True, stop=True, skip_group_check=True)
    last.then_inc(g("L3x_out", s), 1)
    yield


def wide_act(act, g, b, s):
    act.wait_ge(g("L3x_nm", s), 1)
    for t in range(TILES):
        act.activation(b.A[s][:, t, :], b.ps[s][:, 0, t * P:t * P + SK], ACT.Exp, bias=b.nm[s][:, t:t + 1],
                       scale=float(D) ** -0.5, accum_out=b.ssum[s][:, t:t + 1]).then_inc(g("L3x_exp", s), 1)
    yield
    act.wait_ge(g("L3x_At", s), 1)
    act.activation(b.AT[s][:, :], b.ps[s][0:SK, 2, 0:SEQ], ACT.Copy).then_inc(g("L3x_AT", s), 1)
    yield


def wide_dve(dve, link, g, b, s):
    dve.wait_ge(g("L3x_s", s), 1)
    view = b.ps[s][:, 0, 0:2 * P].rearrange("p (t n) -> p t n", t=TILES)[:, :, 0:SK]
    link(dve.tensor_reduce(b.nm[s][:, :], view, X, ALU.max, negate=True))
    dve.tensor_scalar(b.nm[s][:, :], b.nm[s][:, :], float(D) ** -0.5, None, ALU.mult).then_inc(g("L3x_nm", s), 1)
    yield
    dve.wait_ge(g("L3x_exp", s), TILES)
    link(dve.reciprocal(b.ssum[s][:, :], b.ssum[s][:, :]))
    dve.tensor_tensor(b.A[s][:, :, :], b.A[s][:, :, :],
                      b.ssum[s][:, :].unsqueeze(2).to_broadcast([P, TILES, SK]), ALU.mult)\
       .then_inc(g("L3x_A", s), 1)
    yield


UNITS3 = NE + 2


def experts_pe(pe, g, b, s, prev):
    ps, xT = b.ps[s], b.xT[s]
    pe.wait_ge(g(prev + "_xT", s), 1)
    for t in range(TILES):
        for i in range(DC):
            last = pe.matmul(ps[:, 3, t * NE:(t + 1) * NE], lhsT=xT[:, i, t * P:(t + 1) * P], rhs=b.gate_w[:, i, :],
                             start=(i == 0), stop=(i == DC - 1), skip_group_check=True)
    last.then_inc(g("L3f_lg", s), 1)
    pe.matmul(ps[:, 0, :], lhsT=b.ones[0:1, :], rhs=b.sb2_twice[0:1, :], start=True, stop=False,
              skip_group_check=True)
    order = [NE, NE + 1] + list(range(NE))
    for n in range(UNITS3 + 1):
        if n < UNITS3:
            e = order[n]
            for k, w in enumerate((b.w1e, b.w3e)):
                if n >= 1 and k == 0:
                    pe.wait_ge(g("L3f_z", s), 2 * n)
                if n >= 1 and k == 1:
                    pe.wait_ge(g("L3f_b", s), n)
                for i in range(DC):
                    last = pe.matmul(ps[:, 1 + k, 0:SEQ], lhsT=w[:, e, i, :],
                                     rhs=xT[:, i, :], start=(i == 0), stop=(i == DC - 1), skip_group_check=True)
                last.then_inc(g("L3f_h", s), 1)
            if n == 2:
                pe.wait_ge(g("L3f_gw", s), 1)
                for t in range(TILES):
                    last = pe.transpose(ps[0:NE, 3, t * P:(t + 1) * P], b.gw[s][:, t, :], b.ident[:, :])
                last.then_inc(g("L3f_gt", s), 1)
                pe.wait_ge(g("L3f_gT", s), 1)
                for t in range(TILES):
                    pe.matmul(ps[:, 0, t * D:(t + 1) * D], lhsT=b.gT[s][:, t * P:(t + 1) * P], rhs=b.b2e[:, :],
                              start=False, stop=False, skip_group_check=True)
            if e < NE:
                if n >= 3:
                    pe.wait_ge(g("L3f_c", s), n - 2)
                pe.matmul(ps[:, 3, 0:SEQ], lhsT=b.pick[:, e, :], rhs=b.gT[s][:, :],
                          start=True, stop=True, skip_group_check=True).then_inc(g("L3f_G", s), 1)
        if n >= 1:
            e = order[n - 1]
            if e < NE:
                pe.wait_ge(g("L3f_c", s), n - 2)
            else:
                pe.wait_ge(g("L3f_b", s), n)
            for t in range(TILES):
                last = pe.matmul(ps[:, 0, t * D:(t + 1) * D], lhsT=b.he[s][:, (n - 1) % 2, t * P:(t + 1) * P],
                                 rhs=b.w2e[:, e, :], start=False, stop=(n == UNITS3), skip_group_check=True)
            last.then_inc(g("L3f_out" if n == UNITS3 else "L3f_y", s), 1)
        yield


def experts_act(act, g, b, s):
    order = [NE, NE + 1] + list(range(NE))
    act.wait_ge(g("L3f_raw", s), 1)
    act.activation(b.th[s][:, :], b.raw[s][:, :], ACT.Tanh, scale=0.5).then_inc(g("L3f_th", s), 1)
    for n, e in enumerate(order):
        act.wait_ge(g("L3f_h", s), 2 * n + 1)
        if n >= 2:
            act.wait_ge(g("L3f_a", s), n - 1)
        h1 = b.ps[s][:, 1, 0:SEQ]
        act.activation(b.t3[s][:, n % 2, :], h1, ACT.Tanh, scale=0.5, bias=b.b1e_half[:, e:e + 1])\
           .then_inc(g("L3f_z", s), 1)
        act.activation(b.z3[s][:, n % 2, :], h1, ACT.Identity, scale=0.5, bias=b.b1e_half[:, e:e + 1])\
           .then_inc(g("L3f_z", s), 1)
        if n == 2:
            act.wait_ge(g("L3f_gt", s), 1)
            act.activation(b.gT[s][:, :], b.ps[s][0:NE, 3, 0:SEQ], ACT.Copy).then_inc(g("L3f_gT", s), 1)
        yield


def experts_dve(dve, link, g, b, s):
    order = [NE, NE + 1] + list(range(NE))
    m8, i8, f8, sel, gw = b.m8[s], b.i8[s], b.f8[s], b.sel[s], b.gw[s]
    lg = b.lg[s]
    dve.wait_ge(g("L3f_lg", s), 1)
    dve.tensor_copy(b.raw[s][:, :], b.ps[s][:, 3, 0:TILES * NE]).then_inc(g("L3f_raw", s), 1)
    dve.wait_ge(g("L3f_raw", s), 1)
    link(dve.tensor_tensor(lg[:, :, :], b.raw[s][:, :].rearrange("p (t e) -> p t e", t=TILES),
                           b.expert_bias[:, :].unsqueeze(1).to_broadcast([P, TILES, NE]), ALU.add))
    link(*[dve.max(m8[:, t, :], lg[:, t, :]) for t in range(TILES)])
    link(*[dve.max_index(i8[:, t, :], m8[:, t, :], lg[:, t, :]) for t in range(TILES)])
    link(dve.tensor_copy(f8[:, :, :], i8[:, :, :]))
    for t in range(TILES):
        link(dve.tensor_scalar(sel[:, t, :], b.iota[:, :], f8[:, t, 0:1], None, ALU.is_equal))
        link(dve.scalar_tensor_tensor(sel[:, t, :], b.iota[:, :], f8[:, t, 1:2], sel[:, t, :],
                                      ALU.is_equal, ALU.add))
    dve.wait_ge(g("L3f_th", s), 1)
    link(dve.tensor_scalar(gw[:, :, :], b.th[s][:, :].rearrange("p (t e) -> p t e", t=TILES), 0.5, 0.5,
                           ALU.mult, ALU.add))
    link(dve.tensor_tensor(gw[:, :, :], gw[:, :, :], sel[:, :, :], ALU.mult))
    link(dve.tensor_reduce(b.nm[s][:, :], gw[:, :, :], X, ALU.add))
    link(dve.tensor_scalar(b.nm[s][:, :], b.nm[s][:, :], 1e-10, None, ALU.add))
    link(dve.reciprocal(b.nm[s][:, :], b.nm[s][:, :]))
    dve.tensor_tensor(gw[:, :, :], gw[:, :, :], b.nm[s][:, :].unsqueeze(2).to_broadcast([P, TILES, NE]),
                      ALU.mult).then_inc(g("L3f_gw", s), 1)
    for n, e in enumerate(order):
        dve.wait_ge(g("L3f_z", s), 2 * n + 2)
        dve.scalar_tensor_tensor(b.a3[s][:, n % 2, :], b.t3[s][:, n % 2, :], 1.0, b.z3[s][:, n % 2, :],
                                 ALU.add, ALU.mult).then_inc(g("L3f_a", s), 1)
        dve.wait_ge(g("L3f_a", s), n + 1)
        if n >= 2:
            dve.wait_ge(g("L3f_y", s), n - 1)
        dve.wait_ge(g("L3f_h", s), 2 * n + 2)
        dve.scalar_tensor_tensor(b.he[s][:, n % 2, :], b.ps[s][:, 2, 0:SEQ],
                                 b.b3e[:, e:e + 1], b.a3[s][:, n % 2, :], ALU.add, ALU.mult)\
           .then_inc(g("L3f_b", s), 1)
        if e < NE:
            dve.wait_ge(g("L3f_b", s), n + 1)
            dve.wait_ge(g("L3f_G", s), n - 1)
            dve.tensor_tensor(b.he[s][:, n % 2, :], b.he[s][:, n % 2, :],
                              b.ps[s][:, 3, 0:SEQ], ALU.mult)\
               .then_inc(g("L3f_c", s), 1)
        yield


SCAN_CHUNKS = DC * BLK // 2


def project_states(nc, g, b, block):
    halves = [(n, h) for n in range(4) for h in range(DC)]
    units = [("k", n, h) for n, h in halves] + [("v", n, h) for n, h in halves] + [("q", n, h) for n, h in halves]
    NK, RING = len(halves), 6

    @block.tensor
    def _(pe):
        def norm_sum(n):
            pe.wait_ge(g("k_square"), n + 1)
            if n >= 2:
                pe.wait_ge(g("k_norm"), n - 1)
            pe.matmul(b.pst[:, 6 + n % 2, :], lhsT=b.same_block[:, :], rhs=b.sq[:, n % 2, :], start=True,
                      stop=True, skip_group_check=True).then_inc(g("k_sum"), 1)

        for u, (name, n, h) in enumerate(units):
            if u >= RING:
                before = u - RING
                if before < NK:
                    pe.wait_ge(g("k_square"), before + 1)
                else:
                    pe.wait_ge(g("vq_copied"), before - NK + 1)
            for i in range(DC):
                last = pe.matmul(b.pst[:, u % RING, :], lhsT=b.w0[name][:, i, h * P:(h + 1) * P],
                                 rhs=b.xT_all[:, i, n * 512:(n + 1) * 512], start=(i == 0), stop=(i == DC - 1),
                                 skip_group_check=True)
            last.then_inc(g("projected"), 1)
            if 1 <= u <= NK:
                norm_sum(u - 1)

    @block.scalar
    def _(act):
        def root(n):
            act.wait_ge(g("k_sum"), n + 1)
            if n >= 2:
                act.wait_ge(g("k_ready"), n - 1)
            act.activation(b.nrm[:, n % 2, :], b.pst[:, 6 + n % 2, :], ACT.Sqrt).then_inc(g("k_norm"), 1)

        for u, (n, h) in enumerate(halves):
            act.wait_ge(g("projected"), u + 1)
            act.activation(b.kn[:, h, n * 512:(n + 1) * 512], b.pst[:, u % RING, :], ACT.Copy)\
               .then_inc(g("k_copied"), 1)
            if u >= 2:
                act.wait_ge(g("k_sum"), u - 1)
            act.activation(b.sq[:, u % 2, :], b.pst[:, u % RING, :], ACT.Square).then_inc(g("k_square"), 1)
            if u >= 1:
                root(u - 1)
        root(NK - 1)

    @block.vector
    def _(dve):
        link = Chain(dve, g("dve_chain"))
        for u, (n, h) in enumerate(halves):
            dve.wait_ge(g("k_norm"), u + 1)
            dve.wait_ge(g("k_copied"), u + 1)
            r, k = b.nrm[:, u % 2, :], b.kn[:, h, n * 512:(n + 1) * 512]
            link(dve.tensor_scalar(r, r, 1e-6, None, ALU.add))
            link(dve.reciprocal(r, r))
            dve.tensor_tensor(k, k, r, ALU.mult).then_inc(g("k_ready"), 1)
        for u in range(NK, len(units)):
            name, n, h = units[u]
            dve.wait_ge(g("projected"), u + 1)
            dst = b.v0 if name == "v" else b.q0
            dve.tensor_copy(dst[:, h, n * 512:(n + 1) * 512], b.pst[:, u % RING, :]).then_inc(g("vq_copied"), 1)


def scan_step(nc, g, b, block, t):
    at = lambda a, h: a[:, h, :].rearrange("p (t n) -> p t n", t=NB)[:, t, :]
    wide = lambda a: a.unsqueeze(1).to_broadcast([P, 2, SEQ])
    chunks = [(c // 4, c % 4) for c in range(SCAN_CHUNKS)]
    RING = 6

    @block.vector
    def _(dve):
        link = Chain(dve, g("dve_chain"))
        dve.tensor_copy(b.x[0][:, :, :], b.x_all[:, bass.ds(t * TILES, TILES), :]).then_inc(g("x_in"), 1)

        def products(c):
            h, i = chunks[c]
            dve.tensor_tensor(b.work[:, c, :].rearrange("p (i n) -> p i n", i=2), b.S[:, h, 2 * i:2 * i + 2, :],
                              wide(at(b.kn, h)), ALU.mult).then_inc(g("s_k"), 1)

        def update(c):
            h, i = chunks[c]
            w = b.work[:, c, :].rearrange("p (i n) -> p i n", i=2)
            dve.wait_ge(g("delta"), c + 1)
            link(dve.tensor_tensor(w, b.pst[:, c % RING, :].rearrange("p (i n) -> p i n", i=2),
                                   wide(at(b.kn, h)), ALU.mult))
            dve.tensor_tensor(w, w, b.S[:, h, 2 * i:2 * i + 2, :], ALU.add).then_inc(g("s_new"), 1)

        for c in range(SCAN_CHUNKS):
            products(c)
            if c >= 2:
                update(c - 2)
        update(SCAN_CHUNKS - 2)
        update(SCAN_CHUNKS - 1)
        dve.wait_ge(g("gates"), 2)
        dve.scalar_tensor_tensor(b.hqT[0][:, :, :], b.xhq[0][:, :, :], 1.0, b.xhc[0][:, :, :], ALU.add, ALU.mult)\
           .then_inc(g("gated"), 1)
        dve.wait_ge(g("x_in"), 1)
        norm_dve(dve, link, g, b, 0, "L0a", 3, half=True)
        dve.wait_ge(g("L0a_x", 0), TILES)
        dve.tensor_copy(b.x_all[:, bass.ds(t * TILES, TILES), :], b.x[0][:, :, :]).then_inc(g("x_out"), 1)

    @block.tensor
    def _(pe):
        def delta(c):
            h, i = chunks[c]
            pe.wait_ge(g("s_k"), c + 1)
            if c >= RING:
                pe.wait_ge(g("s_new"), c - RING + 1)
            pe.matmul(b.pst[:, c % RING, :], lhsT=b.minus_same_block[:, :], rhs=b.work[:, c, :], start=True,
                      stop=False, skip_group_check=True)
            for m in range(2):
                last = pe.matmul(b.pst[:, c % RING, m * SEQ:(m + 1) * SEQ], lhsT=b.spread[:, 2 * i + m, :],
                                 rhs=at(b.v0, h), start=False, stop=True, skip_group_check=True)
            last.then_inc(g("delta"), 1)

        def read_out(c):
            h, i = chunks[c]
            pe.wait_ge(g("s_q"), c + 1)
            for m in range(2):
                last = pe.matmul(b.pst[:, 6, h * SEQ:(h + 1) * SEQ], lhsT=b.collect[:, 2 * i + m, :],
                                 rhs=b.sq_out[:, c, m * SEQ:(m + 1) * SEQ], start=(i == 0 and m == 0),
                                 stop=(i == 3 and m == 1), skip_group_check=True)
            if c == SCAN_CHUNKS - 1:
                last.then_inc(g("y"), 1)

        for c in range(SCAN_CHUNKS):
            delta(c)
            if c >= 4:
                read_out(c - 4)
        for c in range(SCAN_CHUNKS - 4, SCAN_CHUNKS):
            read_out(c)
        pe.wait_ge(g("gated"), 1)
        for tt in range(TILES):
            for c in range(DC):
                last = pe.transpose(b.pst[:, 3, tt * D + c * P:tt * D + (c + 1) * P],
                                    b.hqT[0][:, c, tt * P:(tt + 1) * P], b.ident[:, :])
        last.then_inc(g("L0a_out", 0), 1)

    @block.scalar
    def _(act):
        for c in range(SCAN_CHUNKS):
            h, i = chunks[c]
            act.wait_ge(g("s_new"), c + 1)
            act.activation(b.S[:, h, 2 * i:2 * i + 2, :], b.work[:, c, :].rearrange("p (i n) -> p i n", i=2),
                           ACT.Tanh).then_inc(g("s_tanh"), 1)
        act.wait_ge(g("y"), 1)
        y = b.pst[:, 6, :]
        act.activation(b.xhq[0][:, :, :].rearrange("p c n -> p (c n)"), y, ACT.Tanh, scale=0.5).then_inc(g("gates"), 1)
        act.activation(b.xhc[0][:, :, :].rearrange("p c n -> p (c n)"), y, ACT.Square).then_inc(g("gates"), 1)

    @block.gpsimd
    def _(pool):
        for c in range(SCAN_CHUNKS):
            h, i = chunks[c]
            pool.wait_ge(g("s_tanh"), c + 1)
            pool.tensor_tensor(b.sq_out[:, c, :].rearrange("p (i n) -> p i n", i=2), b.S[:, h, 2 * i:2 * i + 2, :],
                               wide(at(b.q0, h)), ALU.mult).then_inc(g("s_q"), 1)
        norm_pool(pool, g, b, 0, "L0a")


FC = FF1 // P


class Scale:

    def __init__(self, g, b, name, col):
        self.g, self.b, self.name, self.col = g, b, name, col

    def pe(self, pe):
        g, b, n = self.g, self.b, self.name
        pe.wait_ge(g(n + "_max"), 1)
        pe.transpose(b.pst[0:1, self.col, 0:P], b.gmax[:, self.col:self.col + 1], b.ident[:, :]).then_inc(g(n + "_row"), 1)
        pe.wait_ge(g(n + "_one"), 1)
        pe.matmul(b.pst[:, self.col, P:P + 1], lhsT=b.ones[0:1, :], rhs=b.gone[0:1, self.col:self.col + 1], start=True,
                  stop=True, skip_group_check=True).then_inc(g(n + "_all"), 1)

    def dve(self, dve, link):
        g, b, n, c = self.g, self.b, self.name, self.col
        dve.wait_ge(g(n + "_row"), 1)
        dve.tensor_reduce(b.gone[0:1, c:c + 1], b.pst[0:1, self.col, 0:P], X, ALU.max).then_inc(g(n + "_one"), 1)
        dve.wait_ge(g(n + "_all"), 1)
        link(dve.tensor_scalar(b.scale[:, c:c + 1], b.pst[:, self.col, P:P + 1], 1.0 / QMAX, 1e-12, ALU.mult, ALU.max))
        link(dve.reciprocal(b.inv[:, c:c + 1], b.scale[:, c:c + 1]))


def quantise_x(nc, g, b, block):
    sc = Scale(g, b, "sx", 0)

    @block.vector
    def _(dve):
        link = Chain(dve, g("dve_chain"))
        dve.tensor_reduce(b.gmax[:, 0:1], b.x_all[:, :, :], XY, ALU.max, apply_absolute_value=True)\
           .then_inc(g("sx_max"), 1)
        sc.dve(dve, link)

    @block.tensor
    def _(pe):
        sc.pe(pe)


def up_and_gate(nc, g, b, block, i):
    T4 = 4
    units = [(w, m) for w in range(2) for m in range(FC)]

    @block.vector
    def _(dve):
        link = Chain(dve, g("dve_chain"))
        link(dve.tensor_scalar(b.xq[:, :, :], b.x_all[:, bass.ds(i * T4, T4), :], b.inv[:, 0:1], ROUND,
                               ALU.mult, ALU.add))
        dve.tensor_scalar(b.xq[:, :, :], b.xq[:, :, :], -ROUND, b.scale[:, 0:1], ALU.add, ALU.mult)\
           .then_inc(g("xq"), 1)
        for n, (w, m) in enumerate(units):
            dve.wait_ge(g("ug_copy"), n + 1)
            dve.tensor_reduce(b.umax[:, w, m, bass.ds(i, 1)], b.ug[w][:, m, bass.ds(i * 512, 512)], X, ALU.max,
                              apply_absolute_value=True).then_inc(g("ug_max"), 1)

    @block.tensor
    def _(pe):
        pe.wait_ge(g("xq"), 1)
        for c in range(DC):
            for t in range(T4):
                last = pe.transpose(b.pst[:, c, t * P:(t + 1) * P], b.xq[:, t, c * P:(c + 1) * P], b.ident[:, :])
        last.then_inc(g("xqt"), 1)
        pe.wait_ge(g("xqT"), 1)
        for n, (w, m) in enumerate(units):
            if n >= 4:
                pe.wait_ge(g("ug_copy"), n - 3)
            for c in range(DC):
                last = pe.matmul(b.pst[:, 2 + n % 4, :], lhsT=b.wug[w][:, c, m * P:(m + 1) * P],
                                 rhs=b.xqT[:, c, :], start=(c == 0), stop=(c == DC - 1), skip_group_check=True)
            last.then_inc(g("ug"), 1)

    @block.scalar
    def _(act):
        act.wait_ge(g("xqt"), 1)
        act.activation(b.xqT[:, :, :], b.pst[:, 0:2, :], ACT.Copy).then_inc(g("xqT"), 1)
        for n, (w, m) in enumerate(units):
            act.wait_ge(g("ug"), n + 1)
            act.activation(b.ug[w][:, m, bass.ds(i * 512, 512)], b.pst[:, 2 + n % 4, :], ACT.Copy)\
               .then_inc(g("ug_copy"), 1)


def gate_products(nc, g, b, block):
    su, sg, s2, so = (Scale(g, b, n, c) for c, n in ((1, "su"), (2, "sg"), (3, "s2"), (4, "so")))
    up, gate = b.ug

    def gated(dve, link, m):
        dve.wait_ge(g("sig"), m + 1)
        link(dve.scalar_tensor_tensor(gate[:, m, :], b.sig[:, m % 2, :], 1.0 / 65536.0, gate[:, m, :],
                                      ALU.mult, ALU.mult))
        g_done = dve.tensor_reduce(b.fmax[:, 0, m:m + 1], gate[:, m, :], X, ALU.max, apply_absolute_value=True)
        g_done.then_inc(g("g2"), 1)
        dve.wait_ge(g("g2"), m + 1)

    @block.tensor
    def _(pe):
        for sc in (su, sg, s2, so):
            sc.pe(pe)

    @block.vector
    def _(dve):
        link = Chain(dve, g("dve_chain"))
        dve.tensor_reduce(b.gmax[:, 1:2], b.umax[:, 0, :, :], XY, ALU.max).then_inc(g("su_max"), 1)
        dve.tensor_reduce(b.gmax[:, 2:3], b.umax[:, 1, :, :], XY, ALU.max).then_inc(g("sg_max"), 1)
        su.dve(dve, link)
        sg.dve(dve, link)
        dve.nop().then_inc(g("scales"), 1)
        for m in range(FC):
            link(dve.tensor_scalar(gate[:, m, :], gate[:, m, :], b.inv[:, 2:3], ROUND, ALU.mult, ALU.add))
            dve.tensor_scalar(gate[:, m, :], gate[:, m, :], -ROUND, b.scale[:, 2:3], ALU.add, ALU.mult)\
               .then_inc(g("gq"), 1)
            if m >= 1:
                gated(dve, link, m - 1)
        gated(dve, link, FC - 1)
        dve.tensor_reduce(b.gmax[:, 3:4], b.fmax[:, 0, :], X, ALU.max).then_inc(g("s2_max"), 1)
        s2.dve(dve, link)
        for m in range(FC):
            link(dve.tensor_scalar(gate[:, m, :], gate[:, m, :], b.inv[:, 3:4], ROUND, ALU.mult, ALU.add))
            link(dve.tensor_scalar(gate[:, m, :], gate[:, m, :], -ROUND, b.scale[:, 3:4], ALU.add, ALU.mult))
            dve.wait_ge(g("uq"), m + 1)
            link(dve.tensor_tensor(gate[:, m, :], gate[:, m, :], up[:, m, :], ALU.mult))
            link(dve.tensor_reduce(b.fmax[:, 1, m:m + 1], gate[:, m, :], X, ALU.max, apply_absolute_value=True))
        dve.tensor_reduce(b.gmax[:, 4:5], b.fmax[:, 1, :], X, ALU.max).then_inc(g("so_max"), 1)
        so.dve(dve, link)

    @block.scalar
    def _(act):
        for m in range(FC):
            act.wait_ge(g("gq"), m + 1)
            if m >= 2:
                act.wait_ge(g("g2"), m - 1)
            act.activation(b.sig[:, m % 2, :], gate[:, m, :], ACT.Tanh, scale=0.5).then_inc(g("th"), 1)

    @block.gpsimd
    def _(pool):
        link = Chain(pool, g("pool_chain"))
        pool.wait_ge(g("scales"), 1)
        for m in range(FC):
            link(pool.tensor_scalar(up[:, m, :], up[:, m, :], b.inv[:, 1:2], ROUND, ALU.mult, ALU.add))
            pool.tensor_scalar(up[:, m, :], up[:, m, :], -ROUND, b.scale[:, 1:2], ALU.add, ALU.mult)\
                .then_inc(g("uq"), 1)
            pool.wait_ge(g("th"), m + 1)
            s = b.sig[:, m % 2, :]
            link(pool.tensor_scalar(s, s, 32768.0, ROUND + 32768.0, ALU.mult, ALU.add))
            pool.tensor_scalar(s, s, -ROUND, 65535.0, ALU.add, ALU.min).then_inc(g("sig"), 1)


def down(nc, g, b, block, i):
    @block.vector
    def _(dve):
        link = Chain(dve, g("dve_chain"))
        for s in range(SB):
            for t in range(TILES):
                dve.tensor_copy(b.x[s][:, t, :], b.x_all[:, bass.ds((i * SB + s) * TILES + t, 1), :]
                                .rearrange("p a n -> p (a n)")).then_inc(g("x_in", s), 1)
        for s in range(SB):
            o = b.oq[s]
            link(dve.tensor_scalar(o[:, :, :], b.ug[1][:, :, bass.ds((i * SB + s) * SEQ, SEQ)], b.inv[:, 4:5],
                                   ROUND, ALU.mult, ALU.add))
            dve.tensor_scalar(o[:, :, :], o[:, :, :], -ROUND, b.scale[:, 4:5], ALU.add, ALU.mult)\
               .then_inc(g("oq", s), 1)
        for s in range(SB):
            dve.wait_ge(g("x_in", s), TILES)
            norm_dve(dve, link, g, b, s, "L1f", 0)
        for s in range(SB):
            dve.wait_ge(g("L1f_x", s), TILES)
            for t in range(TILES):
                dve.tensor_copy(b.x_all[:, bass.ds((i * SB + s) * TILES + t, 1), :].rearrange("p a n -> p (a n)"),
                                b.x[s][:, t, :]).then_inc(g("x_out", s), 1)

    @block.tensor
    def _(pe):
        for s in range(SB):
            pe.wait_ge(g("oq", s), 1)
            for t in range(TILES):
                for m in range(FC):
                    last = pe.matmul(b.ps[s][:, 0, t * D:(t + 1) * D], lhsT=b.oq[s][:, m, t * P:(t + 1) * P],
                                     rhs=b.wd[:, m, :], start=(m == 0), stop=(m == FC - 1), skip_group_check=True)
            last.then_inc(g("L1f_out", s), 1)

    @block.gpsimd
    def _(pool):
        for s in range(SB):
            norm_pool(pool, g, b, s, "L1f")


def quantise_weights(nc, g, b, block):
    todo = [(b.wnat[n], b.wsc[n]) for n in range(3)]

    @block.vector
    def _(dve):
        link = Chain(dve, g("dve_chain"))
        for n, (w, sc) in enumerate(todo):
            blocks = w.rearrange("p a (k r) -> p (a k) r", r=32)
            wide = lambda a: a.unsqueeze(2).to_broadcast([P, 48, 32])
            link(dve.tensor_reduce(sc[:, 0, :], blocks, X, ALU.max, apply_absolute_value=True))
            link(dve.tensor_scalar(sc[:, 0, :], sc[:, 0, :], 1.0 / 7.0, 1e-12, ALU.mult, ALU.max))
            link(dve.reciprocal(sc[:, 1, :], sc[:, 0, :]))
            link(dve.tensor_tensor(blocks, blocks, wide(sc[:, 1, :]), ALU.mult))
            link(dve.tensor_scalar(blocks, blocks, ROUND, -ROUND, ALU.add, ALU.add))
            dve.tensor_tensor(blocks, blocks, wide(sc[:, 0, :]), ALU.mult).then_inc(g("wq"), 1)

    @block.tensor
    def _(pe):
        for n in range(3):
            pe.wait_ge(g("wq"), n + 1)
            w = b.wnat[n]
            if n >= 2:
                pe.wait_ge(g("wqT"), 3 * (n - 1))
            for k in range(12):
                a, c = (k // 2, k % 2) if n < 2 else (k // 6, k % 6)
                bank = 3 * (n % 2) + (k // 4)
                last = pe.transpose(b.pst[:, bank, (k % 4) * P:(k % 4 + 1) * P], w[:, a, c * P:(c + 1) * P],
                                    b.ident[:, :])
                if k % 4 == 3:
                    last.then_inc(g("wqt"), 1)

    @block.scalar
    def _(act):
        for n in range(3):
            for q in range(3):
                act.wait_ge(g("wqt"), 3 * n + q + 1)
                bank = b.pst[:, 3 * (n % 2) + q, :]
                if n < 2:
                    dst = b.wug[n][:, :, q * 2 * P:(q + 1) * 2 * P].rearrange("p c (a o) -> p a c o", a=2)
                    src = bank.rearrange("p (a c o) -> p a c o", a=2, c=2)
                    act.activation(dst, src, ACT.Copy).then_inc(g("wqT"), 1)
                else:
                    for j in range(4):
                        k = 4 * q + j
                        ins = act.activation(b.wd[:, k % 6, (k // 6) * P:(k // 6 + 1) * P],
                                             bank[:, j * P:(j + 1) * P], ACT.Copy)
                    ins.then_inc(g("wqT"), 1)


class Buffers:
    pass


def region(nc, body):
    with ExitStack() as ctx:
        g = Signals(nc, ctx)
        with nc.Block(no_gpsimd_drain=True) as block:
            body(g, block)
        runs = g.runs()
        for r in runs[1:]:
            nc.gpsimd.sem_clear(r)
        nc.all_engine_barrier(sems_to_clear=runs[0])


def load(block, g, pairs):
    @block.sync
    def _(sp):
        for dst, src in pairs[0::2]:
            sp.dma_start(dst, src).then_inc(g("loaded"), 16)
        sp.wait_ge(g("loaded"), 16 * len(pairs))

    return pairs[1::2], 16 * len(pairs)


def chunked(ap):
    return ap.rearrange("(c p) n -> p c n", p=P)


def pairs_of(b, sb):
    return lambda name, shape, dt=F32: [sb(f"{b.phase}_{name}_{s}", shape, dt) for s in range(SB)]


def common_buffers(b, pair):
    b.x = pair("x", [P, TILES, D])
    b.r = pair("r", [P, TILES, D])
    b.st = pair("st", [P, TILES, 6])
    b.mv = pair("mv", [P, TILES, 2])
    b.rstd = pair("rstd", [P, TILES])


def heads_buffers(b, pair):
    b.xT = pair("xT", [P, DC, SEQ])
    b.ctx = pair("ctx", [SK, D])
    b.ctxT = pair("ctxT", [P, DC, SK])
    b.qT = pair("qT", [P, HC, SEQ])
    b.kT = pair("kT", [P, HC, SEQ])
    b.vn = pair("vn", [P, TILES, NH * (DH + 1)])
    b.PT = pair("PT", [P, 4, 512])
    b.mneg = pair("mneg", [P, TILES, HC * P])
    b.ri = pair("ri", [P, NH])
    b.A = pair("A", [P, TILES, SK])
    b.AT = pair("AT", [SK, SEQ])
    b.nm = pair("nm", [P, TILES])
    b.ssum = pair("ssum", [P, TILES])


def clear_spares(pool, b):
    for s in range(SB):
        pool.memset(b.mneg[s][:, :, :], 0.0)
        pool.memset(b.vn[s][:, :, :], 1.0)


def take_in(dve, g, b, s, i):
    for t in range(TILES):
        dve.tensor_copy(b.x[s][:, t, :], b.x_all[:, bass.ds((i * SB + s) * TILES + t, 1), :]
                        .rearrange("p a n -> p (a n)")).then_inc(g("in_x", s), 1)
    dve.wait_ge(g("in_x", s), TILES)


def put_back(dve, g, b, s, i, L):
    dve.wait_ge(g(L + "_x", s), TILES)
    for t in range(TILES):
        dve.tensor_copy(b.x_all[:, bass.ds((i * SB + s) * TILES + t, 1), :].rearrange("p a n -> p (a n)"),
                        b.x[s][:, t, :]).then_inc(g("back", s), 1)


def load_context(sp, g, b, i, s):
    sp.dma_start(b.ctx[s][:, :], b.dram["ctx"].rearrange("(i s) k d -> i s k d", s=SB)[i, s])\
        .then_inc(g("ctx", s), 16)
    sp.dma_start(b.ctxT[s][:, :, :], b.dram["ctxT"].rearrange("(i s) (c p) k -> i s p c k", s=SB, p=P)[i, s])\
        .then_inc(g("ctx", s), 16)


def phase_state(nc, b):
    b.phase = "state"
    with ExitStack() as ctx:
        sb = lambda n, shape, dt=F32: ctx.enter_context(nc.sbuf_tensor(n, shape, dt))
        d = b.dram
        pair = pairs_of(b, sb)
        common_buffers(b, pair)
        b.hqT = pair("hqT", [P, DC, SEQ])
        b.xhq = pair("xhq", [P, DC, SEQ])
        b.xhc = pair("xhc", [P, DC, SEQ])
        b.kn, b.v0, b.q0 = (sb(n, [P, DC, TOKENS]) for n in ("kn", "v0", "q0"))
        b.same_block, b.minus_same_block = sb("same_block", [P, P]), sb("minus_same_block", [P, P])
        b.spread, b.collect = sb("spread", [P, BLK, P]), sb("collect", [P, BLK, P])
        with ExitStack() as inner:
            sbi = lambda n, shape, dt=F32: inner.enter_context(nc.sbuf_tensor(n, shape, dt))
            b.xT_all = sbi("xT_all", [P, DC, TOKENS])
            b.w0 = {n: sbi("w0" + n, [P, DC, D]) for n in "kvq"}
            b.sq, b.nrm = sbi("sq", [P, 2, 512]), sbi("nrm", [P, 2, 512])

            def begin(g, block):
                pairs = [(b.xT_all[:, :, :], chunked(d["xT"])),
                         (b.x_all[:, :, :], d["x"].rearrange("(a p) n -> p a n", p=P))]
                pairs += [(b.w0[n][:, :, :], chunked(d["w0" + n])) for n in "kvq"]
                pairs += [(b.same_block[:, :], d["same_block"]), (b.ident[:, :], d["ident"]),
                          (b.spread[:, :, :], d["spread"]), (b.collect[:, :, :], d["collect"])]
                rest, total = load(block, g, pairs)

                @block.scalar
                def _(act):
                    for dst, src in rest:
                        act.dma_start(dst, src).then_inc(g("loaded"), 16)
                    act.wait_ge(g("loaded"), total)

                @block.vector
                def _(dve):
                    dve.memset(b.ones[:, :], 1.0)
                    dve.memset(b.minus_half[:, :], -0.5)
                    dve.wait_ge(g("loaded"), total)
                    dve.tensor_copy(b.identb[:, :], b.ident[:, :])
                    dve.tensor_scalar(b.minus_same_block[:, :], b.same_block[:, :], -1.0, None, ALU.mult)

            region(nc, begin)
            region(nc, lambda g, block: project_states(nc, g, b, block))
        b.S = sb("S", [P, DC, BLK, SEQ])
        b.work, b.sq_out = sb("work", [P, SCAN_CHUNKS, 512]), sb("sq_out", [P, SCAN_CHUNKS, 512])

        def clear(g, block):
            @block.vector
            def _(dve):
                dve.memset(b.S[:, :, :, :], 0.0).then_inc(g("cleared"), 1)

        region(nc, clear)
        with nc.Fori(0, NB) as t:
            region(nc, lambda g, block: scan_step(nc, g, b, block, t))


def phase_first(nc, b):
    b.phase = "first"
    with ExitStack() as ctx:
        sb = lambda n, shape, dt=F32: ctx.enter_context(nc.sbuf_tensor(n, shape, dt))
        d = b.dram
        pair = pairs_of(b, sb)
        common_buffers(b, pair)
        heads_buffers(b, pair)
        b.flow_m = pair("flow_m", [P, DC, SK])
        b.sim = pair("sim", [P, TILES, SK])
        b.nM = pair("nM", [1, 1])
        b.nMb = pair("nMb", [P, 1])
        b.ecol = pair("ecol", [P, TILES])
        b.hc = pair("hc", [P, DC])
        b.sc = pair("sc", [P, TILES, P])
        b.pb = pair("pb", [P, TILES, P])
        b.pbT = pair("pbT", [P, SEQ])
        b.oT = pair("oT", [P, DC, SEQ])
        b.O = pair("O", [P, TILES, D])
        b.mask_u8 = pair("mask_u8", [P, TILES, NH, SK], U8)
        b.maskT_u8 = pair("maskT_u8", [SK, NH, SEQ], U8)
        b.mask = pair("mask", [P, TILES, NH, SK], BF16)
        b.maskT = pair("maskT", [SK, NH, SEQ], BF16)
        b.hqT, b.xhq = [q[:, 0:DC, :] for q in b.qT], [q[:, DC:HC, :] for q in b.qT]
        b.xhc = [k[:, 0:DC, :] for k in b.kT]
        b.bq, b.bk, b.bv = b.hqT, b.xhq, b.xhc
        wsim = sb("wsim", [P, 3 * DC])
        b.w1, w2, b.w3 = wsim[:, 0:2], wsim[:, 2:4], wsim[:, 4:6]
        b.b_sim, b.w2_wide = sb("b_sim", [P, 1]), sb("w2_wide", [P, DC, P])
        wqv, w0f = sb("wqv", [P, 4 * DC, D]), sb("w0f", [P, DC, D])
        l1a, l1o = sb("l1a", [P, DC, 3 * D]), sb("l1o", [P, DC, D])
        lq, lk = sb("lq", [P, DC, HC * P]), sb("lk", [P, DC, HC * P])
        lv, lo = sb("lv", [P, DC, D]), sb("lo", [P, DC, D])
        row = {n: sb("row_" + n, [P, D]) for n in ("qv", "f0", "o1", "v1", "x1")}
        qb, kb = sb("qb", [P, HC]), sb("kb", [P, HC])
        b.causal32 = sb("causal32", [P, P])
        ld, da = sb("ld", [100, 4]), sb("da", [100, D])
        lu, ua = sb("lu", [4, 50]), sb("ua", [50, D])
        t1, t2 = sb("t1", [4, D]), sb("t2", [50, D])
        b.w = {"L0x": wqv, "L0f": w0f, "L1a": l1a, "L1x": {"q": lq, "k": lk, "v": lv}}
        b.wo = {"L1a": l1o, "L1x": lo}
        b.k_bias = {"L1x": kb}
        b.heads = {"L1x": Heads("L1x", [(0, SK)], DH, (4, 4, 1), "per_head")}

        def begin(g, block):
            pairs = [(wsim[:, :], d["wsim"]), (b.b_sim[:, :], d["b_sim"].partition_broadcast(P)),
                     (wqv[:, :, :], chunked(d["wqv"])), (w0f[:, :, :], chunked(d["w0f"])),
                     (l1a[:, :, :], chunked(d["w1a"])), (l1o[:, :, :], chunked(d["w1o"])),
                     (lq[:, :, :], chunked(d["w1xq"])), (lk[:, :, :], chunked(d["w1xk"])),
                     (lv[:, :, :], chunked(d["w1xv"])), (lo[:, :, :], chunked(d["w1xo"])),
                     (qb[:, :], d["b1xq"]), (kb[:, :], d["b1xk"]), (b.causal32[:, :], d["causal"]),
                     (ld[:, :], d["ld"]), (da[:, :], d["da"]), (lu[:, :], d["lu"]), (ua[:, :], d["ua"])]
            pairs += [(row[n][:, :], d["row_" + n].partition_broadcast(P)) for n in row]
            rest, total = load(block, g, pairs)

            @block.scalar
            def _(act):
                for dst, src in rest:
                    act.dma_start(dst, src).then_inc(g("loaded"), 16)
                act.wait_ge(g("lora"), 1)
                act.activation(t1[:, :], b.pst[0:4, 0, 0:D], ACT.Copy).then_inc(g("lora_copied"), 1)
                act.wait_ge(g("lora"), 2)
                act.activation(t2[:, :], b.pst[0:50, 1, 0:D], ACT.Copy).then_inc(g("lora_copied"), 1)

            @block.tensor
            def _(pe):
                pe.wait_ge(g("loaded"), total)
                pe.matmul(b.pst[0:4, 0, 0:D], lhsT=ld[:, :], rhs=da[:, :], start=True, stop=True)\
                  .then_inc(g("lora"), 1)
                pe.wait_ge(g("lora_copied"), 1)
                pe.matmul(b.pst[0:50, 1, 0:D], lhsT=lu[:, :], rhs=t1[:, :], start=True, stop=True)\
                  .then_inc(g("lora"), 1)
                pe.wait_ge(g("lora_copied"), 2)
                for c in range(DC):
                    last = pe.matmul(b.pst[:, 2, c * D:(c + 1) * D], lhsT=t2[:, c * P:(c + 1) * P], rhs=ua[:, :],
                                     start=True, stop=True, skip_group_check=True)
                last.then_inc(g("lora"), 1)

            @block.vector
            def _(dve):
                dve.wait_ge(g("loaded"), total)
                dve.tensor_copy(b.w2_wide[:, :, :], w2.unsqueeze(2).to_broadcast([P, DC, P]))
                dve.wait_ge(g("lora"), 3)
                dve.tensor_tensor(w0f[:, :, :], w0f[:, :, :], b.pst[:, 2, :].rearrange("p (c n) -> p c n", c=DC),
                                  ALU.add)

            @block.gpsimd
            def _(pool):
                clear_spares(pool, b)

        region(nc, begin)

        def turn(i):
            def body(g, block):
                @block.sync
                def _(sp):
                    for s in range(SB):
                        load_context(sp, g, b, i, s)
                    for s in range(SB):
                        for t in range(TILES):
                            src = d["mask"].rearrange("(i s) (t p) h k -> i s t p h k", s=SB, p=P)[i, s, t]
                            sp.dma_start(b.mask_u8[s][:, t, :, :], src).then_inc(g("mask_in", s), 16)
                        src = d["maskT"].rearrange("(i s) k h q -> i s k h q", s=SB)[i, s]
                        sp.dma_start(b.maskT_u8[s][:, :, :], src).then_inc(g("mask_in", s), 16)

                @block.gpsimd
                def _(pool):
                    def masks(s):
                        pool.wait_ge(g("mask_in", s), 48)
                        pool.tensor_scalar(b.mask[s][:, :, :, :], b.mask_u8[s][:, :, :, :], NEG, None, ALU.mult)\
                            .then_inc(g("L1x_mask", s), 1)
                        pool.tensor_scalar(b.maskT[s][:, :, :], b.maskT_u8[s][:, :, :], NEG, None, ALU.mult)\
                            .then_inc(g("L1x_mask", s), 1)

                    for s in range(SB):
                        norm_pool(pool, g, b, s, "L0x")
                    masks(0)
                    for s in range(SB):
                        norm_pool(pool, g, b, s, "L0f")
                    masks(1)
                    for L in ("L1a", "L1x"):
                        for s in range(SB):
                            norm_pool(pool, g, b, s, L)

                def pe_program(pe, s):
                    norm_pe(pe, g, b, s, "in", 2)
                    yield
                    yield from flow_pe(pe, g, b, s, "in")
                    norm_pe(pe, g, b, s, "L0x", 2)
                    yield
                    pe.wait_ge(g("L0x_xT", s), 1)
                    project(pe, b.ps[s], 0, b.xT[s], w0f).then_inc(g("L0f_out", s), 1)
                    yield
                    norm_pe(pe, g, b, s, "L0f", 2)
                    yield
                    yield from block_pe(pe, g, b, s, "L0f")
                    norm_pe(pe, g, b, s, "L1a", 2)
                    yield
                    yield from cross_pe(pe, g, b, s, "L1x", "L1a")
                    yield from heads_pe(pe, g, b, s, b.heads["L1x"])

                @block.tensor
                def _(pe):
                    side_by_side([pe_program(pe, s) for s in range(SB)])

                def act_program(act, s):
                    norm_act(act, g, b, s, "in", 2)
                    yield
                    yield from flow_act(act, g, b, s)
                    norm_act(act, g, b, s, "L0x", 2)
                    yield
                    norm_act(act, g, b, s, "L0f", 2)
                    yield
                    yield from block_act(act, g, b, s)
                    norm_act(act, g, b, s, "L1a", 2)
                    yield
                    yield from cross_act(act, g, b, s, "L1x", qb)
                    yield from heads_act(act, g, b, s, b.heads["L1x"])

                @block.scalar
                def _(act):
                    side_by_side([act_program(act, s) for s in range(SB)])

                def dve_program(dve, link, s):
                    take_in(dve, g, b, s, i)
                    yield
                    yield from flow_dve(dve, link, g, b, s)
                    norm_dve(dve, link, g, b, s, "L0x", 0, row["qv"][:, :])
                    yield
                    norm_dve(dve, link, g, b, s, "L0f", 0, row["f0"][:, :])
                    yield
                    yield from block_dve(dve, link, g, b, s)
                    norm_dve(dve, link, g, b, s, "L1a", 0, row["o1"][:, :])
                    yield
                    yield from cross_dve(dve, g, b, s, "L1x", row["v1"])
                    yield from heads_dve(dve, link, g, b, s, b.heads["L1x"])
                    norm_dve(dve, link, g, b, s, "L1x", 1, row["x1"][:, :])
                    yield
                    put_back(dve, g, b, s, i, "L1x")

                @block.vector
                def _(dve):
                    link = Chain(dve, g("dve_chain"))
                    side_by_side([dve_program(dve, link, s) for s in range(SB)])

            return body

        with nc.Fori(0, NB // SB) as i:
            region(nc, turn(i))


def phase_quantised(nc, b):
    b.phase = "quantised"
    with ExitStack() as ctx:
        sb = lambda n, shape, dt=F32: ctx.enter_context(nc.sbuf_tensor(n, shape, dt))
        d = b.dram
        b.ug = [sb("up", [P, FC, TOKENS]), sb("gate", [P, FC, TOKENS])]
        b.wd = sb("wd", [P, FC, D])
        b.gmax, b.gone, b.scale, b.inv = sb("gmax", [P, 5]), sb("gone", [1, 5]), sb("scale", [P, 5]), sb("inv", [P, 5])
        b.umax, b.fmax = sb("umax", [P, 2, FC, 4]), sb("fmax", [P, 2, FC])
        with ExitStack() as inner:
            sbi = lambda n, shape, dt=F32: inner.enter_context(nc.sbuf_tensor(n, shape, dt))
            b.wug = [sbi("wup", [P, DC, FF1]), sbi("wgate", [P, DC, FF1])]
            shapes = [(FC, D), (FC, D), (DC, FF1)]
            wn = [sbi(f"wnat{n}", [P, a, m]) for n, (a, m) in enumerate(shapes)]
            b.wnat = [w[:, :, :] for w in wn]
            b.wsc = [sbi(f"wsc{n}", [P, 2, 48]) for n in range(3)]
            b.xq, b.xqT = sbi("xq", [P, 4, D]), sbi("xqT", [P, DC, 512])

            def begin(g, block):
                pairs = [(wn[n][:, :, :], chunked(d[k])) for n, k in enumerate(("w_up", "w_gate", "w_down"))]
                rest, total = load(block, g, pairs)

                @block.scalar
                def _(act):
                    for dst, src in rest:
                        act.dma_start(dst, src).then_inc(g("loaded"), 16)

            region(nc, begin)
            region(nc, lambda g, block: quantise_weights(nc, g, b, block))
            region(nc, lambda g, block: quantise_x(nc, g, b, block))
            with nc.Fori(0, 4) as i:
                region(nc, lambda g, block: up_and_gate(nc, g, b, block, i))
        with ExitStack() as inner:
            b.sig = inner.enter_context(nc.sbuf_tensor("sig", [P, 2, TOKENS], F32))
            region(nc, lambda g, block: gate_products(nc, g, b, block))
        pair = pairs_of(b, sb)
        common_buffers(b, pair)
        b.oq = pair("oq", [P, FC, SEQ])
        with nc.Fori(0, NB // SB) as i:
            region(nc, lambda g, block: down(nc, g, b, block, i))


def phase_second(nc, b):
    b.phase = "second"
    with ExitStack() as ctx:
        sb = lambda n, shape, dt=F32: ctx.enter_context(nc.sbuf_tensor(n, shape, dt))
        d = b.dram
        pair = pairs_of(b, sb)
        common_buffers(b, pair)
        heads_buffers(b, pair)
        b.vw = pair("vw", [P, TILES, NH * (DV2 + 1)])
        b.oT = pair("oT", [P, NH * DV2 // P, SEQ])
        b.O = pair("O", [P, TILES, NH * DV2])
        b.hT = b.oT
        aq, ak, av = sb("aq", [P, DC, HC * P]), sb("ak", [P, DC, HC * P]), sb("av", [P, DC, NH * DV2])
        ao = sb("ao", [P, NH * DV2 // P, D])
        xq, xk, xv, xo = sb("xq2", [P, DC, HC * P]), sb("xk2", [P, DC, HC * P]), sb("xv2", [P, DC, D]), sb("xo2", [P, DC, D])
        f1, f2 = sb("f1", [P, DC, FF2]), sb("f2", [P, FF2 // P, D])
        b.b1, row_b2, kb = sb("b1", [P, FF2 // P]), sb("row_b2", [P, D]), sb("kb2", [P, HC])
        causal32 = sb("causal32b", [P, P])
        causalT32 = sb("causalT32", [P, P])
        b.causal, b.causalT = sb("causalb", [P, P], BF16), sb("causalTb", [P, P], BF16)
        sm8, smT8 = sb("sm8", [P, TILES, SK], U8), sb("smT8", [SK, SEQ], U8)
        b.smask, b.smaskT = sb("smask", [P, TILES, SK], BF16), sb("smaskT", [SK, SEQ], BF16)
        valid, gam = sb("valid", [P, TILES]), sb("gam", [P, 2])
        b.w = {"L2a": {"q": aq, "k": ak, "v": av}, "L2x": {"q": xq, "k": xk, "v": xv}, "L2f1": f1, "L2f2": f2}
        b.wo = {"L2a": ao, "L2x": xo}
        b.k_bias = {"L2a": kb, "L2x": kb}
        b.heads = {"L2a": Heads("L2a", [(0, P), (P, P)], DV2, (1, 4, 2), "causal"),
                   "L2x": Heads("L2x", [(0, SK)], DH, (4, 4, 1), "shared")}

        def begin(g, block):
            pairs = [(w[:, :, :], chunked(d[n])) for w, n in (
                (aq, "w2aq"), (ak, "w2ak"), (av, "w2av"), (ao, "w2ao"), (xq, "w2xq"), (xk, "w2xk"), (xv, "w2xv"),
                (xo, "w2xo"), (f1, "w2f1"), (f2, "w2f2"))]
            pairs += [(b.b1[:, :], d["b2f1"]), (row_b2[:, :], d["row_b2"].partition_broadcast(P)),
                      (kb[:, :], d["k_one"]), (causal32[:, :], d["causal"]), (causalT32[:, :], d["causalT"]),
                      (sm8[:, :, :], d["smask"].rearrange("(t p) k -> p t k", p=P)), (smT8[:, :], d["smaskT"])]
            rest, total = load(block, g, pairs)

            @block.scalar
            def _(act):
                for dst, src in rest:
                    act.dma_start(dst, src).then_inc(g("loaded"), 16)

            @block.gpsimd
            def _(pool):
                clear_spares(pool, b)
                for s in range(SB):
                    pool.memset(b.vw[s][:, :, :], 1.0)

            @block.tensor
            def _(pe):
                pe.wait_ge(g("sums"), 2)
                pe.matmul(b.pst[:, 0, 0:2], lhsT=b.ones[:, :], rhs=gam[:, :], start=True, stop=True)\
                  .then_inc(g("gamma"), 1)

            @block.vector
            def _(dve):
                link = Chain(dve, g("dve_chain"))
                dve.wait_ge(g("loaded"), total)
                for n, w in enumerate((f1, f2)):
                    dve.tensor_reduce(gam[:, n:n + 1], w[:, :, :], XY, ALU.add, apply_absolute_value=True)\
                       .then_inc(g("sums"), 1)
                dve.tensor_copy(b.causal[:, :], causal32[:, :])
                dve.tensor_copy(b.causalT[:, :], causalT32[:, :])
                dve.tensor_scalar(b.smask[:, :, :], sm8[:, :, :], -NEG, NEG, ALU.mult, ALU.add)
                dve.tensor_scalar(b.smaskT[:, :], smT8[:, :], -NEG, NEG, ALU.mult, ALU.add)
                dve.tensor_reduce(valid[:, :], sm8[:, :, :], X, ALU.max)
                dve.wait_ge(g("gamma"), 1)
                link(dve.tensor_scalar(gam[:, :], b.pst[:, 0, 0:2], 1.0 / (FF2 * D), EPS, ALU.mult, ALU.add))
                link(dve.reciprocal(gam[:, :], gam[:, :]))
                for n, w in enumerate((f1, f2)):
                    link(dve.tensor_scalar(w[:, :, :], w[:, :, :], gam[:, n:n + 1], ROUND, ALU.mult, ALU.add))
                    link(dve.tensor_scalar(w[:, :, :], w[:, :, :], -ROUND, 1.0, ALU.add, ALU.min))
                    link(dve.tensor_scalar(w[:, :, :], w[:, :, :], -1.0, None, ALU.max))

        region(nc, begin)

        def turn(i):
            def body(g, block):
                @block.sync
                def _(sp):
                    for s in range(SB):
                        load_context(sp, g, b, i, s)

                @block.gpsimd
                def _(pool):
                    for L in ("L2a", "L2x", "L2f"):
                        for s in range(SB):
                            norm_pool(pool, g, b, s, L)

                def pe_program(pe, s):
                    norm_pe(pe, g, b, s, "in", 3)
                    yield
                    yield from causal_pe(pe, g, b, s, "in")
                    norm_pe(pe, g, b, s, "L2a", 3)
                    yield
                    yield from cross_pe(pe, g, b, s, "L2x", "L2a")
                    yield from heads_pe(pe, g, b, s, b.heads["L2x"])
                    norm_pe(pe, g, b, s, "L2x", 3)
                    yield
                    yield from ternary_pe(pe, g, b, s, "L2x")

                @block.tensor
                def _(pe):
                    side_by_side([pe_program(pe, s) for s in range(SB)])

                def act_program(act, s):
                    norm_act(act, g, b, s, "in", 3)
                    yield
                    yield from causal_act(act, g, b, s)
                    norm_act(act, g, b, s, "L2a", 3)
                    yield
                    yield from cross_act(act, g, b, s, "L2x")
                    yield from heads_act(act, g, b, s, b.heads["L2x"])
                    norm_act(act, g, b, s, "L2x", 3)
                    yield
                    yield from ternary_act(act, g, b, s)

                @block.scalar
                def _(act):
                    side_by_side([act_program(act, s) for s in range(SB)])

                def dve_program(dve, link, s):
                    take_in(dve, g, b, s, i)
                    yield
                    yield from causal_dve(dve, link, g, b, s)
                    norm_dve(dve, link, g, b, s, "L2a", 1)
                    yield
                    yield from cross_dve(dve, g, b, s, "L2x")
                    yield from heads_dve(dve, link, g, b, s, b.heads["L2x"], valid)
                    norm_dve(dve, link, g, b, s, "L2x", 1)
                    yield
                    norm_dve(dve, link, g, b, s, "L2f", 0, row_b2[:, :])
                    yield
                    put_back(dve, g, b, s, i, "L2f")

                @block.vector
                def _(dve):
                    link = Chain(dve, g("dve_chain"))
                    side_by_side([dve_program(dve, link, s) for s in range(SB)])

            return body

        with nc.Fori(0, NB // SB) as i:
            region(nc, turn(i))


def phase_third(nc, b, out):
    b.phase = "third"
    with ExitStack() as ctx:
        sb = lambda n, shape, dt=F32: ctx.enter_context(nc.sbuf_tensor(n, shape, dt))
        d = b.dram
        pair = pairs_of(b, sb)
        common_buffers(b, pair)
        heads_buffers(b, pair)
        b.oT = pair("oT", [P, DC, SEQ])
        b.O = pair("O", [P, TILES, D])
        b.rc = pair("rc", [P, 2, SEQ])
        b.rs = pair("rs", [P, 2, SEQ])
        b.th = pair("th", [P, TILES * NE])
        b.raw = pair("raw", [P, TILES * NE])
        b.lg = pair("lg", [P, TILES, NE])
        b.m8 = pair("m8", [P, TILES, 8])
        b.i8 = pair("i8", [P, TILES, 8], U32)
        b.f8 = pair("f8", [P, TILES, 8])
        b.sel = pair("sel", [P, TILES, NE])
        b.gw = pair("gw", [P, TILES, NE])
        b.gT = pair("gT", [NE, SEQ])
        b.t3 = pair("t3", [P, 2, SEQ])
        b.z3 = pair("z3", [P, 2, SEQ])
        b.a3 = pair("a3", [P, 2, SEQ])
        b.he = pair("he", [P, 2, SEQ])
        w3 = {n: sb("w3a_" + n, [P, DC, HC * P]) for n in ("q", "q_rot", "k", "k_rot")}
        w3["v"] = sb("w3a_v", [P, DC, D])
        w3o = sb("w3o", [P, DC, D])
        b.rope_bias = {n: sb("rb_" + n, [P, HC]) for n in ("q", "q_rot", "k", "k_rot")}
        b.cos, b.sin = sb("cos", [P, SEQ]), sb("sin", [P, SEQ])
        b.v_bias, row_o = {"L3a": sb("v_bias", [P, D])}, sb("row_o3", [P, D])
        b.w1e, b.w3e = sb("w1e", [P, UNITS3, DC, FF3]), sb("w3e", [P, UNITS3, DC, FF3])
        b.w2e = sb("w2e", [P, UNITS3, D])
        b.b1e_half, b.b3e, b.b2e = sb("b1e", [P, UNITS3]), sb("b3e", [P, UNITS3]), sb("b2e", [NE, D])
        b.gate_w, b.expert_bias = sb("gate_w", [P, DC, NE]), sb("expert_bias", [P, NE])
        b.pick, b.iota, b.sb2_twice = sb("pick", [NE, NE, P]), sb("iota", [P, NE]), sb("sb2", [1, 2 * D])
        b.w, b.wo = {"L3a": w3}, {"L3a": w3o}
        b.heads = {"L3a": Heads("L3a", [(0, P), (P, P)], DH, (0, 0, 1))}

        def begin(g, block):
            pairs = [(w3[n][:, :, :], chunked(d["w3" + n])) for n in w3]
            pairs += [(b.rope_bias[n][:, :], d["rb_" + n]) for n in b.rope_bias]
            pairs += [(w3o[:, :, :], chunked(d["w3o"])), (b.cos[:, :], d["cos"]), (b.sin[:, :], d["sin"]),
                      (b.v_bias["L3a"][:, :], d["row_v3"].partition_broadcast(P)),
                      (row_o[:, :], d["row_o3"].partition_broadcast(P)),
                      (b.w1e[:, :, :, :], d["w1e"].rearrange("e (c p) f -> p e c f", p=P)),
                      (b.w3e[:, :, :, :], d["w3e"].rearrange("e (c p) f -> p e c f", p=P)),
                      (b.w2e[:, :, :], d["w2e"].rearrange("e p n -> p e n")),
                      (b.b1e_half[:, :], d["b1e"]), (b.b3e[:, :], d["b3e"]), (b.b2e[:, :], d["b2e"]),
                      (b.gate_w[:, :, :], chunked(d["gate_w"])),
                      (b.expert_bias[:, :], d["expert_bias"].partition_broadcast(P)),
                      (b.pick[:, :, :], d["pick"]), (b.iota[:, :], d["iota"].partition_broadcast(P)),
                      (b.sb2_twice[:, :], d["sb2"])]
            rest, total = load(block, g, pairs)

            @block.scalar
            def _(act):
                for dst, src in rest:
                    act.dma_start(dst, src).then_inc(g("loaded"), 16)

            @block.gpsimd
            def _(pool):
                clear_spares(pool, b)

            @block.vector
            def _(dve):
                dve.wait_ge(g("loaded"), total)
                dve.tensor_scalar(b.b1e_half[:, :], b.b1e_half[:, :], 0.5, None, ALU.mult)

        region(nc, begin)

        def turn(i):
            def body(g, block):
                @block.sync
                def _(sp):
                    for s in range(SB):
                        load_context(sp, g, b, i, s)
                    for s in range(SB):
                        sp.wait_ge(g("L3f_x", s), TILES)
                        sp.dma_start(out.rearrange("(i s) (t p) n -> i s p t n", s=SB, p=P)[i, s],
                                     b.x[s][:, :, :]).then_inc(g("stored", s), 16)
                    for s in range(SB):
                        sp.wait_ge(g("stored", s), 16)

                @block.gpsimd
                def _(pool):
                    for L in ("L3a", "L3x", "L3f"):
                        for s in range(SB):
                            norm_pool(pool, g, b, s, L)

                def pe_program(pe, s):
                    norm_pe(pe, g, b, s, "in", 3)
                    yield
                    yield from rotary_pe(pe, g, b, s, "in")
                    norm_pe(pe, g, b, s, "L3a", 3)
                    yield
                    yield from wide_pe(pe, g, b, s, "L3a")
                    norm_pe(pe, g, b, s, "L3x", 3)
                    yield
                    yield from experts_pe(pe, g, b, s, "L3x")

                @block.tensor
                def _(pe):
                    pe.wait_ge(g("ctx", 0), 32)
                    pe.wait_ge(g("ctx", 1), 32)
                    side_by_side([pe_program(pe, s) for s in range(SB)])

                def act_program(act, s):
                    norm_act(act, g, b, s, "in", 3)
                    yield
                    for _ in range(6):
                        yield
                    yield from heads_act(act, g, b, s, b.heads["L3a"])
                    norm_act(act, g, b, s, "L3a", 3)
                    yield
                    yield from wide_act(act, g, b, s)
                    norm_act(act, g, b, s, "L3x", 3)
                    yield
                    yield from experts_act(act, g, b, s)

                @block.scalar
                def _(act):
                    side_by_side([act_program(act, s) for s in range(SB)])

                def dve_program(dve, link, s):
                    take_in(dve, g, b, s, i)
                    yield
                    yield from rotary_dve(dve, link, g, b, s)
                    norm_dve(dve, link, g, b, s, "L3a", 1, row_o[:, :])
                    yield
                    yield from wide_dve(dve, link, g, b, s)
                    norm_dve(dve, link, g, b, s, "L3x", 1)
                    yield
                    yield from experts_dve(dve, link, g, b, s)
                    norm_dve(dve, link, g, b, s, "L3f", 0)
                    yield

                @block.vector
                def _(dve):
                    link = Chain(dve, g("dve_chain"))
                    side_by_side([dve_program(dve, link, s) for s in range(SB)])

            return body

        with nc.Fori(0, NB // SB) as i:
            region(nc, turn(i))


def program(nc, dram, out, phases=5):
    with ExitStack() as ctx:
        b = Buffers()
        b.dram = dram
        sb = lambda n, shape, dt=F32: ctx.enter_context(nc.sbuf_tensor(n, shape, dt))
        b.x_all = sb("x_all", [P, NB * TILES, D])
        b.ident, b.identb, b.ones = sb("ident", [P, P]), sb("identb", [P, P], BF16), sb("ones", [P, P])
        b.minus_half = sb("minus_half", [P, TILES])
        b.pst = ctx.enter_context(nc.psum_tensor("banks", [P, 8, 512], F32))
        b.ps = [b.pst[:, 4 * s:4 * s + 4, :] for s in range(SB)]
        phase_state(nc, b)
        if phases > 1:
            phase_first(nc, b)
        if phases > 2:
            phase_quantised(nc, b)
        if phases > 3:
            phase_second(nc, b)
        if phases > 4:
            phase_third(nc, b, out)
        else:
            def show(g, block):
                @block.sync
                def _(sp):
                    sp.dma_start(out.rearrange("b (t p) n -> p (b t) n", p=P), b.x_all[:, :, :]).then_inc(g("shown"), 16)
                    sp.wait_ge(g("shown"), 16)
            region(nc, show)


def laid_out(a):
    f = np.float32
    rows = lambda v: v.reshape(1, -1)

    def slots(w):
        w = w.reshape(*w.shape[:-1], NH, DH)
        return np.concatenate([w, np.zeros_like(w)], -1).reshape(*w.shape[:-2], NH * SLOT)

    def columns(v):
        return v.reshape(-1, P).T

    one = np.zeros((NH, SLOT), f)
    one[:, ONE_ROW] = 1.0
    one = one.reshape(-1)

    def with_one(v):
        v = slots(v).reshape(NH, SLOT).copy()
        v[:, ONE_ROW] = 1.0
        return v.reshape(-1)

    def half_swapped(w):
        w = w.reshape(*w.shape[:-1], NH, 2, DH // 2)
        return w[..., ::-1, :].reshape(*w.shape[:-3], NH * DH)

    p = np.arange(P)
    same = (p[:, None] // BLK == p[None, :] // BLK)
    spread = np.stack([same & (p[:, None] % BLK == i) for i in range(BLK)], 1).astype(f)
    collect = np.stack([same & (p[None, :] % BLK == i) for i in range(BLK)], 1).astype(f)
    causal = np.where(p[None, :] <= p[:, None], 0.0, NEG).astype(f)
    inv_freq = (f(1.0) / f(10000.0) ** (np.arange(0, DH, 2, dtype=f) / f(DH))).astype(f)
    angle = np.arange(SEQ, dtype=f)[:, None] * inv_freq[None, :]
    cos, sin = np.zeros((SLOT, SEQ), f), np.zeros((SLOT, SEQ), f)
    cos[0:DH] = np.concatenate([np.cos(angle), np.cos(angle)], 1).T
    sin[0:DH] = np.concatenate([-np.sin(angle), np.sin(angle)], 1).T
    cos[ONE_ROW] = 1.0
    x, ctx = a["x"], a["ctx_1024"]
    mask = a["mask_Bx16xSxS2_bk1"]
    smask = a["mask_SxS2_bk0"]
    w3, b3 = a["L3_attn_W_qkv"].reshape(D, 3, D), a["L3_attn_b_qkv"].reshape(3, D)
    sw = lambda n: a[f"L3_ffn_s{n}"].reshape(2, FF3, D)
    return {
        "x": x.reshape(TOKENS, D), "xT": x.reshape(TOKENS, D).T, "ctx": ctx, "ctxT": ctx.transpose(0, 2, 1),
        "mask": mask.transpose(0, 2, 1, 3), "maskT": mask.transpose(0, 3, 1, 2), "smask": smask, "smaskT": smask.T,
        "w0k": a["L0_attn_W_k"].T, "w0v": a["L0_attn_W_v"].T, "w0q": a["L0_attn_W_q"].T,
        "same_block": same.astype(f), "spread": spread, "collect": collect, "ident": np.eye(P, dtype=f),
        "causal": causal, "causalT": causal.T,
        "wsim": columns(a["L0_xattn_w_sim"]), "b_sim": rows(a["L0_xattn_b_sim"]), "wqv": a["L0_xattn_W_qv"],
        "row_qv": rows(a["L0_xattn_b_qv"]), "w0f": a["L0_ffn_W"].T, "row_f0": rows(a["L0_ffn_b"]),
        "ld": a["L0_ffn_lora_down"].T, "da": a["L0_ffn_down_aux"], "lu": a["L0_ffn_lora_up"].T,
        "ua": a["L0_ffn_up_aux"].T,
        "w1a": a["L1_attn_W_qkv"], "w1o": a["L1_attn_W_out"].T, "row_o1": rows(a["L1_attn_b_out"]),
        "w1xq": slots(a["L1_xattn_Wq"]), "w1xk": slots(a["L1_xattn_Wk"]), "w1xv": a["L1_xattn_Wv"],
        "w1xo": a["L1_xattn_Wo"], "b1xq": columns(slots(a["L1_xattn_bq"])),
        "b1xk": columns(with_one(a["L1_xattn_bk"])), "row_v1": rows(a["L1_xattn_bv"]),
        "row_x1": rows(a["L1_xattn_bo"]),
        "w_up": a["L1_ffn_w_up"], "w_gate": a["L1_ffn_w_gate"], "w_down": a["L1_ffn_w_down"],
        "w2aq": slots(a["L2_attn_Wq"]), "w2ak": slots(a["L2_attn_Wk"]), "w2av": a["L2_attn_Wv"],
        "w2ao": a["L2_attn_Wo"], "w2xq": slots(a["L2_xattn_Wq"].T), "w2xk": slots(a["L2_xattn_Wk"].T),
        "w2xv": a["L2_xattn_Wv"].T, "w2xo": a["L2_xattn_Wo"].T, "w2f1": a["L2_ffn_W1"].T,
        "w2f2": a["L2_ffn_W2"].T, "b2f1": columns(a["L2_ffn_b1"]), "row_b2": rows(a["L2_ffn_b2"]),
        "k_one": columns(one),
        "w3q": slots(w3[:, 0]), "w3k": slots(w3[:, 1]), "w3v": w3[:, 2], "w3q_rot": slots(half_swapped(w3[:, 0])),
        "w3k_rot": slots(half_swapped(w3[:, 1])), "rb_q": columns(slots(b3[0])), "rb_k": columns(with_one(b3[1])),
        "rb_q_rot": columns(slots(half_swapped(b3[0]))), "rb_k_rot": columns(slots(half_swapped(b3[1]))),
        "row_v3": rows(b3[2]), "w3o": a["L3_attn_W_out"], "row_o3": rows(a["L3_attn_b_out"]),
        "cos": np.tile(cos, (4, 1)), "sin": np.tile(sin, (4, 1)),
        "gate_w": a["L3_ffn_gate_w"].T, "expert_bias": rows(a["L3_ffn_expert_bias"]),
        "w1e": np.concatenate([a["L3_ffn_w1"], sw("w1")]).transpose(0, 2, 1),
        "w3e": np.concatenate([a["L3_ffn_w3"], sw("w3")]).transpose(0, 2, 1),
        "w2e": np.concatenate([a["L3_ffn_w2"], a["L3_ffn_sw2"].reshape(D, 2, FF3).transpose(1, 0, 2)])
                 .transpose(0, 2, 1),
        "b1e": np.concatenate([a["L3_ffn_b1"], a["L3_ffn_sb1"].reshape(2, FF3)]).T,
        "b3e": np.concatenate([a["L3_ffn_b3"], a["L3_ffn_sb3"].reshape(2, FF3)]).T,
        "b2e": a["L3_ffn_b2"], "sb2": rows(np.tile(a["L3_ffn_sb2"], 2)),
        "pick": np.repeat(np.eye(NE, dtype=f)[:, :, None], P, 2), "iota": rows(np.arange(NE, dtype=f)),
    }


def kernel(**inputs):
    import concourse.bacc as bacc
    from concourse.bass_utils import run_bass_kernel_spmd

    nc = bacc.Bacc("TRN2", target_bir_lowering=False, num_devices=1)
    arrays, dram = {}, {}
    for name, a in laid_out({k: np.asarray(v) for k, v in inputs.items()}).items():
        a = np.ascontiguousarray(a)
        arrays["in_" + name] = a
        dram[name] = nc.dram_tensor("in_" + name, a.shape, mybir.dt.from_np(a.dtype), kind="ExternalInput").ap()
    out = nc.dram_tensor("out_x", (NB, SEQ, D), F32, kind="ExternalOutput").ap()
    program(nc, dram, out)
    r = run_bass_kernel_spmd(nc, [arrays], core_ids=[0])
    return r.results[0]["out_x"]
```

```python
from contextlib import ExitStack

import numpy as np

import concourse.bass as bass
from concourse import mybir

ALU = mybir.AluOpType
ACT = mybir.ActivationFunctionType
F32 = mybir.dt.float32
BF16 = mybir.dt.bfloat16
U8 = mybir.dt.uint8
U32 = mybir.dt.uint32
X = mybir.AxisListType.X
XY = mybir.AxisListType.XY

P = 128
NB, SEQ, D = 8, 256, 256
SK = 120
TILES = SEQ // P
DC = D // P
NH, DH = 16, 16
HC = 4
SLOT = 32
PARTS = 3
PRODUCTS = P // DH
EPS = 1e-5
NEG = -1.0e30
BLK = 8
TOKENS = NB * SEQ
FF1, FF2, FF3, NE = 768, 1024, 128, 16
ROUND = 12582912.0
QMAX = 32767.0
SB = 2
DV2 = 64


class Signals:

    def __init__(self, nc, ctx):
        self.nc, self.ctx, self.by_name = nc, ctx, {}

    def __call__(self, name, s=""):
        key = f"{name}_{s}" if s != "" else name
        if key not in self.by_name:
            self.by_name[key] = self.ctx.enter_context(self.nc.semaphore(key))
        return self.by_name[key]

    def runs(self):
        nums, found = sorted(h.num for h in self.by_name.values()), []
        for n in nums:
            if found and found[-1].stop == n:
                found[-1] = range(found[-1].start, n + 1)
            else:
                found.append(range(n, n + 1))
        return found


class Chain:

    def __init__(self, eng, sem):
        self.eng, self.sem, self.n = eng, sem, 0

    def __call__(self, *instructions):
        for ins in instructions:
            self.n += 1
            ins.then_inc(self.sem, 1)
        self.eng.wait_ge(self.sem, self.n)


def side_by_side(programs):
    live = list(programs)
    while live:
        for p in list(live):
            if next(p, "end") == "end":
                live.remove(p)


def norm_pe(pe, g, b, s, L, bank):
    pe.wait_ge(g(L + "_x", s), TILES)
    for t in range(TILES):
        for c in range(DC):
            last = pe.transpose(b.ps[s][:, bank, c * SEQ + t * P:c * SEQ + (t + 1) * P],
                                b.x[s][:, t, c * P:(c + 1) * P], b.ident[:, :])
    last.then_inc(g(L + "_xt", s), 1)


def norm_act(act, g, b, s, L, bank):
    act.wait_ge(g(L + "_xt", s), 1)
    act.activation(b.xT[s][:, :, :].rearrange("p c n -> p (c n)"), b.ps[s][:, bank, :], ACT.Copy)\
       .then_inc(g(L + "_xT", s), 1)


def norm_dve(dve, link, g, b, s, L, bank, bias=None, half=False, valid=None):
    r, x, st, mv, rstd = b.r[s], b.x[s], b.st[s], b.mv[s], b.rstd[s]
    out = b.ps[s][:, bank, :].rearrange("p (t n) -> p t n", t=TILES)
    dve.wait_ge(g(L + "_out", s), 1)
    if valid is not None:
        link(*[dve.scalar_tensor_tensor(r[:, t, :], out[:, t, :], valid[:, t:t + 1], x[:, t, :], ALU.mult, ALU.add)
               for t in range(TILES)])
    elif half:
        link(dve.scalar_tensor_tensor(r[:, :, :], out, 0.5, x[:, :, :], ALU.mult, ALU.add))
    else:
        link(dve.tensor_tensor(r[:, :, :], out, x[:, :, :], ALU.add))
    if bias is not None:
        link(dve.tensor_tensor(r[:, :, :], r[:, :, :], bias.unsqueeze(1).to_broadcast([P, TILES, D]), ALU.add))
    link(*[dve.bn_stats(st[:, t, :], r[:, t, :]) for t in range(TILES)])
    link(*[dve.bn_aggr(mv[:, t, :], st[:, t, :]) for t in range(TILES)])
    dve.tensor_scalar(mv[:, :, 1], mv[:, :, 1], EPS, None, ALU.add).then_inc(g(L + "_var", s), 1)
    dve.wait_ge(g(L + "_rstd", s), 1)
    for t in range(TILES):
        dve.tensor_scalar(x[:, t, :], r[:, t, :], mv[:, t, 0:1], rstd[:, t:t + 1],
                          ALU.subtract, ALU.mult).then_inc(g(L + "_x", s), 1)


def norm_pool(pool, g, b, s, L):
    pool.wait_ge(g(L + "_var", s), 1)
    pool.tensor_tensor(b.rstd[s][:, :], b.mv[s][:, :, 1], b.minus_half[:, :], ALU.pow)\
        .then_inc(g(L + "_rstd", s), 1)


class Heads:

    def __init__(self, L, keys, dv, parts, mask=None, ob=1):
        self.L, self.keys, self.dv, self.mask, self.ob = L, keys, dv, mask, ob
        self.parts = parts
        self.scale = DH ** -0.5
        self.per = 2 if len(keys) == 1 else 1
        self.units = HC // self.per
        self.chunks = [range(u * self.per, (u + 1) * self.per) for u in range(self.units)]
        self.slot = max(32, dv)
        self.fit = P // self.slot
        self.outs = 4 * self.per // self.fit
        self.nk = sum(ks for _, ks in keys)
        self.maxes = 1 if len(keys) == 2 and mask is None else TILES

    def sees(self, t, k):
        return self.mask != "causal" or k <= t


def split(eng, link, src, parts, rest, done):
    link(eng.tensor_copy(parts[0], src))
    link(eng.tensor_tensor(rest, src, parts[0], ALU.subtract))
    link(eng.tensor_copy(parts[1], rest))
    eng.tensor_tensor(parts[2], rest, parts[1], ALU.subtract).then_inc(done, 1)


def split_q(dve, link, g, b, s, h):
    dve.wait_ge(g(h.L + "_q", s), h.parts[0])
    split(dve, link, b.qT[s][:, :, :], [b.qp[s][:, p, :, :] for p in range(PARTS)], b.r[s][:, :, :],
          g(h.L + "_qp", s))


def split_k(pool, link, g, b, s, h):
    pool.wait_ge(g(h.L + "_k", s), h.parts[1])
    split(pool, link, b.kT[s][:, :, 0:h.nk], [b.kp[s][:, p, :, 0:h.nk] for p in range(PARTS)],
          b.kr[s][:, :, 0:h.nk], g(h.L + "_kp", s))


def stack_round(b, s, h, r):
    n = SEQ if r < 4 else h.nk
    dst = (b.qs if r < 4 else b.ks)[s][:, :, 2 * (r % 4):2 * (r % 4) + 2, 0:n].rearrange("p c h n -> p h c n")
    bank = 2 * (r % 2)
    return dst, b.ps[s][:, bank:bank + 2, 0:DC * n].rearrange("p h (c n) -> p h c n", c=DC)


def stack_pe(pe, g, b, s, h):
    L, ps = h.L, b.ps[s]
    pe.wait_ge(g(L + "_qp", s), 1)
    pe.wait_ge(g(L + "_v", s), h.parts[2])
    for r in range(8):
        sel, parts, n = (b.sel_q, b.qp[s], SEQ) if r < 4 else (b.sel_k, b.kp[s], h.nk)
        if r == 4:
            pe.wait_ge(g(L + "_kp", s), 1)
        if r >= 2:
            if r % 2 == 0:
                pe.wait_ge(g(L + "_placed_even", s), r // 2)
            else:
                pe.wait_ge(g(L + "_placed_odd", s), r // 2)
        for i in range(2):
            for p in range(PARTS):
                last = pe.matmul(ps[:, 2 * (r % 2) + i, 0:DC * n], lhsT=sel[:, p, 2 * (r % 4) + i, :],
                                 rhs=parts[:, p, :, 0:n], start=(p == 0), stop=(p == PARTS - 1),
                                 skip_group_check=True)
        last.then_inc(g(L + "_place", s), 1)
        if r % 2 == 1:
            yield


def stack_act(act, g, b, s, h):
    for r in range(0, 8, 2):
        act.wait_ge(g(h.L + "_place", s), r + 1)
        dst, src = stack_round(b, s, h, r)
        act.activation(dst, src, ACT.Copy).then_inc(g(h.L + "_placed_even", s), 1)
        yield


def stack_dve(dve, g, b, s, h):
    for r in range(1, 8, 2):
        dve.wait_ge(g(h.L + "_place", s), r + 1)
        dst, src = stack_round(b, s, h, r)
        dve.tensor_copy(dst, src).then_inc(g(h.L + "_placed_odd", s), 1)
        yield


def masked(h, b, s, pe, out, t, c, j, flipped):
    if h.mask == "causal":
        add = b.causalT[:, :] if flipped else b.causal[:, :]
    elif h.mask == "per_head":
        add = b.maskT[s][:, c * 4 + j, t * P:(t + 1) * P] if flipped else b.mask[s][:, t, c * 4 + j, :]
    else:
        add = b.smaskT[:, t * P:(t + 1) * P] if flipped else b.smask[:, t, :]
    n = add.shape[0]
    return pe.matmul(out, lhsT=b.identb[0:n, 0:n], rhs=add, start=False, stop=True, skip_group_check=True)


def heads_pe(pe, g, b, s, h):
    L, ps, v = h.L, b.ps[s], (b.vn if h.dv == DH else b.vw)[s]
    qs = b.qs[s][:, :, :, :].rearrange("p c h n -> p (c h) n")
    kst = b.ks[s][:, :, :, :].rearrange("p c h n -> p (c h) n")
    yield from stack_pe(pe, g, b, s, h)
    pe.wait_ge(g(L + "_placed_even", s), 4)
    pe.wait_ge(g(L + "_placed_odd", s), 4)
    if h.mask == "per_head":
        pe.wait_ge(g(L + "_mask", s), 2)
    for u, chunks in enumerate(h.chunks):
        if u >= 1:
            pe.wait_ge(g(L + "_mx", s), h.maxes * u)
        for n, c in enumerate(chunks):
            for t in range(TILES):
                col = (n * TILES + t) * P * len(h.keys)
                width = sum(ks for k, (o, ks) in enumerate(h.keys) if h.sees(t, k))
                for j in range(4):
                    last = pe.matmul(ps[:, j, col:col + width], lhsT=qs[:, 4 * c + j, t * P:(t + 1) * P],
                                     rhs=kst[:, 4 * c + j, 0:width], start=True, stop=True, skip_group_check=True)
                    if h.mask:
                        o = t * P if h.mask == "causal" else 0
                        ks = h.keys[0][1]
                        last = masked(h, b, s, pe, ps[:, j, col + o:col + o + ks], t, c, j, False)
        last.then_inc(g(L + "_s", s), 1)
        yield
    pe.wait_ge(g(L + "_mp", s), 1)
    for t in range(TILES):
        last = pe.matmul(ps[0:PARTS * NH, 0, t * P:(t + 1) * P], lhsT=b.mxp[s][:, t, :, :].rearrange("p a h -> p (a h)"),
                         rhs=b.identb[:, :], start=True, stop=True, skip_group_check=True)
    last.then_inc(g(L + "_mT", s), 1)
    yield
    pe.wait_ge(g(L + "_mxT", s), 1)
    for u, chunks in enumerate(h.chunks):
        for j in range(4):
            if u >= 1 and j == 4 - h.outs:
                pe.wait_ge(g(L + "_o", s), u)
            for n, c in enumerate(chunks):
                for k, (o, ks) in enumerate(h.keys):
                    col = (n + k) * SEQ
                    first = min(t for t in range(TILES) if h.sees(t, k)) * P
                    out = ps[0:ks, j, col + first:col + SEQ]
                    pe.matmul(out, lhsT=kst[:, 4 * c + j, o:o + ks], rhs=qs[:, 4 * c + j, first:SEQ],
                              start=True, stop=False, skip_group_check=True)
                    last = pe.matmul(out, lhsT=b.onehot[:, 4 * c + j, 0:ks], rhs=b.mxT[s][:, first:SEQ],
                                     start=False, stop=True, skip_group_check=True)
                    for t in range(TILES):
                        if h.mask and (h.mask != "causal" or t == k):
                            last = masked(h, b, s, pe, ps[0:ks, j, col + t * P:col + (t + 1) * P], t, c, j, True)
        last.then_inc(g(L + "_st", s), 1)
        yield
        pe.wait_ge(g(L + "_e", s), len(h.keys) * (u + 1))
        for m in range(h.outs):
            bank = 4 - h.outs + m
            heads = range((u * h.outs + m) * h.fit, (u * h.outs + m + 1) * h.fit)
            for sums in range(2):
                for k, (o, ks) in enumerate(h.keys):
                    first = min(t for t in range(TILES) if h.sees(t, k)) * P
                    for i, head in enumerate(heads):
                        n, j = (head // 4) % h.per, head % 4
                        weights = b.ones[0:ks, 0:h.slot] if sums else v[0:ks, k, head * h.slot:(head + 1) * h.slot]
                        last = pe.matmul(ps[i * h.slot:(i + 1) * h.slot, bank, sums * SEQ + first:(sums + 1) * SEQ],
                                         lhsT=weights, rhs=b.PT[s][0:ks, j, (n + k) * SEQ + first:(n + k + 1) * SEQ],
                                         start=(k == 0), stop=(k == len(h.keys) - 1), skip_group_check=True)
        last.then_inc(g(L + "_pv", s), 1)
        yield
    pe.wait_ge(g(L + "_o", s), h.units)
    nC = NH // h.fit
    for t in range(TILES):
        for c in range(nC):
            last = pe.matmul(ps[:, h.ob, t * D:(t + 1) * D], lhsT=b.oT[s][:, c, t * P:(t + 1) * P],
                             rhs=b.wo[L][:, c, :], start=(c == 0), stop=(c == nC - 1), skip_group_check=True)
    last.then_inc(g(L + "_out", s), 1)
    yield


def heads_act(act, g, b, s, h):
    L, ps = h.L, b.ps[s]
    yield from stack_act(act, g, b, s, h)
    for u in range(h.units):
        act.wait_ge(g(L + "_st", s), u + 1)
        if u >= 1:
            act.wait_ge(g(L + "_pv", s), u)
        if len(h.keys) == 1:
            ks = h.keys[0][1]
            act.activation(b.PT[s][0:ks, :, :], ps[0:ks, :, :], ACT.Exp, scale=h.scale).then_inc(g(L + "_e", s), 1)
        else:
            for k in range(2):
                lo = k * SEQ + min(t for t in range(TILES) if h.sees(t, k)) * P
                act.activation(b.PT[s][:, :, lo:(k + 1) * SEQ], ps[:, :, lo:(k + 1) * SEQ], ACT.Exp,
                               scale=h.scale).then_inc(g(L + "_e", s), 1)
        yield


def heads_dve(dve, link, g, b, s, h, floor=None):
    L, ps, w = h.L, b.ps[s], h.dv + 1
    mx = b.mx[s]
    yield from stack_dve(dve, g, b, s, h)
    for u, chunks in enumerate(h.chunks):
        dve.wait_ge(g(L + "_s", s), u + 1)
        heads = slice(4 * chunks.start, 4 * chunks.stop)
        for t in range(h.maxes):
            width = sum(ks for k, (o, ks) in enumerate(h.keys) if h.sees(t, k))
            if h.maxes == 1:
                src = ps[:, :, :].rearrange("p j (t k) -> p j t k", t=TILES)
                dst = mx[:, :, heads].rearrange("p t j -> p j t")
            elif h.per == 2:
                src = ps[:, :, :].rearrange("p j (c t k) -> p t c j k", c=2, t=TILES)[:, t, :, :, 0:width]
                dst = mx[:, t, heads].rearrange("p (c j) -> p c j", c=2)
            else:
                src = ps[:, :, t * SEQ:t * SEQ + width]
                dst = mx[:, t, heads]
            dve.tensor_reduce(dst, src, X, ALU.max, negate=True).then_inc(g(L + "_mx", s), 1)
        yield
    dve.wait_ge(g(L + "_mx", s), h.maxes * h.units)
    split(dve, link, mx[:, :, :], [b.mxp[s][:, :, p, :] for p in range(PARTS)], b.mxr[s][:, :, :], g(L + "_mp", s))
    yield
    dve.wait_ge(g(L + "_mT", s), 1)
    dve.tensor_copy(b.mxT[s][:, :], ps[0:PARTS * NH, 0, 0:SEQ]).then_inc(g(L + "_mxT", s), 1)
    yield
    for u in range(h.units):
        dve.wait_ge(g(L + "_pv", s), u + 1)
        banks = ps[:, 4 - h.outs:4, :]
        values, sums, ri = banks[:, :, 0:SEQ], banks[:, :, SEQ:2 * SEQ], b.r[s][:, 0:h.outs, :]
        if floor:
            link(dve.tensor_scalar(ri, sums, floor, None, ALU.max))
            sums = ri
        link(dve.reciprocal(ri, sums))
        dve.tensor_tensor(b.oT[s][:, u * h.outs:(u + 1) * h.outs, :], values, ri, ALU.mult)\
           .then_inc(g(L + "_o", s), 1)
        dve.wait_ge(g(L + "_o", s), u + 1)
        yield


def cross_pe(pe, g, b, s, L, prev):
    ps, w = b.ps[s], b.w[L]
    pe.wait_ge(g("ctx", s), 32)
    pe.wait_ge(g(prev + "_xT", s), 1)
    for c in range(DC):
        for i in range(DC):
            last = pe.matmul(ps[:, 2, c * P:c * P + SK], lhsT=w["k"][:, i, c * P:(c + 1) * P],
                             rhs=b.ctxT[s][:, i, :], start=(i == 0), stop=(i == DC - 1), skip_group_check=True)
    last.then_inc(g(L + "_pk", s), 1)
    for i in range(DC):
        last = pe.matmul(ps[0:SK, 0, 0:D], lhsT=b.ctxT[s][:, i, :], rhs=w["v"][:, i, :],
                         start=(i == 0), stop=(i == DC - 1), skip_group_check=True)
    last.then_inc(g(L + "_pvv", s), 1)
    yield
    for c in range(DC):
        last = project_T(pe, ps[:, 1, c * SEQ:(c + 1) * SEQ], w["q"], c, b.xT[s])
    last.then_inc(g(L + "_pq", s), 1)
    yield


def with_bias(act, dst, src, bias, n, done):
    for c in range(DC):
        kw = {"bias": bias[:, c:c + 1]} if bias is not None else {}
        act.activation(dst[:, c, 0:n], src(c), ACT.Identity, **kw).then_inc(done, 1)


def cross_act(act, g, b, s, L, q_bias=None, k_bias=None):
    act.wait_ge(g(L + "_pk", s), 1)
    with_bias(act, b.kT[s], lambda c: b.ps[s][:, 2, c * P:c * P + SK], k_bias, SK, g(L + "_k", s))
    yield
    act.wait_ge(g(L + "_pq", s), 1)
    with_bias(act, b.qT[s], lambda c: b.ps[s][:, 1, c * SEQ:(c + 1) * SEQ], q_bias, SEQ, g(L + "_q", s))
    yield


def cross_dve(dve, link, g, b, s, L, v_bias=None):
    dve.wait_ge(g(L + "_pvv", s), 1)
    dst = b.vn[s][0:SK, 0, :].rearrange("p (h w) -> p h w", w=SLOT)[:, :, 0:DH]
    src = b.ps[s][0:SK, 0, 0:D].rearrange("p (h w) -> p h w", w=DH)
    if v_bias is not None:
        ins = dve.tensor_tensor(dst, src, v_bias[0:SK, :].rearrange("p (h w) -> p h w", w=DH), ALU.add)
    else:
        ins = dve.tensor_copy(dst, src)
    ins.then_inc(g(L + "_v", s), 1)
    yield
    split_q(dve, link, g, b, s, b.heads[L])
    yield


def project_T(pe, out, w, c, xT):
    for i in range(DC):
        last = pe.matmul(out, lhsT=w[:, i, c * P:(c + 1) * P], rhs=xT[:, i, :],
                         start=(i == 0), stop=(i == DC - 1), skip_group_check=True)
    return last


def project(pe, ps, bank, xT, w, n=D):
    for t in range(TILES):
        for i in range(DC):
            last = pe.matmul(ps[:, bank, t * n:(t + 1) * n], lhsT=xT[:, i, t * P:(t + 1) * P],
                             rhs=w[:, i, :], start=(i == 0), stop=(i == DC - 1), skip_group_check=True)
    return last


def causal_pe(pe, g, b, s, prev):
    ps, w, xT = b.ps[s], b.w["L2a"], b.xT[s]
    pe.wait_ge(g(prev + "_xT", s), 1)
    for n, name in enumerate("qk"):
        for c in range(DC):
            last = project_T(pe, ps[:, n, c * SEQ:(c + 1) * SEQ], w[name], c, xT)
        last.then_inc(g("L2a_p" + name, s), 1)
    for t in range(TILES):
        if t == 1:
            pe.wait_ge(g("L2a_q", s), 1)
            pe.wait_ge(g("L2a_k", s), 1)
        for half in range(2):
            for i in range(DC):
                last = pe.matmul(ps[:, 2 - 2 * t + half, :], lhsT=xT[:, i, t * P:(t + 1) * P],
                                 rhs=w["v"][:, i, half * 512:(half + 1) * 512],
                                 start=(i == 0), stop=(i == DC - 1), skip_group_check=True)
        last.then_inc(g("L2a_pvv", s), 1)
        yield
    yield from heads_pe(pe, g, b, s, b.heads["L2a"])


def causal_act(act, g, b, s):
    for n, (name, dst) in enumerate((("q", b.qT[s]), ("k", b.kT[s]))):
        act.wait_ge(g("L2a_p" + name, s), 1)
        act.activation(dst[:, :, :].rearrange("p c n -> p (c n)"), b.ps[s][:, n, :], ACT.Copy)\
           .then_inc(g("L2a_" + name, s), 1)
    yield
    yield from heads_act(act, g, b, s, b.heads["L2a"])


def causal_dve(dve, link, g, b, s):
    for t in range(TILES):
        dve.wait_ge(g("L2a_pvv", s), t + 1)
        dve.tensor_copy(b.vw[s][:, t, :].rearrange("p (h w) -> p h w", w=DV2)[:, :, 0:DV2],
                        b.ps[s][:, 2 - 2 * t:4 - 2 * t, :].rearrange("p a (h w) -> p (a h) w", w=DV2))\
           .then_inc(g("L2a_v", s), 1)
        if t == 0:
            split_q(dve, link, g, b, s, b.heads["L2a"])
    yield
    yield from heads_dve(dve, link, g, b, s, b.heads["L2a"])


ROPE_BANK = {"k": 0, "q": 2}


def rotary_pe(pe, g, b, s, prev):
    ps, w, xT = b.ps[s], b.w["L3a"], b.xT[s]
    pe.wait_ge(g(prev + "_xT", s), 1)
    for name in ("k", "q"):
        for rot in range(2):
            for c in range(DC):
                last = project_T(pe, ps[:, ROPE_BANK[name] + rot, c * SEQ:(c + 1) * SEQ],
                                 w[name + ("_rot" if rot else "")], c, xT)
        last.then_inc(g("L3a_p" + name, s), 1)
        yield
    pe.wait_ge(g("L3a_k", s), 1)
    project(pe, ps, 0, xT, w["v"]).then_inc(g("L3a_pvv", s), 1)
    yield
    yield from heads_pe(pe, g, b, s, b.heads["L3a"])


def rotary_dve(dve, link, g, b, s):
    ps = b.ps[s]
    for name, dst in (("k", b.kT[s]), ("q", b.qT[s])):
        dve.wait_ge(g("L3a_p" + name, s), 1)
        bank = ROPE_BANK[name]
        for c in range(DC):
            x_cos = dve.scalar_tensor_tensor(b.rc[s][:, c, :], ps[:, bank, c * SEQ:(c + 1) * SEQ],
                                             b.rope_bias[name][:, c:c + 1], b.cos[:, :], ALU.add, ALU.mult)
            rot_sin = dve.scalar_tensor_tensor(b.rs[s][:, c, :], ps[:, bank + 1, c * SEQ:(c + 1) * SEQ],
                                               b.rope_bias[name + "_rot"][:, c:c + 1], b.sin[:, :], ALU.add, ALU.mult)
            link(x_cos, rot_sin)
        dve.tensor_tensor(dst[:, :, :], b.rc[s][:, :, :], b.rs[s][:, :, :], ALU.add)\
           .then_inc(g("L3a_" + name, s), 1)
        yield
    split_q(dve, link, g, b, s, b.heads["L3a"])
    dve.wait_ge(g("L3a_pvv", s), 1)
    dve.tensor_tensor(b.vn[s][:, :, :].rearrange("p t (h w) -> p t h w", w=SLOT)[:, :, :, 0:DH],
                      ps[:, 0, :].rearrange("p (t h w) -> p t h w", t=TILES, w=DH),
                      b.v_bias["L3a"][:, :].rearrange("p (h w) -> p h w", w=DH).unsqueeze(1)
                       .to_broadcast([P, TILES, NH, DH]), ALU.add).then_inc(g("L3a_v", s), 1)
    yield
    yield from heads_dve(dve, link, g, b, s, b.heads["L3a"])


def flow_pe(pe, g, b, s, prev):
    ps, xT, x = b.ps[s], b.xT[s], b.x[s]
    pe.wait_ge(g(prev + "_xT", s), 1)
    pe.wait_ge(g("ctx", s), 32)
    pe.wait_ge(g("L0x_m", s), DC)
    for t in range(TILES):
        out = ps[:, 2, t * P:t * P + SK]
        for i in range(DC):
            pe.matmul(out, lhsT=xT[:, i, t * P:(t + 1) * P], rhs=b.flow_m[s][:, i, :],
                      start=(i == 0), stop=False, skip_group_check=True)
        for i in range(DC):
            last = pe.matmul(out, lhsT=b.w2_wide[:, i, :], rhs=b.ctxT[s][:, i, :],
                             start=False, stop=(i == DC - 1), skip_group_check=True)
    last.then_inc(g("L0x_sim", s), 1)
    yield
    pe.wait_ge(g("L0x_A", s), 1)
    for t in range(TILES):
        pe.transpose(ps[0:SK, 3, t * P:(t + 1) * P], b.A[s][:, t, :], b.ident[:, :])
    for t in range(TILES):
        last = pe.transpose(ps[0:1, 1, t * P:(t + 1) * P], b.nm[s][:, t:t + 1], b.ident[:, :])
    last.then_inc(g("L0x_At", s), 1)
    yield
    pe.wait_ge(g("L0x_nM", s), 1)
    pe.matmul(ps[:, 2, 2 * P:2 * P + 1], lhsT=b.ones[0:1, :], rhs=b.nM[s][0:1, 0:1], start=True, stop=True,
              skip_group_check=True).then_inc(g("L0x_nMb", s), 1)
    pe.wait_ge(g("L0x_AT", s), 1)
    for i in range(DC):
        pe.matmul(ps[:, 1, i * SEQ:(i + 1) * SEQ], lhsT=b.ctx[s][:, i * P:(i + 1) * P], rhs=b.AT[s][:, :],
                  start=True, stop=True, skip_group_check=True)
    pe.wait_ge(g("L0x_e", s), 1)
    for t in range(TILES):
        pe.matmul(ps[:, 2, 2 * P + 8:2 * P + 9], lhsT=b.ones[:, :], rhs=b.ecol[s][:, t:t + 1],
                  start=(t == 0), stop=(t == TILES - 1), skip_group_check=True)
    for i in range(DC):
        for t in range(TILES):
            last = pe.matmul(ps[:, 2, 2 * P + 16 + i:2 * P + 17 + i], lhsT=x[:, t, i * P:(i + 1) * P],
                             rhs=b.ecol[s][:, t:t + 1], start=(t == 0), stop=(t == TILES - 1),
                             skip_group_check=True)
    last.then_inc(g("L0x_hq", s), 1)
    yield
    pe.wait_ge(g("L0x_f", s), 2)
    pe.wait_ge(g("L0x_hqT", s), 1)
    for t in range(TILES):
        for f, feat in enumerate((xT, b.hqT[s], b.xhq[s], b.xhc[s])):
            for i in range(DC):
                last = pe.matmul(ps[:, 0, t * D:(t + 1) * D], lhsT=feat[:, i, t * P:(t + 1) * P],
                                 rhs=b.w["L0x"][:, 2 * f + i, :], start=(f + i == 0), stop=(f == 3 and i == 1),
                                 skip_group_check=True)
    last.then_inc(g("L0x_out", s), 1)
    yield


def flow_act(act, g, b, s):
    ps = b.ps[s]
    act.wait_ge(g("L0x_nm", s), 1)
    for t in range(TILES):
        act.activation(b.A[s][:, t, :], b.sim[s][:, t, :], ACT.Exp, bias=b.nm[s][:, t:t + 1],
                       accum_out=b.ssum[s][:, t:t + 1]).then_inc(g("L0x_exp", s), 1)
    yield
    act.wait_ge(g("L0x_At", s), 1)
    act.activation(b.AT[s][:, :], ps[0:SK, 3, 0:SEQ], ACT.Copy).then_inc(g("L0x_AT", s), 1)
    yield
    act.wait_ge(g("L0x_nMs", s), 1)
    act.activation(b.ecol[s][:, :], b.nm[s][:, :], ACT.Exp, scale=-1.0, bias=b.nMb[s][:, 0:1])\
       .then_inc(g("L0x_e", s), 1)
    act.wait_ge(g("L0x_hq", s), 1)
    act.activation(b.hqT[s][:, :, :].rearrange("p c n -> p (c n)"), ps[:, 1, :], ACT.Copy)\
       .then_inc(g("L0x_hqT", s), 1)
    yield


def flow_dve(dve, link, g, b, s):
    ps = b.ps[s]
    dve.wait_ge(g("ctx", s), 32)
    for i in range(DC):
        dve.tensor_scalar(b.flow_m[s][:, i, :], b.ctxT[s][:, i, :], b.w3[:, i:i + 1], b.w1[:, i:i + 1],
                          ALU.mult, ALU.add).then_inc(g("L0x_m", s), 1)
    yield
    dve.wait_ge(g("L0x_sim", s), 1)
    sim = ps[:, 2, 0:2 * P].rearrange("p (t n) -> p t n", t=TILES)[:, :, 0:SK]
    link(dve.tensor_scalar(b.sim[s][:, :, :], sim, b.b_sim[:, 0:1], None, ALU.add))
    dve.tensor_reduce(b.nm[s][:, :], b.sim[s][:, :, :], X, ALU.max, negate=True).then_inc(g("L0x_nm", s), 1)
    yield
    dve.wait_ge(g("L0x_exp", s), TILES)
    link(dve.reciprocal(b.ssum[s][:, :], b.ssum[s][:, :]))
    dve.tensor_tensor(b.A[s][:, :, :], b.A[s][:, :, :],
                      b.ssum[s][:, :].unsqueeze(2).to_broadcast([P, TILES, SK]), ALU.mult)\
       .then_inc(g("L0x_A", s), 1)
    yield
    dve.wait_ge(g("L0x_At", s), 1)
    dve.tensor_reduce(b.nM[s][0:1, 0:1], ps[0:1, 1, 0:SEQ], X, ALU.min).then_inc(g("L0x_nM", s), 1)
    dve.wait_ge(g("L0x_nMb", s), 1)
    dve.tensor_copy(b.nMb[s][:, :], ps[:, 2, 2 * P:2 * P + 1]).then_inc(g("L0x_nMs", s), 1)
    yield
    dve.wait_ge(g("L0x_hq", s), 1)
    link(dve.reciprocal(b.nMb[s][:, :], ps[:, 2, 2 * P + 8:2 * P + 9]))
    link(dve.tensor_scalar(b.hc[s][:, :], ps[:, 2, 2 * P + 16:2 * P + 16 + DC], b.nMb[s][:, 0:1], None, ALU.mult))
    dve.wait_ge(g("L0x_hqT", s), 1)
    dve.tensor_tensor(b.xhq[s][:, :, :], b.xT[s][:, :, :], b.hqT[s][:, :, :], ALU.mult).then_inc(g("L0x_f", s), 1)
    dve.tensor_tensor(b.xhc[s][:, :, :], b.xT[s][:, :, :],
                      b.hc[s][:, :].unsqueeze(2).to_broadcast([P, DC, SEQ]), ALU.mult)\
       .then_inc(g("L0x_f", s), 1)
    yield


def block_pe(pe, g, b, s, prev):
    ps, xT, w = b.ps[s], b.xT[s], b.w["L1a"]
    pe.wait_ge(g(prev + "_xT", s), 1)
    for n, bank in enumerate((0, 2)):
        for c in range(DC):
            last = project_T(pe, ps[:, bank, c * SEQ:(c + 1) * SEQ], w[:, :, n * D:(n + 1) * D], c, xT)
        last.then_inc(g("L1a_pqk", s), 1)
    project(pe, ps, 3, xT, w[:, :, 2 * D:3 * D]).then_inc(g("L1a_pvv", s), 1)
    yield
    pe.wait_ge(g("L1a_qk", s), 2)
    for t in range(TILES):
        for c in range(DC):
            last = pe.matmul(ps[:, 1, t * P:(t + 1) * P], lhsT=b.bq[s][:, c, t * P:(t + 1) * P],
                             rhs=b.bk[s][:, c, t * P:(t + 1) * P], start=(c == 0), stop=(c == DC - 1),
                             skip_group_check=True)
    last.then_inc(g("L1a_s", s), 1)
    yield
    pe.wait_ge(g("L1a_p", s), 1)
    for t in range(TILES):
        last = pe.transpose(ps[:, 2, t * P:(t + 1) * P], b.pb[s][:, t, :], b.ident[:, :])
    last.then_inc(g("L1a_pt", s), 1)
    yield
    pe.wait_ge(g("L1a_pT", s), 1)
    pe.wait_ge(g("L1a_v", s), 1)
    for c in range(DC):
        for t in range(TILES):
            last = pe.matmul(ps[:, 3, c * SEQ + t * P:c * SEQ + (t + 1) * P], lhsT=b.bv[s][:, t, c * P:(c + 1) * P],
                             rhs=b.pbT[s][:, t * P:(t + 1) * P], start=True, stop=True, skip_group_check=True)
    last.then_inc(g("L1a_ot", s), 1)
    yield
    pe.wait_ge(g("L1a_oT", s), 1)
    project(pe, ps, 0, b.oT[s], b.wo["L1a"]).then_inc(g("L1a_out", s), 1)
    yield


def block_act(act, g, b, s):
    ps = b.ps[s]
    flat = lambda a: a[:, :, :].rearrange("p c n -> p (c n)")
    for n, (bank, dst) in enumerate(((0, b.bq[s]), (2, b.bk[s]))):
        act.wait_ge(g("L1a_pqk", s), n + 1)
        act.activation(flat(dst), ps[:, bank, :], ACT.Copy).then_inc(g("L1a_qk", s), 1)
    yield
    act.wait_ge(g("L1a_nm", s), 1)
    for t in range(TILES):
        act.activation(b.pb[s][:, t, :], b.sc[s][:, t, :], ACT.Exp, bias=b.nm[s][:, t:t + 1],
                       accum_out=b.ssum[s][:, t:t + 1]).then_inc(g("L1a_exp", s), 1)
    yield
    act.wait_ge(g("L1a_pt", s), 1)
    act.activation(b.pbT[s][:, :], ps[:, 2, 0:SEQ], ACT.Copy).then_inc(g("L1a_pT", s), 1)
    yield
    act.wait_ge(g("L1a_ot", s), 1)
    act.activation(flat(b.oT[s][:, 0:DC, :]), ps[:, 3, :], ACT.Copy).then_inc(g("L1a_oT", s), 1)
    yield


def block_dve(dve, link, g, b, s):
    ps = b.ps[s]
    dve.wait_ge(g("L1a_pvv", s), 1)
    dve.tensor_copy(b.bv[s][:, :, :].rearrange("p t n -> p (t n)"), ps[:, 3, :]).then_inc(g("L1a_v", s), 1)
    yield
    dve.wait_ge(g("L1a_s", s), 1)
    link(dve.scalar_tensor_tensor(b.sc[s][:, :, :], ps[:, 1, 0:SEQ].rearrange("p (t n) -> p t n", t=TILES),
                                  float(D) ** -0.5, b.causal32[:, :].unsqueeze(1).to_broadcast([P, TILES, P]),
                                  ALU.mult, ALU.add))
    dve.tensor_reduce(b.nm[s][:, :], b.sc[s][:, :, :], X, ALU.max, negate=True).then_inc(g("L1a_nm", s), 1)
    yield
    dve.wait_ge(g("L1a_exp", s), TILES)
    link(dve.tensor_scalar(b.ssum[s][:, :], b.ssum[s][:, :], 1e-6, None, ALU.add))
    link(dve.reciprocal(b.ssum[s][:, :], b.ssum[s][:, :]))
    dve.tensor_tensor(b.pb[s][:, :, :], b.pb[s][:, :, :],
                      b.ssum[s][:, :].unsqueeze(2).to_broadcast([P, TILES, P]), ALU.mult)\
       .then_inc(g("L1a_p", s), 1)
    yield


def ternary_pe(pe, g, b, s, prev):
    ps, xT = b.ps[s], b.xT[s]
    pe.wait_ge(g(prev + "_xT", s), 1)
    for f in range(FF2 // P):
        last = project_T(pe, ps[:, f // 2, (f % 2) * SEQ:(f % 2 + 1) * SEQ], b.w["L2f1"], f, xT)
        if f % 2 == 1:
            last.then_inc(g("L2f_h", s), 1)
    yield
    pe.wait_ge(g("L2f_r", s), FF2 // P)
    for t in range(TILES):
        for f in range(FF2 // P):
            last = pe.matmul(ps[:, 0, t * D:(t + 1) * D], lhsT=b.hT[s][:, f, t * P:(t + 1) * P],
                             rhs=b.w["L2f2"][:, f, :], start=(f == 0), stop=(f == FF2 // P - 1),
                             skip_group_check=True)
    last.then_inc(g("L2f_out", s), 1)
    yield


def ternary_act(act, g, b, s):
    for f in range(FF2 // P):
        if f % 2 == 0:
            act.wait_ge(g("L2f_h", s), f // 2 + 1)
        act.activation(b.hT[s][:, f, :], b.ps[s][:, f // 2, (f % 2) * SEQ:(f % 2 + 1) * SEQ], ACT.Relu,
                       bias=b.b1[:, f:f + 1]).then_inc(g("L2f_r", s), 1)
    yield


def wide_pe(pe, g, b, s, prev):
    ps, xT = b.ps[s], b.xT[s]
    pe.wait_ge(g(prev + "_xT", s), 1)
    for t in range(TILES):
        for i in range(DC):
            last = pe.matmul(ps[:, 0, t * P:t * P + SK], lhsT=xT[:, i, t * P:(t + 1) * P], rhs=b.ctxT[s][:, i, :],
                             start=(i == 0), stop=(i == DC - 1), skip_group_check=True)
    last.then_inc(g("L3x_s", s), 1)
    yield
    pe.wait_ge(g("L3x_A", s), 1)
    for t in range(TILES):
        last = pe.transpose(ps[0:SK, 2, t * P:(t + 1) * P], b.A[s][:, t, :], b.ident[:, :])
    last.then_inc(g("L3x_At", s), 1)
    yield
    pe.wait_ge(g("L3x_AT", s), 1)
    for t in range(TILES):
        last = pe.matmul(ps[:, 1, t * D:(t + 1) * D], lhsT=b.AT[s][:, t * P:(t + 1) * P], rhs=b.ctx[s][:, :],
                         start=True, stop=True, skip_group_check=True)
    last.then_inc(g("L3x_out", s), 1)
    yield


def wide_act(act, g, b, s):
    act.wait_ge(g("L3x_nm", s), 1)
    for t in range(TILES):
        act.activation(b.A[s][:, t, :], b.ps[s][:, 0, t * P:t * P + SK], ACT.Exp, bias=b.nm[s][:, t:t + 1],
                       scale=float(D) ** -0.5, accum_out=b.ssum[s][:, t:t + 1]).then_inc(g("L3x_exp", s), 1)
    yield
    act.wait_ge(g("L3x_At", s), 1)
    act.activation(b.AT[s][:, :], b.ps[s][0:SK, 2, 0:SEQ], ACT.Copy).then_inc(g("L3x_AT", s), 1)
    yield


def wide_dve(dve, link, g, b, s):
    dve.wait_ge(g("L3x_s", s), 1)
    view = b.ps[s][:, 0, 0:2 * P].rearrange("p (t n) -> p t n", t=TILES)[:, :, 0:SK]
    link(dve.tensor_reduce(b.nm[s][:, :], view, X, ALU.max, negate=True))
    dve.tensor_scalar(b.nm[s][:, :], b.nm[s][:, :], float(D) ** -0.5, None, ALU.mult).then_inc(g("L3x_nm", s), 1)
    yield
    dve.wait_ge(g("L3x_exp", s), TILES)
    link(dve.reciprocal(b.ssum[s][:, :], b.ssum[s][:, :]))
    dve.tensor_tensor(b.A[s][:, :, :], b.A[s][:, :, :],
                      b.ssum[s][:, :].unsqueeze(2).to_broadcast([P, TILES, SK]), ALU.mult)\
       .then_inc(g("L3x_A", s), 1)
    yield


UNITS3 = NE + 2


def experts_pe(pe, g, b, s, prev):
    ps, xT = b.ps[s], b.xT[s]
    pe.wait_ge(g(prev + "_xT", s), 1)
    for t in range(TILES):
        for i in range(DC):
            last = pe.matmul(ps[:, 3, t * NE:(t + 1) * NE], lhsT=xT[:, i, t * P:(t + 1) * P], rhs=b.gate_w[:, i, :],
                             start=(i == 0), stop=(i == DC - 1), skip_group_check=True)
    last.then_inc(g("L3f_lg", s), 1)
    pe.matmul(ps[:, 0, :], lhsT=b.ones[0:1, :], rhs=b.sb2_twice[0:1, :], start=True, stop=False,
              skip_group_check=True)
    pe.wait_ge(b.experts_in, 48)
    order = [NE, NE + 1] + list(range(NE))
    for n in range(UNITS3 + 1):
        if n < UNITS3:
            e = order[n]
            for k, w in enumerate((b.w1e, b.w3e)):
                if n >= 1 and k == 0:
                    pe.wait_ge(g("L3f_z", s), 2 * n)
                if n >= 1 and k == 1:
                    pe.wait_ge(g("L3f_b", s), n)
                for i in range(DC):
                    last = pe.matmul(ps[:, 1 + k, 0:SEQ], lhsT=w[:, e, i, :],
                                     rhs=xT[:, i, :], start=(i == 0), stop=(i == DC - 1), skip_group_check=True)
                last.then_inc(g("L3f_h", s), 1)
            if n == 2:
                pe.wait_ge(g("L3f_gw", s), 1)
                for t in range(TILES):
                    pe.transpose(ps[0:NE, 3, SEQ + t * P:SEQ + (t + 1) * P], b.gw[s][:, t, :], b.ident[:, :])
                for t in range(TILES):
                    last = pe.matmul(ps[0:PARTS * NE, 3, t * P:(t + 1) * P],
                                     lhsT=b.mxp[s][:, t, :, :].rearrange("p a h -> p (a h)"), rhs=b.identb[:, :],
                                     start=True, stop=True, skip_group_check=True)
                last.then_inc(g("L3f_gt", s), 1)
                pe.wait_ge(g("L3f_gT", s), 2)
                for t in range(TILES):
                    pe.matmul(ps[:, 0, t * D:(t + 1) * D], lhsT=b.gT[s][:, t * P:(t + 1) * P], rhs=b.b2e[:, :],
                              start=False, stop=False, skip_group_check=True)
            if e < NE:
                if n >= 3:
                    pe.wait_ge(g("L3f_c", s), n - 2)
                pe.matmul(ps[:, 3, 0:SEQ], lhsT=b.onehot[:, e, :], rhs=b.mxT[s][:, :],
                          start=True, stop=True, skip_group_check=True).then_inc(g("L3f_G", s), 1)
        if n >= 1:
            e = order[n - 1]
            if e < NE:
                pe.wait_ge(g("L3f_c", s), n - 2)
            else:
                pe.wait_ge(g("L3f_b", s), n)
            for t in range(TILES):
                last = pe.matmul(ps[:, 0, t * D:(t + 1) * D], lhsT=b.he[s][:, (n - 1) % 2, t * P:(t + 1) * P],
                                 rhs=b.w2e[:, e, :], start=False, stop=(n == UNITS3), skip_group_check=True)
            last.then_inc(g("L3f_out" if n == UNITS3 else "L3f_y", s), 1)
        yield


def experts_act(act, g, b, s):
    order = [NE, NE + 1] + list(range(NE))
    act.wait_ge(g("L3f_raw", s), 1)
    act.activation(b.th[s][:, :], b.raw[s][:, :], ACT.Tanh, scale=0.5).then_inc(g("L3f_th", s), 1)
    for n, e in enumerate(order):
        act.wait_ge(g("L3f_h", s), 2 * n + 1)
        if n >= 2:
            act.wait_ge(g("L3f_a", s), n - 1)
        h1 = b.ps[s][:, 1, 0:SEQ]
        act.activation(b.t3[s][:, n % 2, :], h1, ACT.Tanh, scale=0.5, bias=b.b1e_half[:, e:e + 1])\
           .then_inc(g("L3f_z", s), 1)
        act.activation(b.z3[s][:, n % 2, :], h1, ACT.Identity, scale=0.5, bias=b.b1e_half[:, e:e + 1])\
           .then_inc(g("L3f_z", s), 1)
        if n == 2:
            act.wait_ge(g("L3f_gt", s), 1)
            act.activation(b.gT[s][:, :], b.ps[s][0:NE, 3, SEQ:2 * SEQ], ACT.Copy).then_inc(g("L3f_gT", s), 1)
            act.activation(b.mxT[s][:, :], b.ps[s][0:PARTS * NE, 3, 0:SEQ], ACT.Copy).then_inc(g("L3f_gT", s), 1)
        yield


def experts_dve(dve, link, g, b, s):
    order = [NE, NE + 1] + list(range(NE))
    m8, i8, f8, sel, gw = b.m8[s], b.i8[s], b.f8[s], b.sel[s], b.gw[s]
    lg = b.lg[s]
    dve.wait_ge(g("L3f_lg", s), 1)
    dve.tensor_copy(b.raw[s][:, :], b.ps[s][:, 3, 0:TILES * NE]).then_inc(g("L3f_raw", s), 1)
    dve.wait_ge(g("L3f_raw", s), 1)
    link(dve.tensor_tensor(lg[:, :, :], b.raw[s][:, :].rearrange("p (t e) -> p t e", t=TILES),
                           b.expert_bias[:, :].unsqueeze(1).to_broadcast([P, TILES, NE]), ALU.add))
    link(*[dve.max(m8[:, t, :], lg[:, t, :]) for t in range(TILES)])
    link(*[dve.max_index(i8[:, t, :], m8[:, t, :], lg[:, t, :]) for t in range(TILES)])
    link(dve.tensor_copy(f8[:, :, :], i8[:, :, :]))
    for t in range(TILES):
        link(dve.tensor_scalar(sel[:, t, :], b.iota[:, :], f8[:, t, 0:1], None, ALU.is_equal))
        link(dve.scalar_tensor_tensor(sel[:, t, :], b.iota[:, :], f8[:, t, 1:2], sel[:, t, :],
                                      ALU.is_equal, ALU.add))
    dve.wait_ge(g("L3f_th", s), 1)
    link(dve.tensor_scalar(gw[:, :, :], b.th[s][:, :].rearrange("p (t e) -> p t e", t=TILES), 0.5, 0.5,
                           ALU.mult, ALU.add))
    link(dve.tensor_tensor(gw[:, :, :], gw[:, :, :], sel[:, :, :], ALU.mult))
    link(dve.tensor_reduce(b.nm[s][:, :], gw[:, :, :], X, ALU.add))
    link(dve.tensor_scalar(b.nm[s][:, :], b.nm[s][:, :], 1e-10, None, ALU.add))
    link(dve.reciprocal(b.nm[s][:, :], b.nm[s][:, :]))
    link(dve.tensor_tensor(gw[:, :, :], gw[:, :, :], b.nm[s][:, :].unsqueeze(2).to_broadcast([P, TILES, NE]),
                           ALU.mult))
    split(dve, link, gw[:, :, :], [b.mxp[s][:, :, p, :] for p in range(PARTS)], b.mxr[s][:, :, :], g("L3f_gw", s))
    for n, e in enumerate(order):
        dve.wait_ge(g("L3f_z", s), 2 * n + 2)
        dve.scalar_tensor_tensor(b.a3[s][:, n % 2, :], b.t3[s][:, n % 2, :], 1.0, b.z3[s][:, n % 2, :],
                                 ALU.add, ALU.mult).then_inc(g("L3f_a", s), 1)
        dve.wait_ge(g("L3f_a", s), n + 1)
        if n >= 2:
            dve.wait_ge(g("L3f_y", s), n - 1)
        dve.wait_ge(g("L3f_h", s), 2 * n + 2)
        dve.scalar_tensor_tensor(b.he[s][:, n % 2, :], b.ps[s][:, 2, 0:SEQ],
                                 b.b3e[:, e:e + 1], b.a3[s][:, n % 2, :], ALU.add, ALU.mult)\
           .then_inc(g("L3f_b", s), 1)
        if e < NE:
            dve.wait_ge(g("L3f_b", s), n + 1)
            dve.wait_ge(g("L3f_G", s), n - 1)
            dve.tensor_tensor(b.he[s][:, n % 2, :], b.he[s][:, n % 2, :],
                              b.ps[s][:, 3, 0:SEQ], ALU.mult)\
               .then_inc(g("L3f_c", s), 1)
        yield


SCAN_CHUNKS = DC * BLK // 2


def project_states(nc, g, b, block):
    halves = [(n, h) for n in range(4) for h in range(DC)]
    units = [("k", n, h) for n, h in halves] + [("v", n, h) for n, h in halves] + [("q", n, h) for n, h in halves]
    NK, RING = len(halves), 6

    @block.tensor
    def _(pe):
        def norm_sum(n):
            pe.wait_ge(g("k_square"), n + 1)
            if n >= 2:
                pe.wait_ge(g("k_norm"), n - 1)
            pe.matmul(b.pst[:, 6 + n % 2, :], lhsT=b.same_block[:, :], rhs=b.sq[:, n % 2, :], start=True,
                      stop=True, skip_group_check=True).then_inc(g("k_sum"), 1)

        for u, (name, n, h) in enumerate(units):
            if u >= RING:
                before = u - RING
                if before < NK:
                    pe.wait_ge(g("k_square"), before + 1)
                else:
                    pe.wait_ge(g("vq_copied"), before - NK + 1)
            for i in range(DC):
                last = pe.matmul(b.pst[:, u % RING, :], lhsT=b.w0[name][:, i, h * P:(h + 1) * P],
                                 rhs=b.xT_all[:, i, n * 512:(n + 1) * 512], start=(i == 0), stop=(i == DC - 1),
                                 skip_group_check=True)
            last.then_inc(g("projected"), 1)
            if 1 <= u <= NK:
                norm_sum(u - 1)

    @block.scalar
    def _(act):
        def root(n):
            act.wait_ge(g("k_sum"), n + 1)
            if n >= 2:
                act.wait_ge(g("k_ready"), n - 1)
            act.activation(b.nrm[:, n % 2, :], b.pst[:, 6 + n % 2, :], ACT.Sqrt).then_inc(g("k_norm"), 1)

        for u, (n, h) in enumerate(halves):
            act.wait_ge(g("projected"), u + 1)
            act.activation(b.kn[:, h, n * 512:(n + 1) * 512], b.pst[:, u % RING, :], ACT.Copy)\
               .then_inc(g("k_copied"), 1)
            if u >= 2:
                act.wait_ge(g("k_sum"), u - 1)
            act.activation(b.sq[:, u % 2, :], b.pst[:, u % RING, :], ACT.Square).then_inc(g("k_square"), 1)
            if u >= 1:
                root(u - 1)
        root(NK - 1)

    @block.vector
    def _(dve):
        link = Chain(dve, g("dve_chain"))
        for u, (n, h) in enumerate(halves):
            dve.wait_ge(g("k_norm"), u + 1)
            dve.wait_ge(g("k_copied"), u + 1)
            r, k = b.nrm[:, u % 2, :], b.kn[:, h, n * 512:(n + 1) * 512]
            link(dve.tensor_scalar(r, r, 1e-6, None, ALU.add))
            link(dve.reciprocal(r, r))
            dve.tensor_tensor(k, k, r, ALU.mult).then_inc(g("k_ready"), 1)
        for u in range(NK, len(units)):
            name, n, h = units[u]
            dve.wait_ge(g("projected"), u + 1)
            dst = b.v0 if name == "v" else b.q0
            dve.tensor_copy(dst[:, h, n * 512:(n + 1) * 512], b.pst[:, u % RING, :]).then_inc(g("vq_copied"), 1)


def scan_step(nc, g, b, block, t):
    at = lambda a, h: a[:, h, :].rearrange("p (t n) -> p t n", t=NB)[:, t, :]
    wide = lambda a: a.unsqueeze(1).to_broadcast([P, 2, SEQ])
    chunks = [(c // 4, c % 4) for c in range(SCAN_CHUNKS)]
    RING = 6

    @block.vector
    def _(dve):
        link = Chain(dve, g("dve_chain"))
        dve.tensor_copy(b.x[0][:, :, :], b.x_all[:, bass.ds(t * TILES, TILES), :]).then_inc(g("x_in"), 1)

        def products(c):
            h, i = chunks[c]
            dve.tensor_tensor(b.work[:, c, :].rearrange("p (i n) -> p i n", i=2), b.S[:, h, 2 * i:2 * i + 2, :],
                              wide(at(b.kn, h)), ALU.mult).then_inc(g("s_k"), 1)

        def update(c):
            h, i = chunks[c]
            w = b.work[:, c, :].rearrange("p (i n) -> p i n", i=2)
            dve.wait_ge(g("delta"), c + 1)
            link(dve.tensor_tensor(w, b.pst[:, c % RING, :].rearrange("p (i n) -> p i n", i=2),
                                   wide(at(b.kn, h)), ALU.mult))
            dve.tensor_tensor(w, w, b.S[:, h, 2 * i:2 * i + 2, :], ALU.add).then_inc(g("s_new"), 1)

        for c in range(SCAN_CHUNKS):
            products(c)
            if c >= 2:
                update(c - 2)
        update(SCAN_CHUNKS - 2)
        update(SCAN_CHUNKS - 1)
        dve.wait_ge(g("gates"), 2)
        dve.scalar_tensor_tensor(b.hqT[0][:, :, :], b.xhq[0][:, :, :], 1.0, b.xhc[0][:, :, :], ALU.add, ALU.mult)\
           .then_inc(g("gated"), 1)
        dve.wait_ge(g("x_in"), 1)
        norm_dve(dve, link, g, b, 0, "L0a", 3, half=True)
        dve.wait_ge(g("L0a_x", 0), TILES)
        dve.tensor_copy(b.x_all[:, bass.ds(t * TILES, TILES), :], b.x[0][:, :, :]).then_inc(g("x_out"), 1)

    @block.tensor
    def _(pe):
        def delta(c):
            h, i = chunks[c]
            pe.wait_ge(g("s_k"), c + 1)
            if c >= RING:
                pe.wait_ge(g("s_new"), c - RING + 1)
            pe.matmul(b.pst[:, c % RING, :], lhsT=b.minus_same_block[:, :], rhs=b.work[:, c, :], start=True,
                      stop=False, skip_group_check=True)
            for m in range(2):
                last = pe.matmul(b.pst[:, c % RING, m * SEQ:(m + 1) * SEQ], lhsT=b.spread[:, 2 * i + m, :],
                                 rhs=at(b.v0, h), start=False, stop=True, skip_group_check=True)
            last.then_inc(g("delta"), 1)

        def read_out(c):
            h, i = chunks[c]
            pe.wait_ge(g("s_q"), c + 1)
            for m in range(2):
                last = pe.matmul(b.pst[:, 6, h * SEQ:(h + 1) * SEQ], lhsT=b.collect[:, 2 * i + m, :],
                                 rhs=b.sq_out[:, c, m * SEQ:(m + 1) * SEQ], start=(i == 0 and m == 0),
                                 stop=(i == 3 and m == 1), skip_group_check=True)
            if c == SCAN_CHUNKS - 1:
                last.then_inc(g("y"), 1)

        for c in range(SCAN_CHUNKS):
            delta(c)
            if c >= 4:
                read_out(c - 4)
        for c in range(SCAN_CHUNKS - 4, SCAN_CHUNKS):
            read_out(c)
        pe.wait_ge(g("gated"), 1)
        for tt in range(TILES):
            for c in range(DC):
                last = pe.transpose(b.pst[:, 3, tt * D + c * P:tt * D + (c + 1) * P],
                                    b.hqT[0][:, c, tt * P:(tt + 1) * P], b.ident[:, :])
        last.then_inc(g("L0a_out", 0), 1)

    @block.scalar
    def _(act):
        for c in range(SCAN_CHUNKS):
            h, i = chunks[c]
            act.wait_ge(g("s_new"), c + 1)
            act.activation(b.S[:, h, 2 * i:2 * i + 2, :], b.work[:, c, :].rearrange("p (i n) -> p i n", i=2),
                           ACT.Tanh).then_inc(g("s_tanh"), 1)
        act.wait_ge(g("y"), 1)
        y = b.pst[:, 6, :]
        act.activation(b.xhq[0][:, :, :].rearrange("p c n -> p (c n)"), y, ACT.Tanh, scale=0.5).then_inc(g("gates"), 1)
        act.activation(b.xhc[0][:, :, :].rearrange("p c n -> p (c n)"), y, ACT.Square).then_inc(g("gates"), 1)

    @block.gpsimd
    def _(pool):
        for c in range(SCAN_CHUNKS):
            h, i = chunks[c]
            pool.wait_ge(g("s_tanh"), c + 1)
            pool.tensor_tensor(b.sq_out[:, c, :].rearrange("p (i n) -> p i n", i=2), b.S[:, h, 2 * i:2 * i + 2, :],
                               wide(at(b.q0, h)), ALU.mult).then_inc(g("s_q"), 1)
        norm_pool(pool, g, b, 0, "L0a")


FC = FF1 // P


class Scale:

    def __init__(self, g, b, name, col):
        self.g, self.b, self.name, self.col = g, b, name, col

    def pe(self, pe):
        g, b, n = self.g, self.b, self.name
        pe.wait_ge(g(n + "_max"), 1)
        pe.transpose(b.pst[0:1, self.col, 0:P], b.gmax[:, self.col:self.col + 1], b.ident[:, :]).then_inc(g(n + "_row"), 1)
        pe.wait_ge(g(n + "_one"), 1)
        pe.matmul(b.pst[:, self.col, P:P + 1], lhsT=b.ones[0:1, :], rhs=b.gone[0:1, self.col:self.col + 1], start=True,
                  stop=True, skip_group_check=True).then_inc(g(n + "_all"), 1)

    def dve(self, dve, link):
        g, b, n, c = self.g, self.b, self.name, self.col
        dve.wait_ge(g(n + "_row"), 1)
        dve.tensor_reduce(b.gone[0:1, c:c + 1], b.pst[0:1, self.col, 0:P], X, ALU.max).then_inc(g(n + "_one"), 1)
        dve.wait_ge(g(n + "_all"), 1)
        link(dve.tensor_scalar(b.scale[:, c:c + 1], b.pst[:, self.col, P:P + 1], 1.0 / QMAX, 1e-12, ALU.mult, ALU.max))
        link(dve.reciprocal(b.inv[:, c:c + 1], b.scale[:, c:c + 1]))


def quantise_x(nc, g, b, block):
    sc = Scale(g, b, "sx", 0)

    @block.vector
    def _(dve):
        link = Chain(dve, g("dve_chain"))
        dve.tensor_reduce(b.gmax[:, 0:1], b.x_all[:, :, :], XY, ALU.max, apply_absolute_value=True)\
           .then_inc(g("sx_max"), 1)
        sc.dve(dve, link)

    @block.tensor
    def _(pe):
        sc.pe(pe)


def up_and_gate(nc, g, b, block, i):
    T4 = 4
    units = [(w, m) for w in range(2) for m in range(FC)]

    @block.vector
    def _(dve):
        link = Chain(dve, g("dve_chain"))
        link(dve.tensor_scalar(b.xq[:, :, :], b.x_all[:, bass.ds(i * T4, T4), :], b.inv[:, 0:1], ROUND,
                               ALU.mult, ALU.add))
        dve.tensor_scalar(b.xq[:, :, :], b.xq[:, :, :], -ROUND, b.scale[:, 0:1], ALU.add, ALU.mult)\
           .then_inc(g("xq"), 1)
        for n, (w, m) in enumerate(units):
            dve.wait_ge(g("ug_copy"), n + 1)
            dve.tensor_reduce(b.umax[:, w, m, bass.ds(i, 1)], b.ug[w][:, m, bass.ds(i * 512, 512)], X, ALU.max,
                              apply_absolute_value=True).then_inc(g("ug_max"), 1)

    @block.tensor
    def _(pe):
        pe.wait_ge(g("xq"), 1)
        for c in range(DC):
            for t in range(T4):
                last = pe.transpose(b.pst[:, c, t * P:(t + 1) * P], b.xq[:, t, c * P:(c + 1) * P], b.ident[:, :])
        last.then_inc(g("xqt"), 1)
        pe.wait_ge(g("xqT"), 1)
        for n, (w, m) in enumerate(units):
            if n >= 4:
                pe.wait_ge(g("ug_copy"), n - 3)
            for c in range(DC):
                last = pe.matmul(b.pst[:, 2 + n % 4, :], lhsT=b.wug[w][:, c, m * P:(m + 1) * P],
                                 rhs=b.xqT[:, c, :], start=(c == 0), stop=(c == DC - 1), skip_group_check=True)
            last.then_inc(g("ug"), 1)

    @block.scalar
    def _(act):
        act.wait_ge(g("xqt"), 1)
        act.activation(b.xqT[:, :, :], b.pst[:, 0:2, :], ACT.Copy).then_inc(g("xqT"), 1)
        for n, (w, m) in enumerate(units):
            act.wait_ge(g("ug"), n + 1)
            act.activation(b.ug[w][:, m, bass.ds(i * 512, 512)], b.pst[:, 2 + n % 4, :], ACT.Copy)\
               .then_inc(g("ug_copy"), 1)


def gate_products(nc, g, b, block):
    su, sg, s2, so = (Scale(g, b, n, c) for c, n in ((1, "su"), (2, "sg"), (3, "s2"), (4, "so")))
    up, gate = b.ug

    def gated(dve, link, m):
        dve.wait_ge(g("sig"), m + 1)
        link(dve.scalar_tensor_tensor(gate[:, m, :], b.sig[:, m % 2, :], 1.0 / 65536.0, gate[:, m, :],
                                      ALU.mult, ALU.mult))
        g_done = dve.tensor_reduce(b.fmax[:, 0, m:m + 1], gate[:, m, :], X, ALU.max, apply_absolute_value=True)
        g_done.then_inc(g("g2"), 1)
        dve.wait_ge(g("g2"), m + 1)

    @block.tensor
    def _(pe):
        for sc in (su, sg, s2, so):
            sc.pe(pe)

    @block.vector
    def _(dve):
        link = Chain(dve, g("dve_chain"))
        dve.tensor_reduce(b.gmax[:, 1:2], b.umax[:, 0, :, :], XY, ALU.max).then_inc(g("su_max"), 1)
        dve.tensor_reduce(b.gmax[:, 2:3], b.umax[:, 1, :, :], XY, ALU.max).then_inc(g("sg_max"), 1)
        su.dve(dve, link)
        sg.dve(dve, link)
        dve.nop().then_inc(g("scales"), 1)
        for m in range(FC):
            link(dve.tensor_scalar(gate[:, m, :], gate[:, m, :], b.inv[:, 2:3], ROUND, ALU.mult, ALU.add))
            dve.tensor_scalar(gate[:, m, :], gate[:, m, :], -ROUND, b.scale[:, 2:3], ALU.add, ALU.mult)\
               .then_inc(g("gq"), 1)
            if m >= 1:
                gated(dve, link, m - 1)
        gated(dve, link, FC - 1)
        dve.tensor_reduce(b.gmax[:, 3:4], b.fmax[:, 0, :], X, ALU.max).then_inc(g("s2_max"), 1)
        s2.dve(dve, link)
        for m in range(FC):
            link(dve.tensor_scalar(gate[:, m, :], gate[:, m, :], b.inv[:, 3:4], ROUND, ALU.mult, ALU.add))
            link(dve.tensor_scalar(gate[:, m, :], gate[:, m, :], -ROUND, b.scale[:, 3:4], ALU.add, ALU.mult))
            dve.wait_ge(g("uq"), m + 1)
            link(dve.tensor_tensor(gate[:, m, :], gate[:, m, :], up[:, m, :], ALU.mult))
            link(dve.tensor_reduce(b.fmax[:, 1, m:m + 1], gate[:, m, :], X, ALU.max, apply_absolute_value=True))
        dve.tensor_reduce(b.gmax[:, 4:5], b.fmax[:, 1, :], X, ALU.max).then_inc(g("so_max"), 1)
        so.dve(dve, link)

    @block.scalar
    def _(act):
        for m in range(FC):
            act.wait_ge(g("gq"), m + 1)
            if m >= 2:
                act.wait_ge(g("g2"), m - 1)
            act.activation(b.sig[:, m % 2, :], gate[:, m, :], ACT.Tanh, scale=0.5).then_inc(g("th"), 1)

    @block.gpsimd
    def _(pool):
        link = Chain(pool, g("pool_chain"))
        pool.wait_ge(g("scales"), 1)
        for m in range(FC):
            link(pool.tensor_scalar(up[:, m, :], up[:, m, :], b.inv[:, 1:2], ROUND, ALU.mult, ALU.add))
            pool.tensor_scalar(up[:, m, :], up[:, m, :], -ROUND, b.scale[:, 1:2], ALU.add, ALU.mult)\
                .then_inc(g("uq"), 1)
            pool.wait_ge(g("th"), m + 1)
            s = b.sig[:, m % 2, :]
            link(pool.tensor_scalar(s, s, 32768.0, ROUND + 32768.0, ALU.mult, ALU.add))
            pool.tensor_scalar(s, s, -ROUND, 65535.0, ALU.add, ALU.min).then_inc(g("sig"), 1)


def down(nc, g, b, block, i):
    @block.vector
    def _(dve):
        link = Chain(dve, g("dve_chain"))
        for s in range(SB):
            for t in range(TILES):
                dve.tensor_copy(b.x[s][:, t, :], b.x_all[:, bass.ds((i * SB + s) * TILES + t, 1), :]
                                .rearrange("p a n -> p (a n)")).then_inc(g("x_in", s), 1)
        for s in range(SB):
            o = b.oq[s]
            link(dve.tensor_scalar(o[:, :, :], b.ug[1][:, :, bass.ds((i * SB + s) * SEQ, SEQ)], b.inv[:, 4:5],
                                   ROUND, ALU.mult, ALU.add))
            dve.tensor_scalar(o[:, :, :], o[:, :, :], -ROUND, b.scale[:, 4:5], ALU.add, ALU.mult)\
               .then_inc(g("oq", s), 1)
        for s in range(SB):
            dve.wait_ge(g("x_in", s), TILES)
            norm_dve(dve, link, g, b, s, "L1f", 0)
        for s in range(SB):
            dve.wait_ge(g("L1f_x", s), TILES)
            for t in range(TILES):
                dve.tensor_copy(b.x_all[:, bass.ds((i * SB + s) * TILES + t, 1), :].rearrange("p a n -> p (a n)"),
                                b.x[s][:, t, :]).then_inc(g("x_out", s), 1)

    @block.tensor
    def _(pe):
        for s in range(SB):
            pe.wait_ge(g("oq", s), 1)
            for t in range(TILES):
                for m in range(FC):
                    last = pe.matmul(b.ps[s][:, 0, t * D:(t + 1) * D], lhsT=b.oq[s][:, m, t * P:(t + 1) * P],
                                     rhs=b.wd[:, m, :], start=(m == 0), stop=(m == FC - 1), skip_group_check=True)
            last.then_inc(g("L1f_out", s), 1)

    @block.gpsimd
    def _(pool):
        for s in range(SB):
            norm_pool(pool, g, b, s, "L1f")


def quantise_weights(nc, g, b, block):
    todo = [(b.wnat[n], b.wsc[n]) for n in range(3)]

    @block.vector
    def _(dve):
        link = Chain(dve, g("dve_chain"))
        for n, (w, sc) in enumerate(todo):
            blocks = w.rearrange("p a (k r) -> p (a k) r", r=32)
            wide = lambda a: a.unsqueeze(2).to_broadcast([P, 48, 32])
            link(dve.tensor_reduce(sc[:, 0, :], blocks, X, ALU.max, apply_absolute_value=True))
            link(dve.tensor_scalar(sc[:, 0, :], sc[:, 0, :], 1.0 / 7.0, 1e-12, ALU.mult, ALU.max))
            link(dve.reciprocal(sc[:, 1, :], sc[:, 0, :]))
            link(dve.tensor_tensor(blocks, blocks, wide(sc[:, 1, :]), ALU.mult))
            link(dve.tensor_scalar(blocks, blocks, ROUND, -ROUND, ALU.add, ALU.add))
            dve.tensor_tensor(blocks, blocks, wide(sc[:, 0, :]), ALU.mult).then_inc(g("wq"), 1)

    @block.tensor
    def _(pe):
        for n in range(3):
            pe.wait_ge(g("wq"), n + 1)
            w = b.wnat[n]
            if n >= 2:
                pe.wait_ge(g("wqT"), 3 * (n - 1))
            for k in range(12):
                a, c = (k // 2, k % 2) if n < 2 else (k // 6, k % 6)
                bank = 3 * (n % 2) + (k // 4)
                last = pe.transpose(b.pst[:, bank, (k % 4) * P:(k % 4 + 1) * P], w[:, a, c * P:(c + 1) * P],
                                    b.ident[:, :])
                if k % 4 == 3:
                    last.then_inc(g("wqt"), 1)

    @block.scalar
    def _(act):
        for n in range(3):
            for q in range(3):
                act.wait_ge(g("wqt"), 3 * n + q + 1)
                bank = b.pst[:, 3 * (n % 2) + q, :]
                if n < 2:
                    dst = b.wug[n][:, :, q * 2 * P:(q + 1) * 2 * P].rearrange("p c (a o) -> p a c o", a=2)
                    src = bank.rearrange("p (a c o) -> p a c o", a=2, c=2)
                    act.activation(dst, src, ACT.Copy).then_inc(g("wqT"), 1)
                else:
                    for j in range(4):
                        k = 4 * q + j
                        ins = act.activation(b.wd[:, k % 6, (k // 6) * P:(k // 6 + 1) * P],
                                             bank[:, j * P:(j + 1) * P], ACT.Copy)
                    ins.then_inc(g("wqT"), 1)


class Buffers:
    pass


def region(nc, body):
    with ExitStack() as ctx:
        g = Signals(nc, ctx)
        with nc.Block(no_gpsimd_drain=True) as block:
            body(g, block)
        runs = g.runs()
        for r in runs[1:]:
            nc.gpsimd.sem_clear(r)
        nc.all_engine_barrier(sems_to_clear=runs[0])


def load(block, g, pairs):
    @block.sync
    def _(sp):
        for dst, src in pairs[0::2]:
            sp.dma_start(dst, src).then_inc(g("loaded"), 16)
        sp.wait_ge(g("loaded"), 16 * len(pairs))

    return pairs[1::2], 16 * len(pairs)


def chunked(ap):
    return ap.rearrange("(c p) n -> p c n", p=P)


def pairs_of(b, sb):
    return lambda name, shape, dt=F32: [sb(f"{b.phase}_{name}_{s}", shape, dt) for s in range(SB)]


def common_buffers(b, pair):
    b.x = pair("x", [P, TILES, D])
    b.r = pair("r", [P, TILES, D])
    b.st = pair("st", [P, TILES, 6])
    b.mv = pair("mv", [P, TILES, 2])
    b.rstd = pair("rstd", [P, TILES])


def heads_buffers(b, pair, keys, dv=DH):
    b.xT = pair("xT", [P, DC, SEQ])
    b.ctx = pair("ctx", [SK, D])
    b.ctxT = pair("ctxT", [P, DC, SK])
    b.qT = pair("qT", [P, DC, SEQ])
    b.kT = pair("kT", [P, DC, SEQ])
    b.qs = pair("qs", [P, DC, NH // DC, SEQ], BF16)
    b.ks = pair("ks", [P, DC, NH // DC, keys], BF16)
    b.vn = pair("vn", [P, TILES, NH * SLOT])
    b.PT = pair("PT", [P, 4, 512])
    b.mx = pair("mx", [P, TILES, NH])
    b.mxr = pair("mxr", [P, TILES, NH])
    b.mxp = pair("mxp", [P, TILES, PARTS, NH], BF16)
    b.mxT = pair("mxT", [PARTS * NH, SEQ], BF16)
    b.kr = pair("kr", [P, DC, SEQ])
    b.oT = pair("oT", [P, NH * max(SLOT, dv) // P, SEQ])
    words = PARTS * DC * SEQ // 2
    for n, name in enumerate(("qp", "kp")):
        flat = [PT[:, :, :].rearrange("p a n -> p (a n)")[:, n * words:(n + 1) * words] for PT in b.PT]
        parts = [f.bitcast(BF16).rearrange("p (a c n) -> p a c n", a=PARTS, c=DC) for f in flat]
        if n == 0:
            b.qp = parts
        else:
            b.kp = parts
    b.A = [PT[:, 1, SEQ:SEQ + TILES * SK].rearrange("p (t n) -> p t n", t=TILES) for PT in b.PT]
    b.AT = [PT[0:SK, 2, SEQ:2 * SEQ] for PT in b.PT]
    b.nm = pair("nm", [P, TILES])
    b.ssum = pair("ssum", [P, TILES])


def clear_spares(pool, b):
    for s in range(SB):
        pool.memset(b.vn[s][:, :, :], 0.0)


def take_in(dve, g, b, s, i):
    for t in range(TILES):
        dve.tensor_copy(b.x[s][:, t, :], b.x_all[:, bass.ds((i * SB + s) * TILES + t, 1), :]
                        .rearrange("p a n -> p (a n)")).then_inc(g("in_x", s), 1)
    dve.wait_ge(g("in_x", s), TILES)


def put_back(dve, g, b, s, i, L):
    dve.wait_ge(g(L + "_x", s), TILES)
    for t in range(TILES):
        dve.tensor_copy(b.x_all[:, bass.ds((i * SB + s) * TILES + t, 1), :].rearrange("p a n -> p (a n)"),
                        b.x[s][:, t, :]).then_inc(g("back", s), 1)


def load_context(sp, g, b, i, s):
    sp.dma_start(b.ctx[s][:, :], b.dram["ctx"].rearrange("(i s) k d -> i s k d", s=SB)[i, s])\
        .then_inc(g("ctx", s), 16)
    sp.dma_start(b.ctxT[s][:, :, :], b.dram["ctxT"].rearrange("(i s) (c p) k -> i s p c k", s=SB, p=P)[i, s])\
        .then_inc(g("ctx", s), 16)


def phase_state(nc, b):
    b.phase = "state"
    with ExitStack() as ctx:
        sb = lambda n, shape, dt=F32: ctx.enter_context(nc.sbuf_tensor(n, shape, dt))
        d = b.dram
        pair = pairs_of(b, sb)
        common_buffers(b, pair)
        b.hqT = pair("hqT", [P, DC, SEQ])
        b.xhq = pair("xhq", [P, DC, SEQ])
        b.xhc = pair("xhc", [P, DC, SEQ])
        b.kn, b.v0, b.q0 = (sb(n, [P, DC, TOKENS]) for n in ("kn", "v0", "q0"))
        b.same_block, b.minus_same_block = sb("same_block", [P, P]), sb("minus_same_block", [P, P])
        b.spread, b.collect = sb("spread", [P, BLK, P]), sb("collect", [P, BLK, P])
        with ExitStack() as inner:
            sbi = lambda n, shape, dt=F32: inner.enter_context(nc.sbuf_tensor(n, shape, dt))
            b.xT_all = sbi("xT_all", [P, DC, TOKENS])
            b.w0 = {n: sbi("w0" + n, [P, DC, D]) for n in "kvq"}
            b.sq, b.nrm = sbi("sq", [P, 2, 512]), sbi("nrm", [P, 2, 512])

            def begin(g, block):
                pairs = [(b.xT_all[:, :, :], chunked(d["xT"])),
                         (b.x_all[:, :, :], d["x"].rearrange("(a p) n -> p a n", p=P))]
                pairs += [(b.w0[n][:, :, :], chunked(d["w0" + n])) for n in "kvq"]
                pairs += [(b.same_block[:, :], d["same_block"]), (b.ident[:, :], d["ident"]),
                          (b.spread[:, :, :], d["spread"]), (b.collect[:, :, :], d["collect"])]
                rest, total = load(block, g, pairs)

                @block.scalar
                def _(act):
                    for dst, src in rest:
                        act.dma_start(dst, src).then_inc(g("loaded"), 16)
                    act.wait_ge(g("loaded"), total)

                @block.vector
                def _(dve):
                    dve.memset(b.ones[:, :], 1.0)
                    dve.memset(b.minus_half[:, :], -0.5)
                    dve.wait_ge(g("loaded"), total)
                    dve.tensor_copy(b.identb[:, :], b.ident[:, :])
                    dve.tensor_scalar(b.minus_same_block[:, :], b.same_block[:, :], -1.0, None, ALU.mult)

            region(nc, begin)
            region(nc, lambda g, block: project_states(nc, g, b, block))
        b.S = sb("S", [P, DC, BLK, SEQ])
        b.work, b.sq_out = sb("work", [P, SCAN_CHUNKS, 512]), sb("sq_out", [P, SCAN_CHUNKS, 512])

        def clear(g, block):
            @block.vector
            def _(dve):
                dve.memset(b.S[:, :, :, :], 0.0).then_inc(g("cleared"), 1)

        region(nc, clear)
        with nc.Fori(0, NB) as t:
            region(nc, lambda g, block: scan_step(nc, g, b, block, t))


def phase_first(nc, b):
    b.phase = "first"

    def stack_constants(g, block):
        @block.vector
        def _(dve):
            link = Chain(dve, g("dve_chain"))
            link(dve.memset(b.sel_q[:, :, :, :], 0.0), dve.memset(b.sel_k[:, :, :, :], 0.0))
            rows = b.identb[:, :].rearrange("p (h d) -> p h d", d=DH).unsqueeze(2)
            for sel, places in ((b.sel_q, [slice(0, 3), slice(3, 6), slice(6, 8)]),
                                (b.sel_k, [slice(p, PRODUCTS, PARTS) for p in range(PARTS)])):
                for p, places_p in enumerate(places):
                    dst = sel[:, p, :, :].rearrange("p h (t d) -> p h t d", d=DH)[:, :, places_p, :]
                    dve.tensor_copy(dst, rows.to_broadcast([P, P // DH, dst.shape[2], DH]))
            link(dve.tensor_tensor(b.one16[:, :], b.ident[0:48, 0:NH], b.ident[0:48, NH:2 * NH], ALU.add))
            link(dve.tensor_tensor(b.one16[:, :], b.one16[:, :], b.ident[0:48, 2 * NH:3 * NH], ALU.add))
            dve.tensor_copy(b.onehot[:, :, :], b.one16[:, :].unsqueeze(2).to_broadcast([PARTS * NH, NH, P]))

    region(nc, stack_constants)
    with ExitStack() as ctx:
        sb = lambda n, shape, dt=F32: ctx.enter_context(nc.sbuf_tensor(n, shape, dt))
        d = b.dram
        pair = pairs_of(b, sb)
        common_buffers(b, pair)
        heads_buffers(b, pair, SK)
        b.nM = pair("nM", [1, 1])
        b.nMb = pair("nMb", [P, 1])
        b.ecol = pair("ecol", [P, TILES])
        b.hc = pair("hc", [P, DC])
        b.mask_u8 = pair("mask_u8", [P, TILES, NH, SK], U8)
        b.maskT_u8 = pair("maskT_u8", [SK, NH, SEQ], U8)
        b.mask = pair("mask", [P, TILES, NH, SK], BF16)
        b.maskT = pair("maskT", [SK, NH, SEQ], BF16)
        b.hqT, b.xhq, b.xhc = b.qT, b.kT, b.kr
        part = lambda bank, at, n: [PT[:, bank, at:at + n] for PT in b.PT]
        tiles = lambda views: [v.rearrange("p (t n) -> p t n", t=TILES) for v in views]
        b.sim, b.flow_m = tiles(part(0, 0, TILES * SK)), tiles(part(0, TILES * SK, DC * SK))
        b.sc, b.pb, b.pbT = tiles(part(1, 0, SEQ)), tiles(part(2, 0, SEQ)), part(3, 0, SEQ)
        b.bq, b.bk, b.bv = b.hqT, b.xhq, b.xhc
        wsim = sb("wsim", [P, 3 * DC])
        b.w1, w2, b.w3 = wsim[:, 0:2], wsim[:, 2:4], wsim[:, 4:6]
        b.b_sim, b.w2_wide = sb("b_sim", [P, 1]), sb("w2_wide", [P, DC, P])
        wqv, w0f = sb("wqv", [P, 4 * DC, D]), sb("w0f", [P, DC, D])
        l1a, l1o = sb("l1a", [P, DC, 3 * D]), sb("l1o", [P, DC, D])
        lq, lk = sb("lq", [P, DC, D]), sb("lk", [P, DC, D])
        lv, lo = sb("lv", [P, DC, D]), sb("lo", [P, HC, D])
        row = {n: sb("row_" + n, [P, D]) for n in ("qv", "f0", "o1", "v1", "x1")}
        qb, kb = sb("qb", [P, DC]), sb("kb", [P, DC])
        b.causal32 = sb("causal32", [P, P])
        ld, da = sb("ld", [100, 4]), sb("da", [100, D])
        lu, ua = sb("lu", [4, 50]), sb("ua", [50, D])
        t1, t2 = sb("t1", [4, D]), sb("t2", [50, D])
        b.w = {"L0x": wqv, "L0f": w0f, "L1a": l1a, "L1x": {"q": lq, "k": lk, "v": lv}}
        b.wo = {"L1a": l1o, "L1x": lo}
        b.heads = {"L1x": Heads("L1x", [(0, SK)], DH, (2, 2, 1), "per_head")}

        def begin(g, block):
            pairs = [(wsim[:, :], d["wsim"]), (b.b_sim[:, :], d["b_sim"].partition_broadcast(P)),
                     (wqv[:, :, :], chunked(d["wqv"])), (w0f[:, :, :], chunked(d["w0f"])),
                     (l1a[:, :, :], chunked(d["w1a"])), (l1o[:, :, :], chunked(d["w1o"])),
                     (lq[:, :, :], chunked(d["w1xq"])), (lk[:, :, :], chunked(d["w1xk"])),
                     (lv[:, :, :], chunked(d["w1xv"])), (lo[:, :, :], chunked(d["w1xo"])),
                     (qb[:, :], d["b1xq"]), (kb[:, :], d["b1xk"]), (b.causal32[:, :], d["causal"]),
                     (ld[:, :], d["ld"]), (da[:, :], d["da"]), (lu[:, :], d["lu"]), (ua[:, :], d["ua"])]
            pairs += [(row[n][:, :], d["row_" + n].partition_broadcast(P)) for n in row]
            rest, total = load(block, g, pairs)

            @block.scalar
            def _(act):
                for dst, src in rest:
                    act.dma_start(dst, src).then_inc(g("loaded"), 16)
                act.wait_ge(g("lora"), 1)
                act.activation(t1[:, :], b.pst[0:4, 0, 0:D], ACT.Copy).then_inc(g("lora_copied"), 1)
                act.wait_ge(g("lora"), 2)
                act.activation(t2[:, :], b.pst[0:50, 1, 0:D], ACT.Copy).then_inc(g("lora_copied"), 1)

            @block.tensor
            def _(pe):
                pe.wait_ge(g("loaded"), total)
                pe.matmul(b.pst[0:4, 0, 0:D], lhsT=ld[:, :], rhs=da[:, :], start=True, stop=True)\
                  .then_inc(g("lora"), 1)
                pe.wait_ge(g("lora_copied"), 1)
                pe.matmul(b.pst[0:50, 1, 0:D], lhsT=lu[:, :], rhs=t1[:, :], start=True, stop=True)\
                  .then_inc(g("lora"), 1)
                pe.wait_ge(g("lora_copied"), 2)
                for c in range(DC):
                    last = pe.matmul(b.pst[:, 2, c * D:(c + 1) * D], lhsT=t2[:, c * P:(c + 1) * P], rhs=ua[:, :],
                                     start=True, stop=True, skip_group_check=True)
                last.then_inc(g("lora"), 1)

            @block.vector
            def _(dve):
                dve.wait_ge(g("loaded"), total)
                dve.tensor_copy(b.w2_wide[:, :, :], w2.unsqueeze(2).to_broadcast([P, DC, P]))
                dve.wait_ge(g("lora"), 3)
                dve.tensor_tensor(w0f[:, :, :], w0f[:, :, :], b.pst[:, 2, :].rearrange("p (c n) -> p c n", c=DC),
                                  ALU.add)

            @block.gpsimd
            def _(pool):
                clear_spares(pool, b)

        region(nc, begin)

        def turn(i):
            def body(g, block):
                @block.sync
                def _(sp):
                    for s in range(SB):
                        load_context(sp, g, b, i, s)
                    for s in range(SB):
                        for t in range(TILES):
                            src = d["mask"].rearrange("(i s) (t p) h k -> i s t p h k", s=SB, p=P)[i, s, t]
                            sp.dma_start(b.mask_u8[s][:, t, :, :], src).then_inc(g("mask_in", s), 16)
                        src = d["maskT"].rearrange("(i s) k h q -> i s k h q", s=SB)[i, s]
                        sp.dma_start(b.maskT_u8[s][:, :, :], src).then_inc(g("mask_in", s), 16)

                @block.gpsimd
                def _(pool):
                    link = Chain(pool, g("pool_chain"))
                    for s in range(SB):
                        norm_pool(pool, g, b, s, "L0x")
                    for s in range(SB):
                        norm_pool(pool, g, b, s, "L0f")
                    for s in range(SB):
                        norm_pool(pool, g, b, s, "L1a")
                    for s in range(SB):
                        split_k(pool, link, g, b, s, b.heads["L1x"])
                    for s in range(SB):
                        norm_pool(pool, g, b, s, "L1x")

                def pe_program(pe, s):
                    norm_pe(pe, g, b, s, "in", 2)
                    yield
                    yield from flow_pe(pe, g, b, s, "in")
                    norm_pe(pe, g, b, s, "L0x", 2)
                    yield
                    pe.wait_ge(g("L0x_xT", s), 1)
                    project(pe, b.ps[s], 0, b.xT[s], w0f).then_inc(g("L0f_out", s), 1)
                    yield
                    norm_pe(pe, g, b, s, "L0f", 2)
                    yield
                    yield from block_pe(pe, g, b, s, "L0f")
                    norm_pe(pe, g, b, s, "L1a", 2)
                    yield
                    yield from cross_pe(pe, g, b, s, "L1x", "L1a")
                    yield from heads_pe(pe, g, b, s, b.heads["L1x"])

                @block.tensor
                def _(pe):
                    side_by_side([pe_program(pe, s) for s in range(SB)])

                def act_program(act, s):
                    norm_act(act, g, b, s, "in", 2)
                    yield
                    yield from flow_act(act, g, b, s)
                    act.wait_ge(g("mask_in", s), 48)
                    act.activation(b.mask[s][:, :, :, :], b.mask_u8[s][:, :, :, :], ACT.Copy, scale=NEG)\
                       .then_inc(g("L1x_mask", s), 1)
                    act.activation(b.maskT[s][:, :, :], b.maskT_u8[s][:, :, :], ACT.Copy, scale=NEG)\
                       .then_inc(g("L1x_mask", s), 1)
                    norm_act(act, g, b, s, "L0x", 2)
                    yield
                    norm_act(act, g, b, s, "L0f", 2)
                    yield
                    yield from block_act(act, g, b, s)
                    norm_act(act, g, b, s, "L1a", 2)
                    yield
                    yield from cross_act(act, g, b, s, "L1x", qb, kb)
                    yield from heads_act(act, g, b, s, b.heads["L1x"])

                @block.scalar
                def _(act):
                    side_by_side([act_program(act, s) for s in range(SB)])

                def dve_program(dve, link, s):
                    take_in(dve, g, b, s, i)
                    yield
                    yield from flow_dve(dve, link, g, b, s)
                    norm_dve(dve, link, g, b, s, "L0x", 0, row["qv"][:, :])
                    yield
                    norm_dve(dve, link, g, b, s, "L0f", 0, row["f0"][:, :])
                    yield
                    yield from block_dve(dve, link, g, b, s)
                    norm_dve(dve, link, g, b, s, "L1a", 0, row["o1"][:, :])
                    yield
                    yield from cross_dve(dve, link, g, b, s, "L1x", row["v1"])
                    yield from heads_dve(dve, link, g, b, s, b.heads["L1x"])
                    norm_dve(dve, link, g, b, s, "L1x", 1, row["x1"][:, :])
                    yield
                    put_back(dve, g, b, s, i, "L1x")

                @block.vector
                def _(dve):
                    link = Chain(dve, g("dve_chain"))
                    side_by_side([dve_program(dve, link, s) for s in range(SB)])

            return body

        with nc.Fori(0, NB // SB) as i:
            region(nc, turn(i))


def phase_quantised(nc, b):
    b.phase = "quantised"
    with ExitStack() as ctx:
        sb = lambda n, shape, dt=F32: ctx.enter_context(nc.sbuf_tensor(n, shape, dt))
        d = b.dram
        b.ug = [sb("up", [P, FC, TOKENS]), sb("gate", [P, FC, TOKENS])]
        b.wd = sb("wd", [P, FC, D])
        b.gmax, b.gone, b.scale, b.inv = sb("gmax", [P, 5]), sb("gone", [1, 5]), sb("scale", [P, 5]), sb("inv", [P, 5])
        b.umax, b.fmax = sb("umax", [P, 2, FC, 4]), sb("fmax", [P, 2, FC])
        with ExitStack() as inner:
            sbi = lambda n, shape, dt=F32: inner.enter_context(nc.sbuf_tensor(n, shape, dt))
            b.wug = [sbi("wup", [P, DC, FF1]), sbi("wgate", [P, DC, FF1])]
            shapes = [(FC, D), (FC, D), (DC, FF1)]
            wn = [sbi(f"wnat{n}", [P, a, m]) for n, (a, m) in enumerate(shapes)]
            b.wnat = [w[:, :, :] for w in wn]
            b.wsc = [sbi(f"wsc{n}", [P, 2, 48]) for n in range(3)]
            b.xq, b.xqT = sbi("xq", [P, 4, D]), sbi("xqT", [P, DC, 512])

            def begin(g, block):
                pairs = [(wn[n][:, :, :], chunked(d[k])) for n, k in enumerate(("w_up", "w_gate", "w_down"))]
                rest, total = load(block, g, pairs)

                @block.scalar
                def _(act):
                    for dst, src in rest:
                        act.dma_start(dst, src).then_inc(g("loaded"), 16)

            region(nc, begin)
            region(nc, lambda g, block: quantise_weights(nc, g, b, block))
            region(nc, lambda g, block: quantise_x(nc, g, b, block))
            with nc.Fori(0, 4) as i:
                region(nc, lambda g, block: up_and_gate(nc, g, b, block, i))
        with ExitStack() as inner:
            b.sig = inner.enter_context(nc.sbuf_tensor("sig", [P, 2, TOKENS], F32))
            region(nc, lambda g, block: gate_products(nc, g, b, block))
        pair = pairs_of(b, sb)
        common_buffers(b, pair)
        b.oq = pair("oq", [P, FC, SEQ])
        with nc.Fori(0, NB // SB) as i:
            region(nc, lambda g, block: down(nc, g, b, block, i))


def phase_second(nc, b):
    b.phase = "second"
    with ExitStack() as ctx:
        sb = lambda n, shape, dt=F32: ctx.enter_context(nc.sbuf_tensor(n, shape, dt))
        d = b.dram
        pair = pairs_of(b, sb)
        common_buffers(b, pair)
        heads_buffers(b, pair, SEQ, DV2)
        b.vw = pair("vw", [P, TILES, NH * DV2])
        b.hT = b.oT
        aq, ak, av = sb("aq", [P, DC, D]), sb("ak", [P, DC, D]), sb("av", [P, DC, NH * DV2])
        ao = sb("ao", [P, NH * DV2 // P, D])
        xq, xk, xv, xo = sb("xq2", [P, DC, D]), sb("xk2", [P, DC, D]), sb("xv2", [P, DC, D]), sb("xo2", [P, HC, D])
        f1, f2 = sb("f1", [P, DC, FF2]), sb("f2", [P, FF2 // P, D])
        b.b1, row_b2 = sb("b1", [P, FF2 // P]), sb("row_b2", [P, D])
        causal32, causalT32 = b.r[0][:, 0, 0:P], b.r[0][:, 1, 0:P]
        b.causal, b.causalT = sb("causalb", [P, P], BF16), sb("causalTb", [P, P], BF16)
        sm8, smT8 = sb("sm8", [P, TILES, SK], U8), sb("smT8", [SK, SEQ], U8)
        b.smask, b.smaskT = sb("smask", [P, TILES, SK], BF16), sb("smaskT", [SK, SEQ], BF16)
        valid, gam = sb("valid", [P, TILES]), sb("gam", [P, 2])
        b.w = {"L2a": {"q": aq, "k": ak, "v": av}, "L2x": {"q": xq, "k": xk, "v": xv}, "L2f1": f1, "L2f2": f2}
        b.wo = {"L2a": ao, "L2x": xo}
        b.heads = {"L2a": Heads("L2a", [(0, P), (P, P)], DV2, (1, 1, 2), "causal"),
                   "L2x": Heads("L2x", [(0, SK)], DH, (2, 2, 1), "shared")}

        def begin(g, block):
            pairs = [(w[:, :, :], chunked(d[n])) for w, n in (
                (aq, "w2aq"), (ak, "w2ak"), (av, "w2av"), (ao, "w2ao"), (xq, "w2xq"), (xk, "w2xk"), (xv, "w2xv"),
                (xo, "w2xo"), (f1, "w2f1"), (f2, "w2f2"))]
            pairs += [(b.b1[:, :], d["b2f1"]), (row_b2[:, :], d["row_b2"].partition_broadcast(P)),
                      (causal32[:, :], d["causal"]), (causalT32[:, :], d["causalT"]),
                      (sm8[:, :, :], d["smask"].rearrange("(t p) k -> p t k", p=P)), (smT8[:, :], d["smaskT"])]
            rest, total = load(block, g, pairs)

            @block.scalar
            def _(act):
                for dst, src in rest:
                    act.dma_start(dst, src).then_inc(g("loaded"), 16)

            @block.gpsimd
            def _(pool):
                clear_spares(pool, b)

            @block.tensor
            def _(pe):
                pe.wait_ge(g("sums"), 2)
                pe.matmul(b.pst[:, 0, 0:2], lhsT=b.ones[:, :], rhs=gam[:, :], start=True, stop=True)\
                  .then_inc(g("gamma"), 1)

            @block.vector
            def _(dve):
                link = Chain(dve, g("dve_chain"))
                dve.wait_ge(g("loaded"), total)
                for n, w in enumerate((f1, f2)):
                    dve.tensor_reduce(gam[:, n:n + 1], w[:, :, :], XY, ALU.add, apply_absolute_value=True)\
                       .then_inc(g("sums"), 1)
                dve.tensor_copy(b.causal[:, :], causal32[:, :])
                dve.tensor_copy(b.causalT[:, :], causalT32[:, :])
                dve.tensor_scalar(b.smask[:, :, :], sm8[:, :, :], -NEG, NEG, ALU.mult, ALU.add)
                dve.tensor_scalar(b.smaskT[:, :], smT8[:, :], -NEG, NEG, ALU.mult, ALU.add)
                dve.tensor_reduce(valid[:, :], sm8[:, :, :], X, ALU.max)
                dve.wait_ge(g("gamma"), 1)
                link(dve.tensor_scalar(gam[:, :], b.pst[:, 0, 0:2], 1.0 / (FF2 * D), EPS, ALU.mult, ALU.add))
                link(dve.reciprocal(gam[:, :], gam[:, :]))
                for n, w in enumerate((f1, f2)):
                    link(dve.tensor_scalar(w[:, :, :], w[:, :, :], gam[:, n:n + 1], ROUND, ALU.mult, ALU.add))
                    link(dve.tensor_scalar(w[:, :, :], w[:, :, :], -ROUND, 1.0, ALU.add, ALU.min))
                    link(dve.tensor_scalar(w[:, :, :], w[:, :, :], -1.0, None, ALU.max))

        region(nc, begin)

        def turn(i):
            def body(g, block):
                @block.sync
                def _(sp):
                    for s in range(SB):
                        load_context(sp, g, b, i, s)

                @block.gpsimd
                def _(pool):
                    link = Chain(pool, g("pool_chain"))
                    for L in ("L2a", "L2x", "L2f"):
                        for s in range(SB):
                            if L in b.heads:
                                split_k(pool, link, g, b, s, b.heads[L])
                        for s in range(SB):
                            norm_pool(pool, g, b, s, L)

                def pe_program(pe, s):
                    norm_pe(pe, g, b, s, "in", 3)
                    yield
                    yield from causal_pe(pe, g, b, s, "in")
                    norm_pe(pe, g, b, s, "L2a", 3)
                    yield
                    yield from cross_pe(pe, g, b, s, "L2x", "L2a")
                    yield from heads_pe(pe, g, b, s, b.heads["L2x"])
                    norm_pe(pe, g, b, s, "L2x", 3)
                    yield
                    yield from ternary_pe(pe, g, b, s, "L2x")

                @block.tensor
                def _(pe):
                    side_by_side([pe_program(pe, s) for s in range(SB)])

                def act_program(act, s):
                    norm_act(act, g, b, s, "in", 3)
                    yield
                    yield from causal_act(act, g, b, s)
                    norm_act(act, g, b, s, "L2a", 3)
                    yield
                    yield from cross_act(act, g, b, s, "L2x")
                    yield from heads_act(act, g, b, s, b.heads["L2x"])
                    norm_act(act, g, b, s, "L2x", 3)
                    yield
                    yield from ternary_act(act, g, b, s)

                @block.scalar
                def _(act):
                    side_by_side([act_program(act, s) for s in range(SB)])

                def dve_program(dve, link, s):
                    take_in(dve, g, b, s, i)
                    yield
                    yield from causal_dve(dve, link, g, b, s)
                    norm_dve(dve, link, g, b, s, "L2a", 1)
                    yield
                    yield from cross_dve(dve, link, g, b, s, "L2x")
                    yield from heads_dve(dve, link, g, b, s, b.heads["L2x"], 1e-9)
                    norm_dve(dve, link, g, b, s, "L2x", 1, valid=valid)
                    yield
                    norm_dve(dve, link, g, b, s, "L2f", 0, row_b2[:, :])
                    yield
                    put_back(dve, g, b, s, i, "L2f")

                @block.vector
                def _(dve):
                    link = Chain(dve, g("dve_chain"))
                    side_by_side([dve_program(dve, link, s) for s in range(SB)])

            return body

        with nc.Fori(0, NB // SB) as i:
            region(nc, turn(i))


def phase_third(nc, b, out):
    b.phase = "third"
    with ExitStack() as ctx:
        b.experts_in = ctx.enter_context(nc.semaphore("experts_in"))
        sb = lambda n, shape, dt=F32: ctx.enter_context(nc.sbuf_tensor(n, shape, dt))
        d = b.dram
        pair = pairs_of(b, sb)
        common_buffers(b, pair)
        heads_buffers(b, pair, SEQ)
        quarter = lambda a: [PT[:, a, :].rearrange("p (c n) -> p c n", c=2) for PT in b.PT]
        b.rc, b.rs = quarter(3), b.r
        b.t3, b.z3, b.a3, b.he = (quarter(a) for a in range(4))
        b.th = pair("th", [P, TILES * NE])
        b.raw = pair("raw", [P, TILES * NE])
        b.lg = pair("lg", [P, TILES, NE])
        b.m8 = pair("m8", [P, TILES, 8])
        b.i8 = pair("i8", [P, TILES, 8], U32)
        b.f8 = pair("f8", [P, TILES, 8])
        b.sel = pair("sel", [P, TILES, NE])
        b.gw = pair("gw", [P, TILES, NE])
        b.gT = pair("gT", [NE, SEQ])
        w3 = {n: sb("w3a_" + n, [P, DC, D]) for n in ("q", "q_rot", "k", "k_rot")}
        w3["v"] = sb("w3a_v", [P, DC, D])
        w3o = sb("w3o", [P, HC, D])
        b.rope_bias = {n: sb("rb_" + n, [P, DC]) for n in ("q", "q_rot", "k", "k_rot")}
        b.cos, b.sin = sb("cos", [P, SEQ]), sb("sin", [P, SEQ])
        b.v_bias, row_o = {"L3a": sb("v_bias", [P, D])}, sb("row_o3", [P, D])
        b.w1e, b.w3e = sb("w1e", [P, UNITS3, DC, FF3]), sb("w3e", [P, UNITS3, DC, FF3])
        b.w2e = sb("w2e", [P, UNITS3, D])
        b.b1e_half, b.b3e, b.b2e = sb("b1e", [P, UNITS3]), sb("b3e", [P, UNITS3]), sb("b2e", [NE, D])
        b.gate_w, b.expert_bias = sb("gate_w", [P, DC, NE]), sb("expert_bias", [P, NE])
        b.iota, b.sb2_twice = sb("iota", [P, NE]), sb("sb2", [1, 2 * D])
        b.w, b.wo = {"L3a": w3}, {"L3a": w3o}
        b.heads = {"L3a": Heads("L3a", [(0, P), (P, P)], DH, (1, 1, 1))}

        def begin(g, block):
            pairs = [(w3[n][:, :, :], chunked(d["w3" + n])) for n in w3]
            pairs += [(b.rope_bias[n][:, :], d["rb_" + n]) for n in b.rope_bias]
            pairs += [(w3o[:, :, :], chunked(d["w3o"])), (b.cos[:, :], d["cos"]), (b.sin[:, :], d["sin"]),
                      (b.v_bias["L3a"][:, :], d["row_v3"].partition_broadcast(P)),
                      (row_o[:, :], d["row_o3"].partition_broadcast(P)),
                      (b.b1e_half[:, :], d["b1e"]), (b.b3e[:, :], d["b3e"]), (b.b2e[:, :], d["b2e"]),
                      (b.gate_w[:, :, :], chunked(d["gate_w"])),
                      (b.expert_bias[:, :], d["expert_bias"].partition_broadcast(P)),
                      (b.iota[:, :], d["iota"].partition_broadcast(P)),
                      (b.sb2_twice[:, :], d["sb2"])]
            rest, total = load(block, g, pairs)

            @block.scalar
            def _(act):
                for dst, src in rest:
                    act.dma_start(dst, src).then_inc(g("loaded"), 16)
                for dst, src in ((b.w1e[:, :, :, :], d["w1e"].rearrange("e (c p) f -> p e c f", p=P)),
                                 (b.w3e[:, :, :, :], d["w3e"].rearrange("e (c p) f -> p e c f", p=P)),
                                 (b.w2e[:, :, :], d["w2e"].rearrange("e p n -> p e n"))):
                    act.dma_start(dst, src).then_inc(b.experts_in, 16)

            @block.gpsimd
            def _(pool):
                clear_spares(pool, b)

            @block.vector
            def _(dve):
                dve.wait_ge(g("loaded"), total)
                dve.tensor_scalar(b.b1e_half[:, :], b.b1e_half[:, :], 0.5, None, ALU.mult)

        region(nc, begin)

        def turn(i):
            def body(g, block):
                @block.sync
                def _(sp):
                    for s in range(SB):
                        load_context(sp, g, b, i, s)
                    for s in range(SB):
                        sp.wait_ge(g("L3f_x", s), TILES)
                        sp.dma_start(out.rearrange("(i s) (t p) n -> i s p t n", s=SB, p=P)[i, s],
                                     b.x[s][:, :, :]).then_inc(g("stored", s), 16)
                    for s in range(SB):
                        sp.wait_ge(g("stored", s), 16)

                @block.gpsimd
                def _(pool):
                    link = Chain(pool, g("pool_chain"))
                    for L in ("L3a", "L3x", "L3f"):
                        for s in range(SB):
                            if L in b.heads:
                                split_k(pool, link, g, b, s, b.heads[L])
                        for s in range(SB):
                            norm_pool(pool, g, b, s, L)

                def pe_program(pe, s):
                    norm_pe(pe, g, b, s, "in", 3)
                    yield
                    yield from rotary_pe(pe, g, b, s, "in")
                    norm_pe(pe, g, b, s, "L3a", 3)
                    yield
                    yield from wide_pe(pe, g, b, s, "L3a")
                    norm_pe(pe, g, b, s, "L3x", 3)
                    yield
                    yield from experts_pe(pe, g, b, s, "L3x")

                @block.tensor
                def _(pe):
                    pe.wait_ge(g("ctx", 0), 32)
                    pe.wait_ge(g("ctx", 1), 32)
                    side_by_side([pe_program(pe, s) for s in range(SB)])

                def act_program(act, s):
                    norm_act(act, g, b, s, "in", 3)
                    yield
                    for _ in range(6):
                        yield
                    yield from heads_act(act, g, b, s, b.heads["L3a"])
                    norm_act(act, g, b, s, "L3a", 3)
                    yield
                    yield from wide_act(act, g, b, s)
                    norm_act(act, g, b, s, "L3x", 3)
                    yield
                    yield from experts_act(act, g, b, s)

                @block.scalar
                def _(act):
                    side_by_side([act_program(act, s) for s in range(SB)])

                def dve_program(dve, link, s):
                    take_in(dve, g, b, s, i)
                    yield
                    yield from rotary_dve(dve, link, g, b, s)
                    norm_dve(dve, link, g, b, s, "L3a", 1, row_o[:, :])
                    yield
                    yield from wide_dve(dve, link, g, b, s)
                    norm_dve(dve, link, g, b, s, "L3x", 1)
                    yield
                    yield from experts_dve(dve, link, g, b, s)
                    norm_dve(dve, link, g, b, s, "L3f", 0)
                    yield

                @block.vector
                def _(dve):
                    link = Chain(dve, g("dve_chain"))
                    side_by_side([dve_program(dve, link, s) for s in range(SB)])

            return body

        with nc.Fori(0, NB // SB) as i:
            region(nc, turn(i))


def program(nc, dram, out, phases=5):
    with ExitStack() as ctx:
        b = Buffers()
        b.dram = dram
        sb = lambda n, shape, dt=F32: ctx.enter_context(nc.sbuf_tensor(n, shape, dt))
        b.x_all = sb("x_all", [P, NB * TILES, D])
        b.ident, b.identb, b.ones = sb("ident", [P, P]), sb("identb", [P, P], BF16), sb("ones", [P, P])
        b.minus_half = sb("minus_half", [P, TILES])
        b.sel_q = sb("sel_q", [P, PARTS, P // DH, P], BF16)
        b.sel_k = sb("sel_k", [P, PARTS, P // DH, P], BF16)
        b.one16, b.onehot = sb("one16", [PARTS * NH, NH]), sb("onehot", [PARTS * NH, NH, P], BF16)
        b.pst = ctx.enter_context(nc.psum_tensor("banks", [P, 8, 512], F32))
        b.ps = [b.pst[:, 4 * s:4 * s + 4, :] for s in range(SB)]
        phase_state(nc, b)
        if phases > 1:
            phase_first(nc, b)
        if phases > 2:
            phase_quantised(nc, b)
        if phases > 3:
            phase_second(nc, b)
        if phases > 4:
            phase_third(nc, b, out)
        else:
            def show(g, block):
                @block.sync
                def _(sp):
                    sp.dma_start(out.rearrange("b (t p) n -> p (b t) n", p=P), b.x_all[:, :, :]).then_inc(g("shown"), 16)
                    sp.wait_ge(g("shown"), 16)
            region(nc, show)


def laid_out(a):
    f = np.float32
    rows = lambda v: v.reshape(1, -1)

    def slots(w):
        w = w.reshape(NH, DH, -1)
        return np.concatenate([w, np.zeros((NH, SLOT - DH, w.shape[2]), f)], 1).reshape(NH * SLOT, -1)

    def columns(v):
        return v.reshape(-1, P).T

    def half_swapped(w):
        w = w.reshape(*w.shape[:-1], NH, 2, DH // 2)
        return w[..., ::-1, :].reshape(*w.shape[:-3], NH * DH)

    p = np.arange(P)
    same = (p[:, None] // BLK == p[None, :] // BLK)
    spread = np.stack([same & (p[:, None] % BLK == i) for i in range(BLK)], 1).astype(f)
    collect = np.stack([same & (p[None, :] % BLK == i) for i in range(BLK)], 1).astype(f)
    causal = np.where(p[None, :] <= p[:, None], 0.0, NEG).astype(f)
    inv_freq = (f(1.0) / f(10000.0) ** (np.arange(0, DH, 2, dtype=f) / f(DH))).astype(f)
    angle = np.arange(SEQ, dtype=f)[:, None] * inv_freq[None, :]
    cos = np.concatenate([np.cos(angle), np.cos(angle)], 1).T
    sin = np.concatenate([-np.sin(angle), np.sin(angle)], 1).T
    x, ctx = a["x"], a["ctx_1024"]
    mask = a["mask_Bx16xSxS2_bk1"]
    smask = a["mask_SxS2_bk0"]
    w3, b3 = a["L3_attn_W_qkv"].reshape(D, 3, D), a["L3_attn_b_qkv"].reshape(3, D)
    sw = lambda n: a[f"L3_ffn_s{n}"].reshape(2, FF3, D)
    return {
        "x": x.reshape(TOKENS, D), "xT": x.reshape(TOKENS, D).T, "ctx": ctx, "ctxT": ctx.transpose(0, 2, 1),
        "mask": mask.transpose(0, 2, 1, 3), "maskT": mask.transpose(0, 3, 1, 2), "smask": smask, "smaskT": smask.T,
        "w0k": a["L0_attn_W_k"].T, "w0v": a["L0_attn_W_v"].T, "w0q": a["L0_attn_W_q"].T,
        "same_block": same.astype(f), "spread": spread, "collect": collect, "ident": np.eye(P, dtype=f),
        "causal": causal, "causalT": causal.T,
        "wsim": columns(a["L0_xattn_w_sim"]), "b_sim": rows(a["L0_xattn_b_sim"]), "wqv": a["L0_xattn_W_qv"],
        "row_qv": rows(a["L0_xattn_b_qv"]), "w0f": a["L0_ffn_W"].T, "row_f0": rows(a["L0_ffn_b"]),
        "ld": a["L0_ffn_lora_down"].T, "da": a["L0_ffn_down_aux"], "lu": a["L0_ffn_lora_up"].T,
        "ua": a["L0_ffn_up_aux"].T,
        "w1a": a["L1_attn_W_qkv"], "w1o": a["L1_attn_W_out"].T, "row_o1": rows(a["L1_attn_b_out"]),
        "w1xq": a["L1_xattn_Wq"], "w1xk": a["L1_xattn_Wk"], "w1xv": a["L1_xattn_Wv"],
        "w1xo": slots(a["L1_xattn_Wo"]), "b1xq": columns(a["L1_xattn_bq"]),
        "b1xk": columns(a["L1_xattn_bk"]), "row_v1": rows(a["L1_xattn_bv"]),
        "row_x1": rows(a["L1_xattn_bo"]),
        "w_up": a["L1_ffn_w_up"], "w_gate": a["L1_ffn_w_gate"], "w_down": a["L1_ffn_w_down"],
        "w2aq": a["L2_attn_Wq"], "w2ak": a["L2_attn_Wk"], "w2av": a["L2_attn_Wv"],
        "w2ao": a["L2_attn_Wo"], "w2xq": a["L2_xattn_Wq"].T, "w2xk": a["L2_xattn_Wk"].T,
        "w2xv": a["L2_xattn_Wv"].T, "w2xo": slots(a["L2_xattn_Wo"].T), "w2f1": a["L2_ffn_W1"].T,
        "w2f2": a["L2_ffn_W2"].T, "b2f1": columns(a["L2_ffn_b1"]), "row_b2": rows(a["L2_ffn_b2"]),
        "w3q": w3[:, 0], "w3k": w3[:, 1], "w3v": w3[:, 2], "w3q_rot": half_swapped(w3[:, 0]),
        "w3k_rot": half_swapped(w3[:, 1]), "rb_q": columns(b3[0]), "rb_k": columns(b3[1]),
        "rb_q_rot": columns(half_swapped(b3[0])), "rb_k_rot": columns(half_swapped(b3[1])),
        "row_v3": rows(b3[2]), "w3o": slots(a["L3_attn_W_out"]), "row_o3": rows(a["L3_attn_b_out"]),
        "cos": np.tile(cos, (P // DH, 1)), "sin": np.tile(sin, (P // DH, 1)),
        "gate_w": a["L3_ffn_gate_w"].T, "expert_bias": rows(a["L3_ffn_expert_bias"]),
        "w1e": np.concatenate([a["L3_ffn_w1"], sw("w1")]).transpose(0, 2, 1),
        "w3e": np.concatenate([a["L3_ffn_w3"], sw("w3")]).transpose(0, 2, 1),
        "w2e": np.concatenate([a["L3_ffn_w2"], a["L3_ffn_sw2"].reshape(D, 2, FF3).transpose(1, 0, 2)])
                 .transpose(0, 2, 1),
        "b1e": np.concatenate([a["L3_ffn_b1"], a["L3_ffn_sb1"].reshape(2, FF3)]).T,
        "b3e": np.concatenate([a["L3_ffn_b3"], a["L3_ffn_sb3"].reshape(2, FF3)]).T,
        "b2e": a["L3_ffn_b2"], "sb2": rows(np.tile(a["L3_ffn_sb2"], 2)),
        "iota": rows(np.arange(NE, dtype=f)),
    }


def kernel(**inputs):
    import concourse.bacc as bacc
    from concourse.bass_utils import run_bass_kernel_spmd

    nc = bacc.Bacc("TRN2", target_bir_lowering=False, num_devices=1)
    arrays, dram = {}, {}
    for name, a in laid_out({k: np.asarray(v) for k, v in inputs.items()}).items():
        a = np.ascontiguousarray(a)
        arrays["in_" + name] = a
        dram[name] = nc.dram_tensor("in_" + name, a.shape, mybir.dt.from_np(a.dtype), kind="ExternalInput").ap()
    out = nc.dram_tensor("out_x", (NB, SEQ, D), F32, kind="ExternalOutput").ap()
    program(nc, dram, out)
    r = run_bass_kernel_spmd(nc, [arrays], core_ids=[0])
    return r.results[0]["out_x"]
```

```python
from contextlib import ExitStack

import numpy as np

import concourse.bass as bass
from concourse import mybir

ALU = mybir.AluOpType
ACT = mybir.ActivationFunctionType
F32 = mybir.dt.float32
BF16 = mybir.dt.bfloat16
U8 = mybir.dt.uint8
U32 = mybir.dt.uint32
X = mybir.AxisListType.X
XY = mybir.AxisListType.XY

P = 128
NB, SEQ, D = 8, 256, 256
SK = 120
TILES = SEQ // P
DC = D // P
NH, DH = 16, 16
HC = 4
SLOT = 32
PARTS = 3
PRODUCTS = P // DH
EPS = 1e-5
NEG = -1.0e30
BLK = 8
TOKENS = NB * SEQ
FF1, FF2, FF3, NE = 768, 1024, 128, 16
ROUND = 12582912.0
QMAX = 32767.0
SB = 2
DV2 = 64


class Signals:

    def __init__(self, nc, ctx):
        self.nc, self.ctx, self.by_name = nc, ctx, {}

    def __call__(self, name, s=""):
        key = f"{name}_{s}" if s != "" else name
        if key not in self.by_name:
            self.by_name[key] = self.ctx.enter_context(self.nc.semaphore(key))
        return self.by_name[key]

    def runs(self):
        nums, found = sorted(h.num for h in self.by_name.values()), []
        for n in nums:
            if found and found[-1].stop == n:
                found[-1] = range(found[-1].start, n + 1)
            else:
                found.append(range(n, n + 1))
        return found


class Chain:

    def __init__(self, eng, sem):
        self.eng, self.sem, self.n = eng, sem, 0

    def __call__(self, *instructions):
        for ins in instructions:
            self.n += 1
            ins.then_inc(self.sem, 1)
        self.eng.wait_ge(self.sem, self.n)


def side_by_side(programs):
    live = list(programs)
    while live:
        for p in list(live):
            if next(p, "end") == "end":
                live.remove(p)


def norm_pe(pe, g, b, s, L, bank):
    pe.wait_ge(g(L + "_x", s), TILES)
    for t in range(TILES):
        for c in range(DC):
            last = pe.transpose(b.ps[s][:, bank, c * SEQ + t * P:c * SEQ + (t + 1) * P],
                                b.x[s][:, t, c * P:(c + 1) * P], b.ident[:, :])
    last.then_inc(g(L + "_xt", s), 1)


def norm_act(act, g, b, s, L, bank):
    act.wait_ge(g(L + "_xt", s), 1)
    act.activation(b.xT[s][:, :, :].rearrange("p c n -> p (c n)"), b.ps[s][:, bank, :], ACT.Copy)\
       .then_inc(g(L + "_xT", s), 1)


def add_bias(dve, link, b, s, bias):
    link(dve.tensor_tensor(b.r[s][:, :, :], b.x[s][:, :, :], bias.unsqueeze(1).to_broadcast([P, TILES, D]), ALU.add))


def norm_dve(dve, link, g, b, s, L, bank, biased=False, half=False, valid=None):
    r, x, st, mv, rstd = b.r[s], b.x[s], b.st[s], b.mv[s], b.rstd[s]
    out = b.ps[s][:, bank, :].rearrange("p (t n) -> p t n", t=TILES)
    dve.wait_ge(g(L + "_out", s), 1)
    if biased:
        link(dve.tensor_tensor(r[:, :, :], out, r[:, :, :], ALU.add))
    elif valid is not None:
        link(*[dve.scalar_tensor_tensor(r[:, t, :], out[:, t, :], valid[:, t:t + 1], x[:, t, :], ALU.mult, ALU.add)
               for t in range(TILES)])
    elif half:
        link(dve.scalar_tensor_tensor(r[:, :, :], out, 0.5, x[:, :, :], ALU.mult, ALU.add))
    else:
        link(dve.tensor_tensor(r[:, :, :], out, x[:, :, :], ALU.add))
    link(*[dve.bn_stats(st[:, t, :], r[:, t, :]) for t in range(TILES)])
    link(*[dve.bn_aggr(mv[:, t, :], st[:, t, :]) for t in range(TILES)])
    dve.tensor_scalar(mv[:, :, 1], mv[:, :, 1], EPS, None, ALU.add).then_inc(g(L + "_var", s), 1)
    dve.wait_ge(g(L + "_rstd", s), 1)
    for t in range(TILES):
        dve.tensor_scalar(x[:, t, :], r[:, t, :], mv[:, t, 0:1], rstd[:, t:t + 1],
                          ALU.subtract, ALU.mult).then_inc(g(L + "_x", s), 1)


def norm_pool(pool, g, b, s, L):
    pool.wait_ge(g(L + "_var", s), 1)
    pool.tensor_tensor(b.rstd[s][:, :], b.mv[s][:, :, 1], b.minus_half[:, :], ALU.pow)\
        .then_inc(g(L + "_rstd", s), 1)


class Heads:

    def __init__(self, L, keys, dv, parts, mask=None, ob=1):
        self.L, self.keys, self.dv, self.mask, self.ob = L, keys, dv, mask, ob
        self.parts = parts
        self.scale = DH ** -0.5
        self.per = 2 if len(keys) == 1 else 1
        self.units = HC // self.per
        self.chunks = [range(u * self.per, (u + 1) * self.per) for u in range(self.units)]
        self.k_first = len(keys) == 1
        self.slot = max(32, dv)
        self.fit = P // self.slot
        self.outs = 4 * self.per // self.fit
        self.nk = sum(ks for _, ks in keys)
        self.maxes = 1 if len(keys) == 2 and mask is None else TILES

    def sees(self, t, k):
        return self.mask != "causal" or k <= t


def split(eng, link, src, parts, rest, done):
    link(eng.tensor_copy(parts[0], src))
    link(eng.tensor_tensor(rest, src, parts[0], ALU.subtract))
    link(eng.tensor_copy(parts[1], rest))
    eng.tensor_tensor(parts[2], rest, parts[1], ALU.subtract).then_inc(done, 1)


def split_q(dve, link, g, b, s, h):
    dve.wait_ge(g(h.L + "_q", s), h.parts[0])
    split(dve, link, b.qT[s][:, :, :], [b.qp[s][:, p, :, :] for p in range(PARTS)], b.r[s][:, :, :],
          g(h.L + "_qp", s))


def split_k(pool, link, g, b, s, h):
    pool.wait_ge(g(h.L + "_k", s), h.parts[1])
    split(pool, link, b.kT[s][:, :, 0:h.nk], [b.kp[s][:, p, :, 0:h.nk] for p in range(PARTS)],
          b.kr[s][:, :, 0:h.nk], g(h.L + "_kp", s))


def stack_round(b, s, h, r):
    of_q = (r < 4) != h.k_first
    n = SEQ if of_q else h.nk
    dst = (b.qs if of_q else b.ks)[s][:, :, 2 * (r % 4):2 * (r % 4) + 2, 0:n].rearrange("p c h n -> p h c n")
    bank = 2 * (r % 2)
    return of_q, dst, b.ps[s][:, bank:bank + 2, 0:DC * n].rearrange("p h (c n) -> p h c n", c=DC)


def stack_pe(pe, g, b, s, h):
    L, ps = h.L, b.ps[s]
    pe.wait_ge(g(L + "_q", s), h.parts[0])
    pe.wait_ge(g(L + "_k", s), h.parts[1])
    pe.wait_ge(g(L + "_v", s), h.parts[2])
    for r in range(8):
        of_q = (r < 4) != h.k_first
        sel, parts, n = (b.sel_q, b.qp[s], SEQ) if of_q else (b.sel_k, b.kp[s], h.nk)
        if r % 4 == 0:
            if of_q:
                pe.wait_ge(g(L + "_qp", s), 1)
            else:
                pe.wait_ge(g(L + "_kp", s), 1)
        if r >= 2:
            if r % 2 == 0:
                pe.wait_ge(g(L + "_placed_even", s), r // 2)
            else:
                pe.wait_ge(g(L + "_placed_odd", s), r // 2)
        for i in range(2):
            for p in range(PARTS):
                last = pe.matmul(ps[:, 2 * (r % 2) + i, 0:DC * n], lhsT=sel[:, p, 2 * (r % 4) + i, :],
                                 rhs=parts[:, p, :, 0:n], start=(p == 0), stop=(p == PARTS - 1),
                                 skip_group_check=True)
        last.then_inc(g(L + "_place", s), 1)
        if r % 2 == 1:
            yield


def stack_act(act, g, b, s, h):
    for r in range(0, 8, 2):
        act.wait_ge(g(h.L + "_place", s), r + 1)
        _, dst, src = stack_round(b, s, h, r)
        act.activation(dst, src, ACT.Copy).then_inc(g(h.L + "_placed_even", s), 1)
        yield


def stack_dve(dve, g, b, s, h):
    for r in range(1, 8, 2):
        dve.wait_ge(g(h.L + "_place", s), r + 1)
        _, dst, src = stack_round(b, s, h, r)
        dve.tensor_copy(dst, src).then_inc(g(h.L + "_placed_odd", s), 1)
        yield


def masked(h, b, s, pe, out, t, c, j, flipped):
    if h.mask == "causal":
        add = b.causalT[:, :] if flipped else b.causal[:, :]
    elif h.mask == "per_head":
        add = b.maskT[s][:, c * 4 + j, t * P:(t + 1) * P] if flipped else b.mask[s][:, t, c * 4 + j, :]
    else:
        add = b.smaskT[:, t * P:(t + 1) * P] if flipped else b.smask[:, t, :]
    n = add.shape[0]
    return pe.matmul(out, lhsT=b.identb[0:n, 0:n], rhs=add, start=False, stop=True, skip_group_check=True)


def heads_pe(pe, g, b, s, h):
    L, ps, v = h.L, b.ps[s], (b.vn if h.dv == DH else b.vw)[s]
    qs = b.qs[s][:, :, :, :].rearrange("p c h n -> p (c h) n")
    kst = b.ks[s][:, :, :, :].rearrange("p c h n -> p (c h) n")
    yield from stack_pe(pe, g, b, s, h)
    pe.wait_ge(g(L + "_placed_even", s), 4)
    pe.wait_ge(g(L + "_placed_odd", s), 4)
    if h.mask == "per_head":
        pe.wait_ge(g(L + "_mask", s), 2)
    for u, chunks in enumerate(h.chunks):
        if u >= 1:
            pe.wait_ge(g(L + "_mx", s), h.maxes * u)
        for n, c in enumerate(chunks):
            for t in range(TILES):
                col = (n * TILES + t) * P * len(h.keys)
                width = sum(ks for k, (o, ks) in enumerate(h.keys) if h.sees(t, k))
                for j in range(4):
                    last = pe.matmul(ps[:, j, col:col + width], lhsT=qs[:, 4 * c + j, t * P:(t + 1) * P],
                                     rhs=kst[:, 4 * c + j, 0:width], start=True, stop=True, skip_group_check=True)
                    if h.mask:
                        o = t * P if h.mask == "causal" else 0
                        ks = h.keys[0][1]
                        last = masked(h, b, s, pe, ps[:, j, col + o:col + o + ks], t, c, j, False)
        last.then_inc(g(L + "_s", s), 1)
        yield
    pe.wait_ge(g(L + "_mp", s), 1)
    for t in range(TILES):
        last = pe.matmul(ps[0:PARTS * NH, 0, t * P:(t + 1) * P], lhsT=b.mxp[s][:, t, :, :].rearrange("p a h -> p (a h)"),
                         rhs=b.identb[:, :], start=True, stop=True, skip_group_check=True)
    last.then_inc(g(L + "_mT", s), 1)
    yield
    pe.wait_ge(g(L + "_mxT", s), 1)
    for u, chunks in enumerate(h.chunks):
        for j in range(4):
            if u >= 1 and j == 4 - h.outs:
                pe.wait_ge(g(L + "_o", s), u)
            for n, c in enumerate(chunks):
                for k, (o, ks) in enumerate(h.keys):
                    col = (n + k) * SEQ
                    first = min(t for t in range(TILES) if h.sees(t, k)) * P
                    out = ps[0:ks, j, col + first:col + SEQ]
                    pe.matmul(out, lhsT=kst[:, 4 * c + j, o:o + ks], rhs=qs[:, 4 * c + j, first:SEQ],
                              start=True, stop=False, skip_group_check=True)
                    last = pe.matmul(out, lhsT=b.onehot[:, 4 * c + j, 0:ks], rhs=b.mxT[s][:, first:SEQ],
                                     start=False, stop=True, skip_group_check=True)
                    for t in range(TILES):
                        if h.mask and (h.mask != "causal" or t == k):
                            last = masked(h, b, s, pe, ps[0:ks, j, col + t * P:col + (t + 1) * P], t, c, j, True)
        last.then_inc(g(L + "_st", s), 1)
        yield
        pe.wait_ge(g(L + "_e", s), len(h.keys) * (u + 1))
        for m in range(h.outs):
            bank = 4 - h.outs + m
            heads = range((u * h.outs + m) * h.fit, (u * h.outs + m + 1) * h.fit)
            for sums in range(2):
                for k, (o, ks) in enumerate(h.keys):
                    first = min(t for t in range(TILES) if h.sees(t, k)) * P
                    for i, head in enumerate(heads):
                        n, j = (head // 4) % h.per, head % 4
                        weights = b.ones[0:ks, 0:h.slot] if sums else v[0:ks, k, head * h.slot:(head + 1) * h.slot]
                        last = pe.matmul(ps[i * h.slot:(i + 1) * h.slot, bank, sums * SEQ + first:(sums + 1) * SEQ],
                                         lhsT=weights, rhs=b.PT[s][0:ks, j, (n + k) * SEQ + first:(n + k + 1) * SEQ],
                                         start=(k == 0), stop=(k == len(h.keys) - 1), skip_group_check=True)
        last.then_inc(g(L + "_pv", s), 1)
        yield
    pe.wait_ge(g(L + "_o", s), h.units)
    nC = NH // h.fit
    for t in range(TILES):
        for c in range(nC):
            last = pe.matmul(ps[:, h.ob, t * D:(t + 1) * D], lhsT=b.oT[s][:, c, t * P:(t + 1) * P],
                             rhs=b.wo[L][:, c, :], start=(c == 0), stop=(c == nC - 1), skip_group_check=True)
    last.then_inc(g(L + "_out", s), 1)
    yield


def heads_act(act, g, b, s, h):
    L, ps = h.L, b.ps[s]
    yield from stack_act(act, g, b, s, h)
    for u in range(h.units):
        act.wait_ge(g(L + "_st", s), u + 1)
        if u >= 1:
            act.wait_ge(g(L + "_pv", s), u)
        if len(h.keys) == 1:
            ks = h.keys[0][1]
            act.activation(b.PT[s][0:ks, :, :], ps[0:ks, :, :], ACT.Exp, scale=h.scale).then_inc(g(L + "_e", s), 1)
        else:
            for k in range(2):
                lo = k * SEQ + min(t for t in range(TILES) if h.sees(t, k)) * P
                act.activation(b.PT[s][:, :, lo:(k + 1) * SEQ], ps[:, :, lo:(k + 1) * SEQ], ACT.Exp,
                               scale=h.scale).then_inc(g(L + "_e", s), 1)
        yield


def heads_dve(dve, link, g, b, s, h, floor=None):
    L, ps, w = h.L, b.ps[s], h.dv + 1
    mx = b.mx[s]
    yield from stack_dve(dve, g, b, s, h)
    for u, chunks in enumerate(h.chunks):
        dve.wait_ge(g(L + "_s", s), u + 1)
        heads = slice(4 * chunks.start, 4 * chunks.stop)
        for t in range(h.maxes):
            width = sum(ks for k, (o, ks) in enumerate(h.keys) if h.sees(t, k))
            if h.maxes == 1:
                src = ps[:, :, :].rearrange("p j (t k) -> p j t k", t=TILES)
                dst = mx[:, :, heads].rearrange("p t j -> p j t")
            elif h.per == 2:
                src = ps[:, :, :].rearrange("p j (c t k) -> p t c j k", c=2, t=TILES)[:, t, :, :, 0:width]
                dst = mx[:, t, heads].rearrange("p (c j) -> p c j", c=2)
            else:
                src = ps[:, :, t * SEQ:t * SEQ + width]
                dst = mx[:, t, heads]
            dve.tensor_reduce(dst, src, X, ALU.max, negate=True).then_inc(g(L + "_mx", s), 1)
        yield
    dve.wait_ge(g(L + "_mx", s), h.maxes * h.units)
    split(dve, link, mx[:, :, :], [b.mxp[s][:, :, p, :] for p in range(PARTS)], b.mxr[s][:, :, :], g(L + "_mp", s))
    yield
    dve.wait_ge(g(L + "_mT", s), 1)
    dve.tensor_copy(b.mxT[s][:, :], ps[0:PARTS * NH, 0, 0:SEQ]).then_inc(g(L + "_mxT", s), 1)
    yield
    for u in range(h.units):
        dve.wait_ge(g(L + "_pv", s), u + 1)
        banks = ps[:, 4 - h.outs:4, :]
        values, sums, ri = banks[:, :, 0:SEQ], banks[:, :, SEQ:2 * SEQ], b.r[s][:, 0:h.outs, :]
        if floor:
            link(dve.tensor_scalar(ri, sums, floor, None, ALU.max))
            sums = ri
        link(dve.reciprocal(ri, sums))
        dve.tensor_tensor(b.oT[s][:, u * h.outs:(u + 1) * h.outs, :], values, ri, ALU.mult)\
           .then_inc(g(L + "_o", s), 1)
        dve.wait_ge(g(L + "_o", s), u + 1)
        yield


CROSS_BANKS = {"L1x": {"k": 3, "v": 1, "q": 0}, "L2x": {"k": 2, "v": 0, "q": 1}}


def context_pe(pe, g, b, s, L):
    ps, w, bank = b.ps[s], b.w[L], CROSS_BANKS[L]
    pe.wait_ge(g("ctx", s), 32)
    for c in range(DC):
        for i in range(DC):
            last = pe.matmul(ps[:, bank["k"], c * P:c * P + SK], lhsT=w["k"][:, i, c * P:(c + 1) * P],
                             rhs=b.ctxT[s][:, i, :], start=(i == 0), stop=(i == DC - 1), skip_group_check=True)
    last.then_inc(g(L + "_pk", s), 1)
    for i in range(DC):
        last = pe.matmul(ps[0:SK, bank["v"], 0:D], lhsT=b.ctxT[s][:, i, :], rhs=w["v"][:, i, :],
                         start=(i == 0), stop=(i == DC - 1), skip_group_check=True)
    last.then_inc(g(L + "_pvv", s), 1)
    yield


def cross_pe(pe, g, b, s, L, prev):
    pe.wait_ge(g(prev + "_xT", s), 1)
    for c in range(DC):
        last = project_T(pe, b.ps[s][:, CROSS_BANKS[L]["q"], c * SEQ:(c + 1) * SEQ], b.w[L]["q"], c, b.xT[s])
    last.then_inc(g(L + "_pq", s), 1)
    yield


def with_bias(act, dst, src, bias, n, done):
    for c in range(DC):
        kw = {"bias": bias[:, c:c + 1]} if bias is not None else {}
        act.activation(dst[:, c, 0:n], src(c), ACT.Identity, **kw).then_inc(done, 1)


def context_act(act, g, b, s, L, k_bias=None):
    act.wait_ge(g(L + "_pk", s), 1)
    with_bias(act, b.kT[s], lambda c: b.ps[s][:, CROSS_BANKS[L]["k"], c * P:c * P + SK], k_bias, SK, g(L + "_k", s))
    yield


def cross_act(act, g, b, s, L, q_bias=None):
    act.wait_ge(g(L + "_pq", s), 1)
    with_bias(act, b.qT[s], lambda c: b.ps[s][:, CROSS_BANKS[L]["q"], c * SEQ:(c + 1) * SEQ], q_bias, SEQ,
              g(L + "_q", s))
    yield


def cross_dve(dve, link, g, b, s, L, v_bias=None):
    dve.wait_ge(g(L + "_pvv", s), 1)
    dst = b.vn[s][0:SK, 0, :].rearrange("p (h w) -> p h w", w=SLOT)[:, :, 0:DH]
    src = b.ps[s][0:SK, CROSS_BANKS[L]["v"], 0:D].rearrange("p (h w) -> p h w", w=DH)
    if v_bias is not None:
        ins = dve.tensor_tensor(dst, src, v_bias[0:SK, :].rearrange("p (h w) -> p h w", w=DH), ALU.add)
    else:
        ins = dve.tensor_copy(dst, src)
    ins.then_inc(g(L + "_v", s), 1)
    yield
    split_q(dve, link, g, b, s, b.heads[L])
    yield


def project_T(pe, out, w, c, xT):
    for i in range(DC):
        last = pe.matmul(out, lhsT=w[:, i, c * P:(c + 1) * P], rhs=xT[:, i, :],
                         start=(i == 0), stop=(i == DC - 1), skip_group_check=True)
    return last


def project(pe, ps, bank, xT, w, n=D):
    for t in range(TILES):
        for i in range(DC):
            last = pe.matmul(ps[:, bank, t * n:(t + 1) * n], lhsT=xT[:, i, t * P:(t + 1) * P],
                             rhs=w[:, i, :], start=(i == 0), stop=(i == DC - 1), skip_group_check=True)
    return last


def causal_pe(pe, g, b, s, prev):
    ps, w, xT = b.ps[s], b.w["L2a"], b.xT[s]
    pe.wait_ge(g(prev + "_xT", s), 1)
    for n, name in enumerate("qk"):
        for c in range(DC):
            last = project_T(pe, ps[:, n, c * SEQ:(c + 1) * SEQ], w[name], c, xT)
        last.then_inc(g("L2a_p" + name, s), 1)
    for t in range(TILES):
        if t == 1:
            pe.wait_ge(g("L2a_q", s), 1)
            pe.wait_ge(g("L2a_k", s), 1)
        for half in range(2):
            for i in range(DC):
                last = pe.matmul(ps[:, 2 - 2 * t + half, :], lhsT=xT[:, i, t * P:(t + 1) * P],
                                 rhs=w["v"][:, i, half * 512:(half + 1) * 512],
                                 start=(i == 0), stop=(i == DC - 1), skip_group_check=True)
        last.then_inc(g("L2a_pvv", s), 1)
        yield
    yield from heads_pe(pe, g, b, s, b.heads["L2a"])


def causal_act(act, g, b, s):
    for n, (name, dst) in enumerate((("q", b.qT[s]), ("k", b.kT[s]))):
        act.wait_ge(g("L2a_p" + name, s), 1)
        act.activation(dst[:, :, :].rearrange("p c n -> p (c n)"), b.ps[s][:, n, :], ACT.Copy)\
           .then_inc(g("L2a_" + name, s), 1)
    yield
    yield from heads_act(act, g, b, s, b.heads["L2a"])


def causal_dve(dve, link, g, b, s):
    for t in range(TILES):
        dve.wait_ge(g("L2a_pvv", s), t + 1)
        dve.tensor_copy(b.vw[s][:, t, :].rearrange("p (h w) -> p h w", w=DV2)[:, :, 0:DV2],
                        b.ps[s][:, 2 - 2 * t:4 - 2 * t, :].rearrange("p a (h w) -> p (a h) w", w=DV2))\
           .then_inc(g("L2a_v", s), 1)
        if t == 0:
            split_q(dve, link, g, b, s, b.heads["L2a"])
    yield
    yield from heads_dve(dve, link, g, b, s, b.heads["L2a"])


ROPE_BANK = {"k": 0, "q": 2}


def rotary_pe(pe, g, b, s, prev):
    ps, w, xT = b.ps[s], b.w["L3a"], b.xT[s]
    pe.wait_ge(g(prev + "_xT", s), 1)
    for name in ("k", "q"):
        for rot in range(2):
            for c in range(DC):
                last = project_T(pe, ps[:, ROPE_BANK[name] + rot, c * SEQ:(c + 1) * SEQ],
                                 w[name + ("_rot" if rot else "")], c, xT)
        last.then_inc(g("L3a_p" + name, s), 1)
        yield
    pe.wait_ge(g("L3a_k", s), 1)
    project(pe, ps, 0, xT, w["v"]).then_inc(g("L3a_pvv", s), 1)
    yield
    yield from heads_pe(pe, g, b, s, b.heads["L3a"])


def rotary_dve(dve, link, g, b, s):
    ps = b.ps[s]
    for name, dst in (("k", b.kT[s]), ("q", b.qT[s])):
        dve.wait_ge(g("L3a_p" + name, s), 1)
        bank = ROPE_BANK[name]
        for c in range(DC):
            x_cos = dve.scalar_tensor_tensor(b.rc[s][:, c, :], ps[:, bank, c * SEQ:(c + 1) * SEQ],
                                             b.rope_bias[name][:, c:c + 1], b.cos[:, :], ALU.add, ALU.mult)
            rot_sin = dve.scalar_tensor_tensor(b.rs[s][:, c, :], ps[:, bank + 1, c * SEQ:(c + 1) * SEQ],
                                               b.rope_bias[name + "_rot"][:, c:c + 1], b.sin[:, :], ALU.add, ALU.mult)
            link(x_cos, rot_sin)
        dve.tensor_tensor(dst[:, :, :], b.rc[s][:, :, :], b.rs[s][:, :, :], ALU.add)\
           .then_inc(g("L3a_" + name, s), 1)
        yield
    split_q(dve, link, g, b, s, b.heads["L3a"])
    dve.wait_ge(g("L3a_pvv", s), 1)
    dve.tensor_tensor(b.vn[s][:, :, :].rearrange("p t (h w) -> p t h w", w=SLOT)[:, :, :, 0:DH],
                      ps[:, 0, :].rearrange("p (t h w) -> p t h w", t=TILES, w=DH),
                      b.v_bias["L3a"][:, :].rearrange("p (h w) -> p h w", w=DH).unsqueeze(1)
                       .to_broadcast([P, TILES, NH, DH]), ALU.add).then_inc(g("L3a_v", s), 1)
    yield
    yield from heads_dve(dve, link, g, b, s, b.heads["L3a"])


def flow_pe(pe, g, b, s, prev):
    ps, xT, x = b.ps[s], b.xT[s], b.x[s]
    pe.wait_ge(g(prev + "_xT", s), 1)
    pe.wait_ge(g("ctx", s), 32)
    pe.wait_ge(g("L0x_m", s), DC)
    for t in range(TILES):
        out = ps[:, 2, t * P:t * P + SK]
        for i in range(DC):
            pe.matmul(out, lhsT=xT[:, i, t * P:(t + 1) * P], rhs=b.flow_m[s][:, i, :],
                      start=(i == 0), stop=False, skip_group_check=True)
        for i in range(DC):
            last = pe.matmul(out, lhsT=b.w2_wide[:, i, :], rhs=b.ctxT[s][:, i, :],
                             start=False, stop=(i == DC - 1), skip_group_check=True)
    last.then_inc(g("L0x_sim", s), 1)
    yield
    pe.wait_ge(g("L0x_A", s), 1)
    for t in range(TILES):
        pe.transpose(ps[0:SK, 3, t * P:(t + 1) * P], b.A[s][:, t, :], b.ident[:, :])
    for t in range(TILES):
        last = pe.transpose(ps[0:1, 1, t * P:(t + 1) * P], b.nm[s][:, t:t + 1], b.ident[:, :])
    last.then_inc(g("L0x_At", s), 1)
    yield
    pe.wait_ge(g("L0x_nM", s), 1)
    pe.matmul(ps[:, 2, 2 * P:2 * P + 1], lhsT=b.ones[0:1, :], rhs=b.nM[s][0:1, 0:1], start=True, stop=True,
              skip_group_check=True).then_inc(g("L0x_nMb", s), 1)
    pe.wait_ge(g("L0x_AT", s), 1)
    for i in range(DC):
        pe.matmul(ps[:, 1, i * SEQ:(i + 1) * SEQ], lhsT=b.ctx[s][:, i * P:(i + 1) * P], rhs=b.AT[s][:, :],
                  start=True, stop=True, skip_group_check=True)
    pe.wait_ge(g("L0x_e", s), 1)
    for t in range(TILES):
        pe.matmul(ps[:, 2, 2 * P + 8:2 * P + 9], lhsT=b.ones[:, :], rhs=b.ecol[s][:, t:t + 1],
                  start=(t == 0), stop=(t == TILES - 1), skip_group_check=True)
    for i in range(DC):
        for t in range(TILES):
            last = pe.matmul(ps[:, 2, 2 * P + 16 + i:2 * P + 17 + i], lhsT=x[:, t, i * P:(i + 1) * P],
                             rhs=b.ecol[s][:, t:t + 1], start=(t == 0), stop=(t == TILES - 1),
                             skip_group_check=True)
    last.then_inc(g("L0x_hq", s), 1)
    yield
    pe.wait_ge(g("L0x_f", s), 2)
    pe.wait_ge(g("L0x_hqT", s), 1)
    for t in range(TILES):
        for f, feat in enumerate((xT, b.hqT[s], b.xhq[s], b.xhc[s])):
            for i in range(DC):
                last = pe.matmul(ps[:, 0, t * D:(t + 1) * D], lhsT=feat[:, i, t * P:(t + 1) * P],
                                 rhs=b.w["L0x"][:, 2 * f + i, :], start=(f + i == 0), stop=(f == 3 and i == 1),
                                 skip_group_check=True)
    last.then_inc(g("L0x_out", s), 1)
    yield


def flow_act(act, g, b, s):
    ps = b.ps[s]
    act.wait_ge(g("L0x_nm", s), 1)
    for t in range(TILES):
        act.activation(b.A[s][:, t, :], b.sim[s][:, t, :], ACT.Exp, bias=b.nm[s][:, t:t + 1],
                       accum_out=b.ssum[s][:, t:t + 1]).then_inc(g("L0x_exp", s), 1)
    yield
    act.wait_ge(g("L0x_At", s), 1)
    act.activation(b.AT[s][:, :], ps[0:SK, 3, 0:SEQ], ACT.Copy).then_inc(g("L0x_AT", s), 1)
    yield
    act.wait_ge(g("L0x_nMs", s), 1)
    act.activation(b.ecol[s][:, :], b.nm[s][:, :], ACT.Exp, scale=-1.0, bias=b.nMb[s][:, 0:1])\
       .then_inc(g("L0x_e", s), 1)
    act.wait_ge(g("L0x_hq", s), 1)
    act.activation(b.hqT[s][:, :, :].rearrange("p c n -> p (c n)"), ps[:, 1, :], ACT.Copy)\
       .then_inc(g("L0x_hqT", s), 1)
    yield


def flow_dve(dve, link, g, b, s):
    ps = b.ps[s]
    dve.wait_ge(g("ctx", s), 32)
    for i in range(DC):
        dve.tensor_scalar(b.flow_m[s][:, i, :], b.ctxT[s][:, i, :], b.w3[:, i:i + 1], b.w1[:, i:i + 1],
                          ALU.mult, ALU.add).then_inc(g("L0x_m", s), 1)
    yield
    dve.wait_ge(g("L0x_sim", s), 1)
    sim = ps[:, 2, 0:2 * P].rearrange("p (t n) -> p t n", t=TILES)[:, :, 0:SK]
    link(dve.tensor_scalar(b.sim[s][:, :, :], sim, b.b_sim[:, 0:1], None, ALU.add))
    dve.tensor_reduce(b.nm[s][:, :], b.sim[s][:, :, :], X, ALU.max, negate=True).then_inc(g("L0x_nm", s), 1)
    yield
    dve.wait_ge(g("L0x_exp", s), TILES)
    link(dve.reciprocal(b.ssum[s][:, :], b.ssum[s][:, :]))
    dve.tensor_tensor(b.A[s][:, :, :], b.A[s][:, :, :],
                      b.ssum[s][:, :].unsqueeze(2).to_broadcast([P, TILES, SK]), ALU.mult)\
       .then_inc(g("L0x_A", s), 1)
    yield
    dve.wait_ge(g("L0x_At", s), 1)
    dve.tensor_reduce(b.nM[s][0:1, 0:1], ps[0:1, 1, 0:SEQ], X, ALU.min).then_inc(g("L0x_nM", s), 1)
    dve.wait_ge(g("L0x_nMb", s), 1)
    dve.tensor_copy(b.nMb[s][:, :], ps[:, 2, 2 * P:2 * P + 1]).then_inc(g("L0x_nMs", s), 1)
    yield
    dve.wait_ge(g("L0x_hq", s), 1)
    link(dve.reciprocal(b.nMb[s][:, :], ps[:, 2, 2 * P + 8:2 * P + 9]))
    link(dve.tensor_scalar(b.hc[s][:, :], ps[:, 2, 2 * P + 16:2 * P + 16 + DC], b.nMb[s][:, 0:1], None, ALU.mult))
    dve.wait_ge(g("L0x_hqT", s), 1)
    dve.tensor_tensor(b.xhq[s][:, :, :], b.xT[s][:, :, :], b.hqT[s][:, :, :], ALU.mult).then_inc(g("L0x_f", s), 1)
    dve.tensor_tensor(b.xhc[s][:, :, :], b.xT[s][:, :, :],
                      b.hc[s][:, :].unsqueeze(2).to_broadcast([P, DC, SEQ]), ALU.mult)\
       .then_inc(g("L0x_f", s), 1)
    yield


def block_pe(pe, g, b, s, prev):
    ps, xT, w = b.ps[s], b.xT[s], b.w["L1a"]
    pe.wait_ge(g(prev + "_xT", s), 1)
    for n, bank in enumerate((0, 2)):
        for c in range(DC):
            last = project_T(pe, ps[:, bank, c * SEQ:(c + 1) * SEQ], w[:, :, n * D:(n + 1) * D], c, xT)
        last.then_inc(g("L1a_pqk", s), 1)
    project(pe, ps, 3, xT, w[:, :, 2 * D:3 * D]).then_inc(g("L1a_pvv", s), 1)
    yield
    pe.wait_ge(g("L1a_qk", s), 2)
    for t in range(TILES):
        for c in range(DC):
            last = pe.matmul(ps[:, 1, t * P:(t + 1) * P], lhsT=b.bq[s][:, c, t * P:(t + 1) * P],
                             rhs=b.bk[s][:, c, t * P:(t + 1) * P], start=(c == 0), stop=(c == DC - 1),
                             skip_group_check=True)
    last.then_inc(g("L1a_s", s), 1)
    yield
    pe.wait_ge(g("L1a_p", s), 1)
    for t in range(TILES):
        last = pe.transpose(ps[:, 2, t * P:(t + 1) * P], b.pb[s][:, t, :], b.ident[:, :])
    last.then_inc(g("L1a_pt", s), 1)
    yield
    pe.wait_ge(g("L1a_pT", s), 1)
    pe.wait_ge(g("L1a_v", s), 1)
    for c in range(DC):
        for t in range(TILES):
            last = pe.matmul(ps[:, 3, c * SEQ + t * P:c * SEQ + (t + 1) * P], lhsT=b.bv[s][:, t, c * P:(c + 1) * P],
                             rhs=b.pbT[s][:, t * P:(t + 1) * P], start=True, stop=True, skip_group_check=True)
    last.then_inc(g("L1a_ot", s), 1)
    yield
    pe.wait_ge(g("L1a_oT", s), 1)
    project(pe, ps, 0, b.oT[s], b.wo["L1a"]).then_inc(g("L1a_out", s), 1)
    yield


def block_act(act, g, b, s):
    ps = b.ps[s]
    flat = lambda a: a[:, :, :].rearrange("p c n -> p (c n)")
    for n, (bank, dst) in enumerate(((0, b.bq[s]), (2, b.bk[s]))):
        act.wait_ge(g("L1a_pqk", s), n + 1)
        act.activation(flat(dst), ps[:, bank, :], ACT.Copy).then_inc(g("L1a_qk", s), 1)
    yield
    act.wait_ge(g("L1a_nm", s), 1)
    for t in range(TILES):
        act.activation(b.pb[s][:, t, :], b.sc[s][:, t, :], ACT.Exp, bias=b.nm[s][:, t:t + 1],
                       accum_out=b.ssum[s][:, t:t + 1]).then_inc(g("L1a_exp", s), 1)
    yield
    act.wait_ge(g("L1a_pt", s), 1)
    act.activation(b.pbT[s][:, :], ps[:, 2, 0:SEQ], ACT.Copy).then_inc(g("L1a_pT", s), 1)
    yield
    act.wait_ge(g("L1a_ot", s), 1)
    act.activation(flat(b.oT[s][:, 0:DC, :]), ps[:, 3, :], ACT.Copy).then_inc(g("L1a_oT", s), 1)
    yield


def block_dve(dve, link, g, b, s):
    ps = b.ps[s]
    dve.wait_ge(g("L1a_pvv", s), 1)
    dve.tensor_copy(b.bv[s][:, :, :].rearrange("p t n -> p (t n)"), ps[:, 3, :]).then_inc(g("L1a_v", s), 1)
    yield
    dve.wait_ge(g("L1a_s", s), 1)
    link(dve.scalar_tensor_tensor(b.sc[s][:, :, :], ps[:, 1, 0:SEQ].rearrange("p (t n) -> p t n", t=TILES),
                                  float(D) ** -0.5, b.causal32[:, :].unsqueeze(1).to_broadcast([P, TILES, P]),
                                  ALU.mult, ALU.add))
    dve.tensor_reduce(b.nm[s][:, :], b.sc[s][:, :, :], X, ALU.max, negate=True).then_inc(g("L1a_nm", s), 1)
    yield
    dve.wait_ge(g("L1a_exp", s), TILES)
    link(dve.tensor_scalar(b.ssum[s][:, :], b.ssum[s][:, :], 1e-6, None, ALU.add))
    link(dve.reciprocal(b.ssum[s][:, :], b.ssum[s][:, :]))
    dve.tensor_tensor(b.pb[s][:, :, :], b.pb[s][:, :, :],
                      b.ssum[s][:, :].unsqueeze(2).to_broadcast([P, TILES, P]), ALU.mult)\
       .then_inc(g("L1a_p", s), 1)
    yield


def ternary_pe(pe, g, b, s, prev):
    ps, xT = b.ps[s], b.xT[s]
    pe.wait_ge(g(prev + "_xT", s), 1)
    for f in range(FF2 // P):
        last = project_T(pe, ps[:, f // 2, (f % 2) * SEQ:(f % 2 + 1) * SEQ], b.w["L2f1"], f, xT)
        if f % 2 == 1:
            last.then_inc(g("L2f_h", s), 1)
    yield
    pe.wait_ge(g("L2f_r", s), FF2 // P)
    for t in range(TILES):
        for f in range(FF2 // P):
            last = pe.matmul(ps[:, 0, t * D:(t + 1) * D], lhsT=b.hT[s][:, f, t * P:(t + 1) * P],
                             rhs=b.w["L2f2"][:, f, :], start=(f == 0), stop=(f == FF2 // P - 1),
                             skip_group_check=True)
    last.then_inc(g("L2f_out", s), 1)
    yield


def ternary_act(act, g, b, s):
    for f in range(FF2 // P):
        if f % 2 == 0:
            act.wait_ge(g("L2f_h", s), f // 2 + 1)
        act.activation(b.hT[s][:, f, :], b.ps[s][:, f // 2, (f % 2) * SEQ:(f % 2 + 1) * SEQ], ACT.Relu,
                       bias=b.b1[:, f:f + 1]).then_inc(g("L2f_r", s), 1)
    yield


def wide_pe(pe, g, b, s, prev):
    ps, xT = b.ps[s], b.xT[s]
    pe.wait_ge(g("ctx", s), 32)
    pe.wait_ge(g(prev + "_xT", s), 1)
    for t in range(TILES):
        for i in range(DC):
            last = pe.matmul(ps[:, 0, t * P:t * P + SK], lhsT=xT[:, i, t * P:(t + 1) * P], rhs=b.ctxT[s][:, i, :],
                             start=(i == 0), stop=(i == DC - 1), skip_group_check=True)
    last.then_inc(g("L3x_s", s), 1)
    yield
    pe.wait_ge(g("L3x_A", s), 1)
    for t in range(TILES):
        last = pe.transpose(ps[0:SK, 2, t * P:(t + 1) * P], b.A[s][:, t, :], b.ident[:, :])
    last.then_inc(g("L3x_At", s), 1)
    yield
    pe.wait_ge(g("L3x_AT", s), 1)
    for t in range(TILES):
        last = pe.matmul(ps[:, 1, t * D:(t + 1) * D], lhsT=b.AT[s][:, t * P:(t + 1) * P], rhs=b.ctx[s][:, :],
                         start=True, stop=True, skip_group_check=True)
    last.then_inc(g("L3x_out", s), 1)
    yield


def wide_act(act, g, b, s):
    act.wait_ge(g("L3x_nm", s), 1)
    for t in range(TILES):
        act.activation(b.A[s][:, t, :], b.ps[s][:, 0, t * P:t * P + SK], ACT.Exp, bias=b.nm[s][:, t:t + 1],
                       scale=float(D) ** -0.5, accum_out=b.ssum[s][:, t:t + 1]).then_inc(g("L3x_exp", s), 1)
    yield
    act.wait_ge(g("L3x_At", s), 1)
    act.activation(b.AT[s][:, :], b.ps[s][0:SK, 2, 0:SEQ], ACT.Copy).then_inc(g("L3x_AT", s), 1)
    yield


def wide_dve(dve, link, g, b, s):
    dve.wait_ge(g("L3x_s", s), 1)
    view = b.ps[s][:, 0, 0:2 * P].rearrange("p (t n) -> p t n", t=TILES)[:, :, 0:SK]
    link(dve.tensor_reduce(b.nm[s][:, :], view, X, ALU.max, negate=True))
    dve.tensor_scalar(b.nm[s][:, :], b.nm[s][:, :], float(D) ** -0.5, None, ALU.mult).then_inc(g("L3x_nm", s), 1)
    yield
    dve.wait_ge(g("L3x_exp", s), TILES)
    link(dve.reciprocal(b.ssum[s][:, :], b.ssum[s][:, :]))
    dve.tensor_tensor(b.A[s][:, :, :], b.A[s][:, :, :],
                      b.ssum[s][:, :].unsqueeze(2).to_broadcast([P, TILES, SK]), ALU.mult)\
       .then_inc(g("L3x_A", s), 1)
    yield


UNITS3 = NE + 2


def experts_pe(pe, g, b, s, prev):
    ps, xT = b.ps[s], b.xT[s]
    pe.wait_ge(g(prev + "_xT", s), 1)
    for t in range(TILES):
        for i in range(DC):
            last = pe.matmul(ps[:, 3, t * NE:(t + 1) * NE], lhsT=xT[:, i, t * P:(t + 1) * P], rhs=b.gate_w[:, i, :],
                             start=(i == 0), stop=(i == DC - 1), skip_group_check=True)
    last.then_inc(g("L3f_lg", s), 1)
    pe.matmul(ps[:, 0, :], lhsT=b.ones[0:1, :], rhs=b.sb2_twice[0:1, :], start=True, stop=False,
              skip_group_check=True)
    pe.wait_ge(b.experts_in, 48)
    order = [NE, NE + 1] + list(range(NE))
    for n in range(UNITS3 + 1):
        if n < UNITS3:
            e = order[n]
            for k, w in enumerate((b.w1e, b.w3e)):
                if n >= 1 and k == 0:
                    pe.wait_ge(g("L3f_z", s), 2 * n)
                if n >= 1 and k == 1:
                    pe.wait_ge(g("L3f_b", s), n)
                for i in range(DC):
                    last = pe.matmul(ps[:, 1 + k, 0:SEQ], lhsT=w[:, e, i, :],
                                     rhs=xT[:, i, :], start=(i == 0), stop=(i == DC - 1), skip_group_check=True)
                last.then_inc(g("L3f_h", s), 1)
            if n == 2:
                pe.wait_ge(g("L3f_gw", s), 1)
                for t in range(TILES):
                    pe.transpose(ps[0:NE, 3, SEQ + t * P:SEQ + (t + 1) * P], b.gw[s][:, t, :], b.ident[:, :])
                for t in range(TILES):
                    last = pe.matmul(ps[0:PARTS * NE, 3, t * P:(t + 1) * P],
                                     lhsT=b.mxp[s][:, t, :, :].rearrange("p a h -> p (a h)"), rhs=b.identb[:, :],
                                     start=True, stop=True, skip_group_check=True)
                last.then_inc(g("L3f_gt", s), 1)
                pe.wait_ge(g("L3f_gT", s), 2)
                for t in range(TILES):
                    pe.matmul(ps[:, 0, t * D:(t + 1) * D], lhsT=b.gT[s][:, t * P:(t + 1) * P], rhs=b.b2e[:, :],
                              start=False, stop=False, skip_group_check=True)
            if e < NE:
                if n >= 3:
                    pe.wait_ge(g("L3f_c", s), n - 2)
                pe.matmul(ps[:, 3, 0:SEQ], lhsT=b.onehot[:, e, :], rhs=b.mxT[s][:, :],
                          start=True, stop=True, skip_group_check=True).then_inc(g("L3f_G", s), 1)
        if n >= 1:
            e = order[n - 1]
            if e < NE:
                pe.wait_ge(g("L3f_c", s), n - 2)
            else:
                pe.wait_ge(g("L3f_b", s), n)
            for t in range(TILES):
                last = pe.matmul(ps[:, 0, t * D:(t + 1) * D], lhsT=b.he[s][:, (n - 1) % 2, t * P:(t + 1) * P],
                                 rhs=b.w2e[:, e, :], start=False, stop=(n == UNITS3), skip_group_check=True)
            last.then_inc(g("L3f_out" if n == UNITS3 else "L3f_y", s), 1)
        yield


def experts_act(act, g, b, s):
    order = [NE, NE + 1] + list(range(NE))
    act.wait_ge(g("L3f_raw", s), 1)
    act.activation(b.th[s][:, :], b.raw[s][:, :], ACT.Tanh, scale=0.5).then_inc(g("L3f_th", s), 1)
    for n, e in enumerate(order):
        act.wait_ge(g("L3f_h", s), 2 * n + 1)
        if n >= 2:
            act.wait_ge(g("L3f_a", s), n - 1)
        h1 = b.ps[s][:, 1, 0:SEQ]
        act.activation(b.t3[s][:, n % 2, :], h1, ACT.Tanh, scale=0.5, bias=b.b1e_half[:, e:e + 1])\
           .then_inc(g("L3f_z", s), 1)
        act.activation(b.z3[s][:, n % 2, :], h1, ACT.Identity, scale=0.5, bias=b.b1e_half[:, e:e + 1])\
           .then_inc(g("L3f_z", s), 1)
        if n == 2:
            act.wait_ge(g("L3f_gt", s), 1)
            act.activation(b.gT[s][:, :], b.ps[s][0:NE, 3, SEQ:2 * SEQ], ACT.Copy).then_inc(g("L3f_gT", s), 1)
            act.activation(b.mxT[s][:, :], b.ps[s][0:PARTS * NE, 3, 0:SEQ], ACT.Copy).then_inc(g("L3f_gT", s), 1)
        yield


def experts_dve(dve, link, g, b, s):
    order = [NE, NE + 1] + list(range(NE))
    m8, i8, f8, sel, gw = b.m8[s], b.i8[s], b.f8[s], b.sel[s], b.gw[s]
    lg = b.lg[s]
    dve.wait_ge(g("L3f_lg", s), 1)
    dve.tensor_copy(b.raw[s][:, :], b.ps[s][:, 3, 0:TILES * NE]).then_inc(g("L3f_raw", s), 1)
    dve.wait_ge(g("L3f_raw", s), 1)
    link(dve.tensor_tensor(lg[:, :, :], b.raw[s][:, :].rearrange("p (t e) -> p t e", t=TILES),
                           b.expert_bias[:, :].unsqueeze(1).to_broadcast([P, TILES, NE]), ALU.add))
    link(*[dve.max(m8[:, t, :], lg[:, t, :]) for t in range(TILES)])
    link(*[dve.max_index(i8[:, t, :], m8[:, t, :], lg[:, t, :]) for t in range(TILES)])
    link(dve.tensor_copy(f8[:, :, :], i8[:, :, :]))
    for t in range(TILES):
        link(dve.tensor_scalar(sel[:, t, :], b.iota[:, :], f8[:, t, 0:1], None, ALU.is_equal))
        link(dve.scalar_tensor_tensor(sel[:, t, :], b.iota[:, :], f8[:, t, 1:2], sel[:, t, :],
                                      ALU.is_equal, ALU.add))
    dve.wait_ge(g("L3f_th", s), 1)
    link(dve.tensor_scalar(gw[:, :, :], b.th[s][:, :].rearrange("p (t e) -> p t e", t=TILES), 0.5, 0.5,
                           ALU.mult, ALU.add))
    link(dve.tensor_tensor(gw[:, :, :], gw[:, :, :], sel[:, :, :], ALU.mult))
    link(dve.tensor_reduce(b.nm[s][:, :], gw[:, :, :], X, ALU.add))
    link(dve.tensor_scalar(b.nm[s][:, :], b.nm[s][:, :], 1e-10, None, ALU.add))
    link(dve.reciprocal(b.nm[s][:, :], b.nm[s][:, :]))
    link(dve.tensor_tensor(gw[:, :, :], gw[:, :, :], b.nm[s][:, :].unsqueeze(2).to_broadcast([P, TILES, NE]),
                           ALU.mult))
    split(dve, link, gw[:, :, :], [b.mxp[s][:, :, p, :] for p in range(PARTS)], b.mxr[s][:, :, :], g("L3f_gw", s))
    for n, e in enumerate(order):
        dve.wait_ge(g("L3f_z", s), 2 * n + 2)
        dve.scalar_tensor_tensor(b.a3[s][:, n % 2, :], b.t3[s][:, n % 2, :], 1.0, b.z3[s][:, n % 2, :],
                                 ALU.add, ALU.mult).then_inc(g("L3f_a", s), 1)
        dve.wait_ge(g("L3f_a", s), n + 1)
        if n >= 2:
            dve.wait_ge(g("L3f_y", s), n - 1)
        dve.wait_ge(g("L3f_h", s), 2 * n + 2)
        dve.scalar_tensor_tensor(b.he[s][:, n % 2, :], b.ps[s][:, 2, 0:SEQ],
                                 b.b3e[:, e:e + 1], b.a3[s][:, n % 2, :], ALU.add, ALU.mult)\
           .then_inc(g("L3f_b", s), 1)
        if e < NE:
            dve.wait_ge(g("L3f_b", s), n + 1)
            dve.wait_ge(g("L3f_G", s), n - 1)
            dve.tensor_tensor(b.he[s][:, n % 2, :], b.he[s][:, n % 2, :],
                              b.ps[s][:, 3, 0:SEQ], ALU.mult)\
               .then_inc(g("L3f_c", s), 1)
        yield


SCAN_CHUNKS = DC * BLK // 2


def project_states(nc, g, b, block):
    halves = [(n, h) for n in range(4) for h in range(DC)]
    units = [("k", n, h) for n, h in halves] + [("v", n, h) for n, h in halves] + [("q", n, h) for n, h in halves]
    NK, RING = len(halves), 6
    d = b.dram

    @block.sync
    def _(sp):
        sp.dma_start(b.w0["k"][:, :, :], chunked(d["w0k"])).then_inc(g("w0_in", "k"), 16)
        for n in range(4):
            sp.dma_start(b.xT_all[:, :, n * 512:(n + 1) * 512], chunked(d["xT"])[:, :, n * 512:(n + 1) * 512])\
              .then_inc(g("xT_in", n), 16)
        for name in "vq":
            sp.dma_start(b.w0[name][:, :, :], chunked(d["w0" + name])).then_inc(g("w0_in", name), 16)
        later = [(b.x_all[:, :, :], d["x"].rearrange("(a p) n -> p a n", p=P)), (b.spread[:, :, :], d["spread"]),
                 (b.collect[:, :, :], d["collect"])]
        for dst, src in later:
            sp.dma_start(dst, src).then_inc(g("later"), 16)
        sp.wait_ge(g("later"), 16 * len(later))
        for dst, src in b.prefetch:
            sp.dma_start(dst, src).then_inc(b.first_in, 16)

    @block.tensor
    def _(pe):
        pe.wait_ge(g("small_in"), 32)
        def norm_sum(n):
            pe.wait_ge(g("k_square"), n + 1)
            if n >= 2:
                pe.wait_ge(g("k_norm"), n - 1)
            pe.matmul(b.pst[:, 6 + n % 2, :], lhsT=b.same_block[:, :], rhs=b.sq[:, n % 2, :], start=True,
                      stop=True, skip_group_check=True).then_inc(g("k_sum"), 1)

        for u, (name, n, h) in enumerate(units):
            if u >= RING:
                before = u - RING
                if before < NK:
                    pe.wait_ge(g("k_square"), before + 1)
                else:
                    pe.wait_ge(g("vq_copied"), before - NK + 1)
            if u % NK == 0:
                pe.wait_ge(g("w0_in", name), 16)
            if u < NK and h == 0:
                pe.wait_ge(g("xT_in", n), 16)
            for i in range(DC):
                last = pe.matmul(b.pst[:, u % RING, :], lhsT=b.w0[name][:, i, h * P:(h + 1) * P],
                                 rhs=b.xT_all[:, i, n * 512:(n + 1) * 512], start=(i == 0), stop=(i == DC - 1),
                                 skip_group_check=True)
            last.then_inc(g("projected"), 1)
            if 1 <= u <= NK:
                norm_sum(u - 1)

    @block.scalar
    def _(act):
        for dst, src in ((b.same_block[:, :], d["same_block"]), (b.ident[:, :], d["ident"])):
            act.dma_start(dst, src).then_inc(g("small_in"), 16)

        def root(n):
            act.wait_ge(g("k_sum"), n + 1)
            if n >= 2:
                act.wait_ge(g("k_ready"), n - 1)
            act.activation(b.nrm[:, n % 2, :], b.pst[:, 6 + n % 2, :], ACT.Sqrt).then_inc(g("k_norm"), 1)

        for u, (n, h) in enumerate(halves):
            act.wait_ge(g("projected"), u + 1)
            act.activation(b.kn[:, h, n * 512:(n + 1) * 512], b.pst[:, u % RING, :], ACT.Copy)\
               .then_inc(g("k_copied"), 1)
            if u >= 2:
                act.wait_ge(g("k_sum"), u - 1)
            act.activation(b.sq[:, u % 2, :], b.pst[:, u % RING, :], ACT.Square).then_inc(g("k_square"), 1)
            if u >= 1:
                root(u - 1)
        root(NK - 1)

    @block.vector
    def _(dve):
        dve.memset(b.ones[:, :], 1.0)
        dve.memset(b.minus_half[:, :], -0.5)
        dve.wait_ge(g("small_in"), 32)
        dve.tensor_copy(b.identb[:, :], b.ident[:, :])
        dve.tensor_scalar(b.minus_same_block[:, :], b.same_block[:, :], -1.0, None, ALU.mult)
        link = Chain(dve, g("dve_chain"))
        for u, (n, h) in enumerate(halves):
            dve.wait_ge(g("k_norm"), u + 1)
            dve.wait_ge(g("k_copied"), u + 1)
            r, k = b.nrm[:, u % 2, :], b.kn[:, h, n * 512:(n + 1) * 512]
            link(dve.tensor_scalar(r, r, 1e-6, None, ALU.add))
            link(dve.reciprocal(r, r))
            dve.tensor_tensor(k, k, r, ALU.mult).then_inc(g("k_ready"), 1)
        for u in range(NK, len(units)):
            name, n, h = units[u]
            dve.wait_ge(g("projected"), u + 1)
            dst = b.v0 if name == "v" else b.q0
            dve.tensor_copy(dst[:, h, n * 512:(n + 1) * 512], b.pst[:, u % RING, :]).then_inc(g("vq_copied"), 1)


SCAN_STEPS = 4
SCAN_BANKS = (0, 1, 2, 4, 5)
Y_BANK = 6


def scan_steps(nc, g, b, block, turn):
    at = lambda a, h, n: a[:, h, :].rearrange("p (t n) -> p t n", t=NB)[:, turn * SCAN_STEPS + n, :]
    wide = lambda a: a.unsqueeze(1).to_broadcast([P, 2, SEQ])
    two = lambda a: a.rearrange("p (i n) -> p i n", i=2)
    chunks = [(c // 4, c % 4) for c in range(SCAN_CHUNKS)]
    RING = len(SCAN_BANKS)
    tokens = lambda n: b.x_all[:, bass.ds((turn * SCAN_STEPS + n) * TILES, TILES), :]

    @block.vector
    def _(dve):
        link = Chain(dve, g("dve_chain"))

        def products(n, c):
            h, i = chunks[c]
            if n >= 1:
                dve.wait_ge(g("s_tanh", n - 1), c + 1)
            dve.tensor_tensor(two(b.work[:, c, :]), b.S[:, h, 2 * i:2 * i + 2, :], wide(at(b.kn, h, n)), ALU.mult)\
               .then_inc(g("s_k", n), 1)

        def update(n, c):
            h, i = chunks[c]
            w = two(b.work[:, c, :])
            dve.wait_ge(g("delta", n), c + 1)
            link(dve.tensor_tensor(w, two(b.pst[:, SCAN_BANKS[c % RING], :]), wide(at(b.kn, h, n)), ALU.mult))
            dve.tensor_tensor(w, w, b.S[:, h, 2 * i:2 * i + 2, :], ALU.add).then_inc(g("s_new", n), 1)

        def gate(n):
            s = n % SB
            dve.wait_ge(g("gates", n), 2)
            dve.scalar_tensor_tensor(b.hqT[s][:, :, :], b.xhq[s][:, :, :], 1.0, b.xhc[s][:, :, :],
                                     ALU.add, ALU.mult).then_inc(g("gated", n), 1)

        def finish(n):
            s = n % SB
            link(dve.tensor_copy(b.x[s][:, :, :], tokens(n)))
            norm_dve(dve, link, g, b, s, f"L0a{n}", 3, half=True)
            dve.wait_ge(g(f"L0a{n}_x", s), TILES)
            link(dve.tensor_copy(tokens(n), b.x[s][:, :, :]))

        for n in range(SCAN_STEPS):
            for c in range(SCAN_CHUNKS):
                products(n, c)
                if c >= 2:
                    update(n, c - 2)
                if n >= 1 and c == 3:
                    gate(n - 1)
                if n >= 1 and c == 6:
                    finish(n - 1)
            update(n, SCAN_CHUNKS - 2)
            update(n, SCAN_CHUNKS - 1)
        gate(SCAN_STEPS - 1)
        finish(SCAN_STEPS - 1)

    @block.tensor
    def _(pe):
        def delta(n, c):
            h, i = chunks[c]
            bank = SCAN_BANKS[c % RING]
            pe.wait_ge(g("s_k", n), c + 1)
            if c >= RING:
                pe.wait_ge(g("s_new", n), c - RING + 1)
            elif n >= 1:
                pe.wait_ge(g("s_new", n - 1), SCAN_CHUNKS)
            pe.matmul(b.pst[:, bank, :], lhsT=b.minus_same_block[:, :], rhs=b.work[:, c, :], start=True,
                      stop=False, skip_group_check=True)
            for m in range(2):
                last = pe.matmul(b.pst[:, bank, m * SEQ:(m + 1) * SEQ], lhsT=b.spread[:, 2 * i + m, :],
                                 rhs=at(b.v0, h, n), start=False, stop=True, skip_group_check=True)
            last.then_inc(g("delta", n), 1)

        def read_out(n, c):
            h, i = chunks[c]
            if n >= 1 and c == 0:
                pe.wait_ge(g("gates", n - 1), 2)
            pe.wait_ge(g("s_q", n), c + 1)
            for m in range(2):
                last = pe.matmul(b.pst[:, Y_BANK, h * SEQ:(h + 1) * SEQ], lhsT=b.collect[:, 2 * i + m, :],
                                 rhs=b.sq_out[:, c, m * SEQ:(m + 1) * SEQ], start=(i == 0 and m == 0),
                                 stop=(i == 3 and m == 1), skip_group_check=True)
            if c == SCAN_CHUNKS - 1:
                last.then_inc(g("y", n), 1)

        def output(n):
            s = n % SB
            pe.wait_ge(g("gated", n), 1)
            if n >= SB:
                pe.wait_ge(g(f"L0a{n - SB}_var", s), 1)
            for tt in range(TILES):
                for c in range(DC):
                    last = pe.transpose(b.ps[s][:, 3, tt * D + c * P:tt * D + (c + 1) * P],
                                        b.hqT[s][:, c, tt * P:(tt + 1) * P], b.ident[:, :])
            last.then_inc(g(f"L0a{n}_out", s), 1)

        for n in range(SCAN_STEPS):
            for c in range(SCAN_CHUNKS):
                delta(n, c)
                if n >= 1 and c == 4:
                    output(n - 1)
                if c >= 4:
                    read_out(n, c - 4)
            for c in range(SCAN_CHUNKS - 4, SCAN_CHUNKS):
                read_out(n, c)
        output(SCAN_STEPS - 1)

    @block.scalar
    def _(act):
        for n in range(SCAN_STEPS):
            s = n % SB
            for c in range(SCAN_CHUNKS):
                h, i = chunks[c]
                act.wait_ge(g("s_new", n), c + 1)
                if n >= 1:
                    act.wait_ge(g("s_q", n - 1), c + 1)
                act.activation(b.S[:, h, 2 * i:2 * i + 2, :], two(b.work[:, c, :]), ACT.Tanh)\
                   .then_inc(g("s_tanh", n), 1)
            act.wait_ge(g("y", n), 1)
            if n >= SB:
                act.wait_ge(g("gated", n - SB), 1)
            y = b.pst[:, Y_BANK, :]
            flat = lambda a: a[:, :, :].rearrange("p c n -> p (c n)")
            act.activation(flat(b.xhq[s]), y, ACT.Tanh, scale=0.5).then_inc(g("gates", n), 1)
            act.activation(flat(b.xhc[s]), y, ACT.Square).then_inc(g("gates", n), 1)

    @block.gpsimd
    def _(pool):
        for n in range(SCAN_STEPS):
            if n >= 1:
                pool.wait_ge(g("y", n - 1), 1)
            for c in range(SCAN_CHUNKS):
                h, i = chunks[c]
                pool.wait_ge(g("s_tanh", n), c + 1)
                pool.tensor_tensor(two(b.sq_out[:, c, :]), b.S[:, h, 2 * i:2 * i + 2, :], wide(at(b.q0, h, n)),
                                   ALU.mult).then_inc(g("s_q", n), 1)
                if n >= 1 and c == 3:
                    norm_pool(pool, g, b, (n - 1) % SB, f"L0a{n - 1}")
        norm_pool(pool, g, b, (SCAN_STEPS - 1) % SB, f"L0a{SCAN_STEPS - 1}")


FC = FF1 // P
POOL_PRODUCTS, DVE_PRODUCTS = (0, 2, 4), (1, 3, 5)


class Scale:

    def __init__(self, g, b, name, col):
        self.g, self.b, self.name, self.col = g, b, name, col

    def pe(self, pe):
        g, b, n = self.g, self.b, self.name
        pe.wait_ge(g(n + "_max"), 1)
        pe.transpose(b.pst[0:1, self.col, 0:P], b.gmax[:, self.col:self.col + 1], b.ident[:, :]).then_inc(g(n + "_row"), 1)
        pe.wait_ge(g(n + "_one"), 1)
        pe.matmul(b.pst[:, self.col, P:P + 1], lhsT=b.ones[0:1, :], rhs=b.gone[0:1, self.col:self.col + 1], start=True,
                  stop=True, skip_group_check=True).then_inc(g(n + "_all"), 1)

    def dve(self, dve, link):
        g, b, n, c = self.g, self.b, self.name, self.col
        dve.wait_ge(g(n + "_row"), 1)
        dve.tensor_reduce(b.gone[0:1, c:c + 1], b.pst[0:1, self.col, 0:P], X, ALU.max).then_inc(g(n + "_one"), 1)
        dve.wait_ge(g(n + "_all"), 1)
        link(dve.tensor_scalar(b.scale[:, c:c + 1], b.pst[:, self.col, P:P + 1], 1.0 / QMAX, 1e-12, ALU.mult, ALU.max))
        link(dve.reciprocal(b.inv[:, c:c + 1], b.scale[:, c:c + 1]))


def up_and_gate(nc, g, b, block, i):
    T4 = 4
    units = [(w, m) for w in range(2) for m in range(FC)]

    @block.vector
    def _(dve):
        link = Chain(dve, g("dve_chain"))
        link(dve.tensor_scalar(b.xq[:, :, :], b.x_all[:, bass.ds(i * T4, T4), :], b.inv[:, 6:7], ROUND,
                               ALU.mult, ALU.add))
        dve.tensor_scalar(b.xq[:, :, :], b.xq[:, :, :], -ROUND, b.scale[:, 6:7], ALU.add, ALU.mult)\
           .then_inc(g("xq"), 1)
        for n, (w, m) in enumerate(units):
            dve.wait_ge(g("ug_copy"), n + 1)
            dve.tensor_reduce(b.umax[:, w, m, bass.ds(i, 1)], b.ug[w][:, m, bass.ds(i * 512, 512)], X, ALU.max,
                              apply_absolute_value=True).then_inc(g("ug_max"), 1)

    @block.tensor
    def _(pe):
        pe.wait_ge(g("xq"), 1)
        for c in range(DC):
            for t in range(T4):
                last = pe.transpose(b.pst[:, c, t * P:(t + 1) * P], b.xq[:, t, c * P:(c + 1) * P], b.ident[:, :])
        last.then_inc(g("xqt"), 1)
        pe.wait_ge(g("xqT"), 1)
        for n, (w, m) in enumerate(units):
            if n >= 4:
                pe.wait_ge(g("ug_copy"), n - 3)
            for c in range(DC):
                last = pe.matmul(b.pst[:, 2 + n % 4, :], lhsT=b.wug[w][:, c, m * P:(m + 1) * P],
                                 rhs=b.xqT[:, c, :], start=(c == 0), stop=(c == DC - 1), skip_group_check=True)
            last.then_inc(g("ug"), 1)

    @block.scalar
    def _(act):
        act.wait_ge(g("xqt"), 1)
        act.activation(b.xqT[:, :, :], b.pst[:, 0:2, :], ACT.Copy).then_inc(g("xqT"), 1)
        for n, (w, m) in enumerate(units):
            act.wait_ge(g("ug"), n + 1)
            act.activation(b.ug[w][:, m, bass.ds(i * 512, 512)], b.pst[:, 2 + n % 4, :], ACT.Copy)\
               .then_inc(g("ug_copy"), 1)


def gate_products(nc, g, b, block):
    su, sg, s2, so = (Scale(g, b, n, c) for c, n in ((1, "su"), (2, "sg"), (3, "s2"), (4, "so")))
    up, gate = b.ug

    def gated(dve, link, m):
        dve.wait_ge(g("sig_up"), m + 1)
        s = b.sig[:, m % 2, :]
        link(dve.tensor_scalar(s, s, -ROUND, 65535.0, ALU.add, ALU.min))
        link(dve.scalar_tensor_tensor(gate[:, m, :], b.sig[:, m % 2, :], 1.0 / 65536.0, gate[:, m, :],
                                      ALU.mult, ALU.mult))
        g_done = dve.tensor_reduce(b.fmax[:, 0, m:m + 1], gate[:, m, :], X, ALU.max, apply_absolute_value=True)
        g_done.then_inc(g("g2"), 1)
        dve.wait_ge(g("g2"), m + 1)

    @block.tensor
    def _(pe):
        for sc in (su, sg, s2, so):
            sc.pe(pe)

    @block.vector
    def _(dve):
        link = Chain(dve, g("dve_chain"))
        dve.memset(b.raise_round[:, 0:1], ROUND)
        dve.memset(b.raise_round[:, 1:2], ROUND + 32768.0)
        dve.tensor_reduce(b.gmax[:, 1:2], b.umax[:, 0, :, :], XY, ALU.max).then_inc(g("su_max"), 1)
        dve.tensor_reduce(b.gmax[:, 2:3], b.umax[:, 1, :, :], XY, ALU.max).then_inc(g("sg_max"), 1)
        su.dve(dve, link)
        sg.dve(dve, link)
        dve.nop().then_inc(g("scales"), 1)
        for m in range(FC):
            dve.wait_ge(g("gate_up"), m + 1)
            dve.tensor_scalar(gate[:, m, :], gate[:, m, :], -ROUND, b.scale[:, 2:3], ALU.add, ALU.mult)\
               .then_inc(g("gq"), 1)
            if m >= 1:
                gated(dve, link, m - 1)
        gated(dve, link, FC - 1)
        dve.tensor_reduce(b.gmax[:, 3:4], b.fmax[:, 0, :], X, ALU.max).then_inc(g("s2_max"), 1)
        s2.dve(dve, link)
        dve.nop().then_inc(g("scales"), 1)
        largest = lambda m: link(dve.tensor_reduce(b.fmax[:, 1, m:m + 1], gate[:, m, :], X, ALU.max,
                                                   apply_absolute_value=True))
        for m in range(FC):
            dve.wait_ge(g("gate_up"), FC + m + 1)
            dve.tensor_scalar(gate[:, m, :], gate[:, m, :], -ROUND, b.scale[:, 3:4], ALU.add, ALU.mult)\
               .then_inc(g("g3"), 1)
            if m in DVE_PRODUCTS:
                dve.wait_ge(g("g3"), m + 1)
                dve.wait_ge(g("uq"), m + 1)
                link(dve.tensor_tensor(gate[:, m, :], gate[:, m, :], up[:, m, :], ALU.mult))
                largest(m)
        for n, m in enumerate(POOL_PRODUCTS):
            dve.wait_ge(g("product"), n + 1)
            largest(m)
        dve.tensor_reduce(b.gmax[:, 4:5], b.fmax[:, 1, :], X, ALU.max).then_inc(g("so_max"), 1)
        so.dve(dve, link)

    @block.scalar
    def _(act):
        up_by = lambda n: b.raise_round[:, n:n + 1]

        def raised(a, m, col, done):
            act.activation(a[:, m, :], a[:, m, :], ACT.Identity, scale=b.inv[:, col:col + 1], bias=up_by(0))\
               .then_inc(g(done), 1)

        act.wait_ge(g("scales"), 1)
        raised(gate, 0, 2, "gate_up")
        for m in range(FC):
            if m + 1 < FC:
                raised(gate, m + 1, 2, "gate_up")
            act.wait_ge(g("gq"), m + 1)
            if m >= 2:
                act.wait_ge(g("g2"), m - 1)
            s = b.sig[:, m % 2, :]
            act.activation(s, gate[:, m, :], ACT.Tanh, scale=0.5).then_inc(g("th"), 1)
            act.wait_ge(g("th"), m + 1)
            act.activation(s, s, ACT.Identity, scale=32768.0, bias=up_by(1)).then_inc(g("sig_up"), 1)
            raised(up, m, 1, "up_up")
        act.wait_ge(g("scales"), 2)
        for m in range(FC):
            raised(gate, m, 3, "gate_up")

    @block.gpsimd
    def _(pool):
        for m in range(FC):
            pool.wait_ge(g("up_up"), m + 1)
            pool.tensor_scalar(up[:, m, :], up[:, m, :], -ROUND, b.scale[:, 1:2], ALU.add, ALU.mult)\
                .then_inc(g("uq"), 1)
        for m in POOL_PRODUCTS:
            pool.wait_ge(g("g3"), m + 1)
            pool.wait_ge(g("uq"), m + 1)
            pool.tensor_tensor(gate[:, m, :], gate[:, m, :], up[:, m, :], ALU.mult).then_inc(g("product"), 1)


DOWN = 4


def down(nc, g, b, block, i):
    @block.vector
    def _(dve):
        link = Chain(dve, g("dve_chain"))
        for s in range(DOWN):
            for t in range(TILES):
                dve.tensor_copy(b.x[s][:, t, :], b.x_all[:, bass.ds((i * DOWN + s) * TILES + t, 1), :]
                                .rearrange("p a n -> p (a n)")).then_inc(g("x_in", s), 1)
        for s in range(DOWN):
            o = b.oq[s]
            link(dve.tensor_scalar(o[:, :, :], b.ug[1][:, :, bass.ds((i * DOWN + s) * SEQ, SEQ)], b.inv[:, 4:5],
                                   ROUND, ALU.mult, ALU.add))
            dve.tensor_scalar(o[:, :, :], o[:, :, :], -ROUND, b.scale[:, 4:5], ALU.add, ALU.mult)\
               .then_inc(g("oq", s), 1)
        for s in range(DOWN):
            dve.wait_ge(g("x_in", s), TILES)
            norm_dve(dve, link, g, b, s, "L1f", 0)
        for s in range(DOWN):
            dve.wait_ge(g("L1f_x", s), TILES)
            for t in range(TILES):
                dve.tensor_copy(b.x_all[:, bass.ds((i * DOWN + s) * TILES + t, 1), :].rearrange("p a n -> p (a n)"),
                                b.x[s][:, t, :]).then_inc(g("x_out", s), 1)

    @block.tensor
    def _(pe):
        for s in range(DOWN):
            pe.wait_ge(g("oq", s), 1)
            for t in range(TILES):
                for m in range(FC):
                    last = pe.matmul(b.ps[s][:, 0, t * D:(t + 1) * D], lhsT=b.oq[s][:, m, t * P:(t + 1) * P],
                                     rhs=b.wd[:, m, :], start=(m == 0), stop=(m == FC - 1), skip_group_check=True)
            last.then_inc(g("L1f_out", s), 1)

    @block.gpsimd
    def _(pool):
        for s in range(DOWN):
            norm_pool(pool, g, b, s, "L1f")


def quantise_weights(nc, g, b, block):
    sx = Scale(g, b, "sx", 6)
    todo = [(b.wnat[n], b.wsc[n]) for n in range(3)]

    @block.sync
    def _(sp):
        for n, name in enumerate(("w_up", "w_gate", "w_down")):
            sp.dma_start(b.wnat[n], chunked(b.dram[name])).then_inc(g("loaded", n), 16)
        for n in range(3):
            sp.wait_ge(g("loaded", n), 16)

    @block.vector
    def _(dve):
        link = Chain(dve, g("dve_chain"))
        dve.tensor_reduce(b.gmax[:, 6:7], b.x_all[:, :, :], XY, ALU.max, apply_absolute_value=True)\
           .then_inc(g("sx_max"), 1)
        sx.dve(dve, link)
        for n, (w, sc) in enumerate(todo):
            dve.wait_ge(g("loaded", n), 16)
            blocks = w.rearrange("p a (k r) -> p (a k) r", r=32)
            wide = lambda a: a.unsqueeze(2).to_broadcast([P, 48, 32])
            link(dve.tensor_reduce(sc[:, 0, :], blocks, X, ALU.max, apply_absolute_value=True))
            link(dve.tensor_scalar(sc[:, 0, :], sc[:, 0, :], 1.0 / 7.0, 1e-12, ALU.mult, ALU.max))
            link(dve.reciprocal(sc[:, 1, :], sc[:, 0, :]))
            link(dve.tensor_tensor(blocks, blocks, wide(sc[:, 1, :]), ALU.mult))
            link(dve.tensor_scalar(blocks, blocks, ROUND, -ROUND, ALU.add, ALU.add))
            dve.tensor_tensor(blocks, blocks, wide(sc[:, 0, :]), ALU.mult).then_inc(g("wq"), 1)

    @block.tensor
    def _(pe):
        sx.pe(pe)
        for n in range(3):
            pe.wait_ge(g("wq"), n + 1)
            w = b.wnat[n]
            if n >= 2:
                pe.wait_ge(g("wqT"), 3 * (n - 1))
            for k in range(12):
                a, c = (k // 2, k % 2) if n < 2 else (k // 6, k % 6)
                bank = 3 * (n % 2) + (k // 4)
                last = pe.transpose(b.pst[:, bank, (k % 4) * P:(k % 4 + 1) * P], w[:, a, c * P:(c + 1) * P],
                                    b.ident[:, :])
                if k % 4 == 3:
                    last.then_inc(g("wqt"), 1)

    @block.scalar
    def _(act):
        for n in range(3):
            for q in range(3):
                act.wait_ge(g("wqt"), 3 * n + q + 1)
                bank = b.pst[:, 3 * (n % 2) + q, :]
                if n < 2:
                    dst = b.wug[n][:, :, q * 2 * P:(q + 1) * 2 * P].rearrange("p c (a o) -> p a c o", a=2)
                    src = bank.rearrange("p (a c o) -> p a c o", a=2, c=2)
                    act.activation(dst, src, ACT.Copy).then_inc(g("wqT"), 1)
                else:
                    for j in range(4):
                        k = 4 * q + j
                        ins = act.activation(b.wd[:, k % 6, (k // 6) * P:(k // 6 + 1) * P],
                                             bank[:, j * P:(j + 1) * P], ACT.Copy)
                    ins.then_inc(g("wqT"), 1)


class Buffers:
    pass


def region(nc, body):
    with ExitStack() as ctx:
        g = Signals(nc, ctx)
        with nc.Block(no_gpsimd_drain=True) as block:
            body(g, block)
        runs = g.runs()
        for r in runs[1:]:
            nc.gpsimd.sem_clear(r)
        nc.all_engine_barrier(sems_to_clear=runs[0])


def load(block, g, pairs, first=()):
    @block.sync
    def _(sp):
        for dst, src, done in first:
            sp.dma_start(dst, src).then_inc(done, 16)
        for dst, src in pairs[0::2]:
            sp.dma_start(dst, src).then_inc(g("loaded"), 16)
        sp.wait_ge(g("loaded"), 16 * len(pairs))

    return pairs[1::2], 16 * len(pairs)


def chunked(ap):
    return ap.rearrange("(c p) n -> p c n", p=P)


def pairs_of(b, sb, n=SB):
    return lambda name, shape, dt=F32: [sb(f"{b.phase}_{name}_{s}", shape, dt) for s in range(n)]


def common_buffers(b, pair):
    b.x = pair("x", [P, TILES, D])
    b.r = pair("r", [P, TILES, D])
    b.st = pair("st", [P, TILES, 6])
    b.mv = pair("mv", [P, TILES, 2])
    b.rstd = pair("rstd", [P, TILES])


def heads_buffers(b, pair, keys, dv=DH):
    b.xT = pair("xT", [P, DC, SEQ])
    b.ctx = pair("ctx", [SK, D])
    b.ctxT = pair("ctxT", [P, DC, SK])
    b.qT = pair("qT", [P, DC, SEQ])
    b.kT = pair("kT", [P, DC, SEQ])
    b.qs = pair("qs", [P, DC, NH // DC, SEQ], BF16)
    b.ks = pair("ks", [P, DC, NH // DC, keys], BF16)
    b.vn = pair("vn", [P, TILES, NH * SLOT])
    b.PT = pair("PT", [P, 4, 512])
    b.mx = pair("mx", [P, TILES, NH])
    b.mxr = pair("mxr", [P, TILES, NH])
    b.mxp = pair("mxp", [P, TILES, PARTS, NH], BF16)
    b.mxT = pair("mxT", [PARTS * NH, SEQ], BF16)
    b.kr = pair("kr", [P, DC, SEQ])
    b.oT = pair("oT", [P, NH * max(SLOT, dv) // P, SEQ])
    words = PARTS * DC * SEQ // 2
    for n, name in enumerate(("qp", "kp")):
        flat = [PT[:, :, :].rearrange("p a n -> p (a n)")[:, n * words:(n + 1) * words] for PT in b.PT]
        parts = [f.bitcast(BF16).rearrange("p (a c n) -> p a c n", a=PARTS, c=DC) for f in flat]
        if n == 0:
            b.qp = parts
        else:
            b.kp = parts
    b.A = [PT[:, 1, SEQ:SEQ + TILES * SK].rearrange("p (t n) -> p t n", t=TILES) for PT in b.PT]
    b.AT = [PT[0:SK, 2, SEQ:2 * SEQ] for PT in b.PT]
    b.nm = pair("nm", [P, TILES])
    b.ssum = pair("ssum", [P, TILES])


def clear_spares(pool, b):
    for s in range(SB):
        pool.memset(b.vn[s][:, :, :], 0.0)


def take_in(dve, g, b, s, i):
    for t in range(TILES):
        dve.tensor_copy(b.x[s][:, t, :], b.x_all[:, bass.ds((i * SB + s) * TILES + t, 1), :]
                        .rearrange("p a n -> p (a n)")).then_inc(g("in_x", s), 1)
    dve.wait_ge(g("in_x", s), TILES)


def put_back(dve, g, b, s, i, L):
    dve.wait_ge(g(L + "_x", s), TILES)
    for t in range(TILES):
        dve.tensor_copy(b.x_all[:, bass.ds((i * SB + s) * TILES + t, 1), :].rearrange("p a n -> p (a n)"),
                        b.x[s][:, t, :]).then_inc(g("back", s), 1)


def load_context(sp, g, b, i, s):
    sp.dma_start(b.ctx[s][:, :], b.dram["ctx"].rearrange("(i s) k d -> i s k d", s=SB)[i, s])\
        .then_inc(g("ctx", s), 16)
    sp.dma_start(b.ctxT[s][:, :, :], b.dram["ctxT"].rearrange("(i s) (c p) k -> i s p c k", s=SB, p=P)[i, s])\
        .then_inc(g("ctx", s), 16)


def phase_state(nc, b):
    b.phase = "state"
    with ExitStack() as ctx:
        sb = lambda n, shape, dt=F32: ctx.enter_context(nc.sbuf_tensor(n, shape, dt))
        d = b.dram
        pair = pairs_of(b, sb)
        common_buffers(b, pair)
        b.hqT = pair("hqT", [P, DC, SEQ])
        b.xhq = pair("xhq", [P, DC, SEQ])
        b.xhc = pair("xhc", [P, DC, SEQ])
        b.kn, b.v0, b.q0 = (sb(n, [P, DC, TOKENS]) for n in ("kn", "v0", "q0"))
        b.same_block, b.minus_same_block = sb("same_block", [P, P]), sb("minus_same_block", [P, P])
        b.spread, b.collect = sb("spread", [P, BLK, P]), sb("collect", [P, BLK, P])
        with ExitStack() as inner:
            sbi = lambda n, shape, dt=F32: inner.enter_context(nc.sbuf_tensor(n, shape, dt))
            b.xT_all = sbi("xT_all", [P, DC, TOKENS])
            b.w0 = {n: sbi("w0" + n, [P, DC, D]) for n in "kvq"}
            b.sq, b.nrm = sbi("sq", [P, 2, 512]), sbi("nrm", [P, 2, 512])

            region(nc, lambda g, block: project_states(nc, g, b, block))
        b.S = sb("S", [P, DC, BLK, SEQ])
        b.work, b.sq_out = sb("work", [P, SCAN_CHUNKS, 512]), sb("sq_out", [P, SCAN_CHUNKS, 512])

        def clear(g, block):
            @block.vector
            def _(dve):
                dve.memset(b.S[:, :, :, :], 0.0).then_inc(g("cleared"), 1)

        region(nc, clear)
        with nc.Fori(0, NB // SCAN_STEPS) as turn:
            region(nc, lambda g, block: scan_steps(nc, g, b, block, turn))


def first_weights(nc, b, ctx):
    sb = lambda n, shape, dt=F32: ctx.enter_context(nc.sbuf_tensor(n, shape, dt))
    d = b.dram
    wsim = sb("wsim", [P, 3 * DC])
    b.b_sim, b.causal32 = sb("b_sim", [P, 1]), sb("causal32", [P, P])
    wqv, w0f = sb("wqv", [P, 4 * DC, D]), sb("w0f", [P, DC, D])
    l1a, l1o = sb("l1a", [P, DC, 3 * D]), sb("l1o", [P, DC, D])
    lq, lk = sb("lq", [P, DC, D]), sb("lk", [P, DC, D])
    lv, lo = sb("lv", [P, DC, D]), sb("lo", [P, HC, D])
    row = {n: sb("row_" + n, [P, D]) for n in ("qv", "f0", "o1", "v1", "x1")}
    qb, kb = sb("qb", [P, DC]), sb("kb", [P, DC])
    ld, da = sb("ld", [100, 4]), sb("da", [100, D])
    lu, ua = sb("lu", [4, 50]), sb("ua", [50, D])
    b.first_weights = (wsim, wqv, w0f, l1a, l1o, lq, lk, lv, lo, row, qb, kb, ld, da, lu, ua)
    b.prefetch = [(wsim[:, :], d["wsim"]), (b.b_sim[:, :], d["b_sim"].partition_broadcast(P)),
                  (wqv[:, :, :], chunked(d["wqv"])), (w0f[:, :, :], chunked(d["w0f"])),
                  (l1a[:, :, :], chunked(d["w1a"])), (l1o[:, :, :], chunked(d["w1o"])),
                  (lq[:, :, :], chunked(d["w1xq"])), (lk[:, :, :], chunked(d["w1xk"])),
                  (lv[:, :, :], chunked(d["w1xv"])), (lo[:, :, :], chunked(d["w1xo"])),
                  (qb[:, :], d["b1xq"]), (kb[:, :], d["b1xk"]), (b.causal32[:, :], d["causal"]),
                  (ld[:, :], d["ld"]), (da[:, :], d["da"]), (lu[:, :], d["lu"]), (ua[:, :], d["ua"])]
    b.prefetch += [(row[n][:, :], d["row_" + n].partition_broadcast(P)) for n in row]


def phase_first(nc, b):
    b.phase = "first"

    def stack_constants(g, block):
        @block.vector
        def _(dve):
            link = Chain(dve, g("dve_chain"))
            link(dve.memset(b.sel_q[:, :, :, :], 0.0), dve.memset(b.sel_k[:, :, :, :], 0.0))
            rows = b.identb[:, :].rearrange("p (h d) -> p h d", d=DH).unsqueeze(2)
            for sel, places in ((b.sel_q, [slice(0, 3), slice(3, 6), slice(6, 8)]),
                                (b.sel_k, [slice(p, PRODUCTS, PARTS) for p in range(PARTS)])):
                for p, places_p in enumerate(places):
                    dst = sel[:, p, :, :].rearrange("p h (t d) -> p h t d", d=DH)[:, :, places_p, :]
                    dve.tensor_copy(dst, rows.to_broadcast([P, P // DH, dst.shape[2], DH]))
            link(dve.tensor_tensor(b.one16[:, :], b.ident[0:48, 0:NH], b.ident[0:48, NH:2 * NH], ALU.add))
            link(dve.tensor_tensor(b.one16[:, :], b.one16[:, :], b.ident[0:48, 2 * NH:3 * NH], ALU.add))
            dve.tensor_copy(b.onehot[:, :, :], b.one16[:, :].unsqueeze(2).to_broadcast([PARTS * NH, NH, P]))

    region(nc, stack_constants)
    with ExitStack() as ctx:
        sb = lambda n, shape, dt=F32: ctx.enter_context(nc.sbuf_tensor(n, shape, dt))
        d = b.dram
        pair = pairs_of(b, sb)
        common_buffers(b, pair)
        heads_buffers(b, pair, SK)
        b.nM = pair("nM", [1, 1])
        b.nMb = pair("nMb", [P, 1])
        b.ecol = pair("ecol", [P, TILES])
        b.hc = pair("hc", [P, DC])
        b.mask_u8 = pair("mask_u8", [P, TILES, NH, SK], U8)
        b.maskT_u8 = pair("maskT_u8", [SK, NH, SEQ], U8)
        b.mask = pair("mask", [P, TILES, NH, SK], BF16)
        b.maskT = pair("maskT", [SK, NH, SEQ], BF16)
        b.hqT, b.xhq, b.xhc = b.qT, b.kT, b.kr
        part = lambda bank, at, n: [PT[:, bank, at:at + n] for PT in b.PT]
        tiles = lambda views: [v.rearrange("p (t n) -> p t n", t=TILES) for v in views]
        b.sim, b.flow_m = tiles(part(0, 0, TILES * SK)), tiles(part(0, TILES * SK, DC * SK))
        b.sc, b.pb, b.pbT = tiles(part(1, 0, SEQ)), tiles(part(2, 0, SEQ)), part(3, 0, SEQ)
        b.bq, b.bk, b.bv = b.hqT, b.xhq, b.xhc
        (wsim, wqv, w0f, l1a, l1o, lq, lk, lv, lo, row, qb, kb, ld, da, lu, ua) = b.first_weights
        b.w1, w2, b.w3 = wsim[:, 0:2], wsim[:, 2:4], wsim[:, 4:6]
        b.w2_wide = sb("w2_wide", [P, DC, P])
        t1, t2 = sb("t1", [4, D]), sb("t2", [50, D])
        b.w = {"L0x": wqv, "L0f": w0f, "L1a": l1a, "L1x": {"q": lq, "k": lk, "v": lv}}
        b.wo = {"L1a": l1o, "L1x": lo}
        b.heads = {"L1x": Heads("L1x", [(0, SK)], DH, (2, 2, 1), "per_head")}

        def begin(g, block):
            total = 16 * len(b.prefetch)

            @block.scalar
            def _(act):
                act.wait_ge(g("lora"), 1)
                act.activation(t1[:, :], b.pst[0:4, 0, 0:D], ACT.Copy).then_inc(g("lora_copied"), 1)
                act.wait_ge(g("lora"), 2)
                act.activation(t2[:, :], b.pst[0:50, 1, 0:D], ACT.Copy).then_inc(g("lora_copied"), 1)

            @block.tensor
            def _(pe):
                pe.wait_ge(b.first_in, total)
                pe.matmul(b.pst[0:4, 0, 0:D], lhsT=ld[:, :], rhs=da[:, :], start=True, stop=True)\
                  .then_inc(g("lora"), 1)
                pe.wait_ge(g("lora_copied"), 1)
                pe.matmul(b.pst[0:50, 1, 0:D], lhsT=lu[:, :], rhs=t1[:, :], start=True, stop=True)\
                  .then_inc(g("lora"), 1)
                pe.wait_ge(g("lora_copied"), 2)
                for c in range(DC):
                    last = pe.matmul(b.pst[:, 2, c * D:(c + 1) * D], lhsT=t2[:, c * P:(c + 1) * P], rhs=ua[:, :],
                                     start=True, stop=True, skip_group_check=True)
                last.then_inc(g("lora"), 1)

            @block.vector
            def _(dve):
                dve.wait_ge(b.first_in, total)
                dve.tensor_copy(b.w2_wide[:, :, :], w2.unsqueeze(2).to_broadcast([P, DC, P]))
                dve.wait_ge(g("lora"), 3)
                dve.tensor_tensor(w0f[:, :, :], w0f[:, :, :], b.pst[:, 2, :].rearrange("p (c n) -> p c n", c=DC),
                                  ALU.add)

            @block.gpsimd
            def _(pool):
                clear_spares(pool, b)

        region(nc, begin)

        def turn(i):
            def body(g, block):
                @block.sync
                def _(sp):
                    for s in range(SB):
                        load_context(sp, g, b, i, s)
                    for s in range(SB):
                        for t in range(TILES):
                            src = d["mask"].rearrange("(i s) (t p) h k -> i s t p h k", s=SB, p=P)[i, s, t]
                            sp.dma_start(b.mask_u8[s][:, t, :, :], src).then_inc(g("mask_in", s), 16)
                        src = d["maskT"].rearrange("(i s) k h q -> i s k h q", s=SB)[i, s]
                        sp.dma_start(b.maskT_u8[s][:, :, :], src).then_inc(g("mask_in", s), 16)

                @block.gpsimd
                def _(pool):
                    link = Chain(pool, g("pool_chain"))
                    for s in range(SB):
                        norm_pool(pool, g, b, s, "L0x")
                    for s in range(SB):
                        norm_pool(pool, g, b, s, "L0f")
                    for s in range(SB):
                        norm_pool(pool, g, b, s, "L1a")
                    for s in range(SB):
                        split_k(pool, link, g, b, s, b.heads["L1x"])
                    for s in range(SB):
                        norm_pool(pool, g, b, s, "L1x")

                def pe_program(pe, s):
                    norm_pe(pe, g, b, s, "in", 2)
                    yield from flow_pe(pe, g, b, s, "in")
                    norm_pe(pe, g, b, s, "L0x", 2)
                    pe.wait_ge(g("L0x_xT", s), 1)
                    project(pe, b.ps[s], 0, b.xT[s], w0f).then_inc(g("L0f_out", s), 1)
                    yield
                    norm_pe(pe, g, b, s, "L0f", 2)
                    yield from block_pe(pe, g, b, s, "L0f")
                    yield from context_pe(pe, g, b, s, "L1x")
                    norm_pe(pe, g, b, s, "L1a", 2)
                    yield from cross_pe(pe, g, b, s, "L1x", "L1a")
                    yield from heads_pe(pe, g, b, s, b.heads["L1x"])

                @block.tensor
                def _(pe):
                    side_by_side([pe_program(pe, s) for s in range(SB)])

                def act_program(act, s):
                    norm_act(act, g, b, s, "in", 2)
                    yield
                    yield from flow_act(act, g, b, s)
                    act.wait_ge(g("mask_in", s), 48)
                    act.activation(b.mask[s][:, :, :, :], b.mask_u8[s][:, :, :, :], ACT.Copy, scale=NEG)\
                       .then_inc(g("L1x_mask", s), 1)
                    act.activation(b.maskT[s][:, :, :], b.maskT_u8[s][:, :, :], ACT.Copy, scale=NEG)\
                       .then_inc(g("L1x_mask", s), 1)
                    norm_act(act, g, b, s, "L0x", 2)
                    yield
                    norm_act(act, g, b, s, "L0f", 2)
                    yield
                    yield from block_act(act, g, b, s)
                    yield from context_act(act, g, b, s, "L1x", kb)
                    norm_act(act, g, b, s, "L1a", 2)
                    yield
                    yield from cross_act(act, g, b, s, "L1x", qb)
                    yield from heads_act(act, g, b, s, b.heads["L1x"])

                @block.scalar
                def _(act):
                    side_by_side([act_program(act, s) for s in range(SB)])

                def dve_program(dve, link, s):
                    take_in(dve, g, b, s, i)
                    yield
                    yield from flow_dve(dve, link, g, b, s)
                    add_bias(dve, link, b, s, row["qv"][:, :])
                    yield
                    norm_dve(dve, link, g, b, s, "L0x", 0, biased=True)
                    yield
                    add_bias(dve, link, b, s, row["f0"][:, :])
                    yield
                    norm_dve(dve, link, g, b, s, "L0f", 0, biased=True)
                    yield
                    yield from block_dve(dve, link, g, b, s)
                    add_bias(dve, link, b, s, row["o1"][:, :])
                    yield
                    norm_dve(dve, link, g, b, s, "L1a", 0, biased=True)
                    yield
                    yield from cross_dve(dve, link, g, b, s, "L1x", row["v1"])
                    yield from heads_dve(dve, link, g, b, s, b.heads["L1x"])
                    add_bias(dve, link, b, s, row["x1"][:, :])
                    yield
                    norm_dve(dve, link, g, b, s, "L1x", 1, biased=True)
                    yield
                    put_back(dve, g, b, s, i, "L1x")

                @block.vector
                def _(dve):
                    link = Chain(dve, g("dve_chain"))
                    side_by_side([dve_program(dve, link, s) for s in range(SB)])

            return body

        with nc.Fori(0, NB // SB) as i:
            region(nc, turn(i))


def phase_quantised(nc, b):
    b.phase = "quantised"
    with ExitStack() as ctx:
        sb = lambda n, shape, dt=F32: ctx.enter_context(nc.sbuf_tensor(n, shape, dt))
        d = b.dram
        b.ug = [sb("up", [P, FC, TOKENS]), sb("gate", [P, FC, TOKENS])]
        b.wd = sb("wd", [P, FC, D])
        b.gmax, b.gone, b.scale, b.inv = sb("gmax", [P, 7]), sb("gone", [1, 7]), sb("scale", [P, 7]), sb("inv", [P, 7])
        b.raise_round = sb("raise_round", [P, 2])
        b.umax, b.fmax = sb("umax", [P, 2, FC, 4]), sb("fmax", [P, 2, FC])
        with ExitStack() as inner:
            sbi = lambda n, shape, dt=F32: inner.enter_context(nc.sbuf_tensor(n, shape, dt))
            b.wug = [sbi("wup", [P, DC, FF1]), sbi("wgate", [P, DC, FF1])]
            shapes = [(FC, D), (FC, D), (DC, FF1)]
            wn = [sbi(f"wnat{n}", [P, a, m]) for n, (a, m) in enumerate(shapes)]
            b.wnat = [w[:, :, :] for w in wn]
            b.wsc = [sbi(f"wsc{n}", [P, 2, 48]) for n in range(3)]
            b.xq, b.xqT = sbi("xq", [P, 4, D]), sbi("xqT", [P, DC, 512])

            region(nc, lambda g, block: quantise_weights(nc, g, b, block))
            with nc.Fori(0, 4) as i:
                region(nc, lambda g, block: up_and_gate(nc, g, b, block, i))
        with ExitStack() as inner:
            b.sig = inner.enter_context(nc.sbuf_tensor("sig", [P, 2, TOKENS], F32))
            region(nc, lambda g, block: gate_products(nc, g, b, block))
        each = pairs_of(b, sb, DOWN)
        common_buffers(b, each)
        b.oq = each("oq", [P, FC, SEQ])
        of_streams, b.ps = b.ps, [b.pst[:, 2 * s:2 * s + 2, :] for s in range(DOWN)]
        with nc.Fori(0, NB // DOWN) as i:
            region(nc, lambda g, block: down(nc, g, b, block, i))
        b.ps = of_streams


def phase_second(nc, b):
    b.phase = "second"
    with ExitStack() as ctx:
        sb = lambda n, shape, dt=F32: ctx.enter_context(nc.sbuf_tensor(n, shape, dt))
        d = b.dram
        pair = pairs_of(b, sb)
        common_buffers(b, pair)
        heads_buffers(b, pair, SEQ, DV2)
        b.vw = pair("vw", [P, TILES, NH * DV2])
        b.hT = b.oT
        aq, ak, av = sb("aq", [P, DC, D]), sb("ak", [P, DC, D]), sb("av", [P, DC, NH * DV2])
        ao = sb("ao", [P, NH * DV2 // P, D])
        xq, xk, xv, xo = sb("xq2", [P, DC, D]), sb("xk2", [P, DC, D]), sb("xv2", [P, DC, D]), sb("xo2", [P, HC, D])
        f1, f2 = sb("f1", [P, DC, FF2]), sb("f2", [P, FF2 // P, D])
        b.b1, row_b2 = sb("b1", [P, FF2 // P]), sb("row_b2", [P, D])
        causal32, causalT32 = b.r[0][:, 0, 0:P], b.r[0][:, 1, 0:P]
        b.causal, b.causalT = sb("causalb", [P, P], BF16), sb("causalTb", [P, P], BF16)
        sm8, smT8 = sb("sm8", [P, TILES, SK], U8), sb("smT8", [SK, SEQ], U8)
        b.smask, b.smaskT = sb("smask", [P, TILES, SK], BF16), sb("smaskT", [SK, SEQ], BF16)
        valid, gam = sb("valid", [P, TILES]), sb("gam", [P, 2])
        b.w = {"L2a": {"q": aq, "k": ak, "v": av}, "L2x": {"q": xq, "k": xk, "v": xv}, "L2f1": f1, "L2f2": f2}
        b.wo = {"L2a": ao, "L2x": xo}
        b.heads = {"L2a": Heads("L2a", [(0, P), (P, P)], DV2, (1, 1, 2), "causal"),
                   "L2x": Heads("L2x", [(0, SK)], DH, (2, 2, 1), "shared")}

        def begin(g, block):
            pairs = [(w[:, :, :], chunked(d[n])) for w, n in (
                (aq, "w2aq"), (ak, "w2ak"), (av, "w2av"), (ao, "w2ao"), (xq, "w2xq"), (xk, "w2xk"), (xv, "w2xv"),
                (xo, "w2xo"))]
            pairs += [(b.b1[:, :], d["b2f1"]), (row_b2[:, :], d["row_b2"].partition_broadcast(P)),
                      (causal32[:, :], d["causal"]), (causalT32[:, :], d["causalT"]),
                      (sm8[:, :, :], d["smask"].rearrange("(t p) k -> p t k", p=P)), (smT8[:, :], d["smaskT"])]
            rest, total = load(block, g, pairs, [(f1[:, :, :], chunked(d["w2f1"]), g("ternary", 0))])

            @block.scalar
            def _(act):
                act.dma_start(f2[:, :, :], chunked(d["w2f2"])).then_inc(g("ternary", 1), 16)
                for dst, src in rest:
                    act.dma_start(dst, src).then_inc(g("loaded"), 16)

            @block.gpsimd
            def _(pool):
                clear_spares(pool, b)

            @block.tensor
            def _(pe):
                pe.wait_ge(g("sums"), 2)
                pe.matmul(b.pst[:, 0, 0:2], lhsT=b.ones[:, :], rhs=gam[:, :], start=True, stop=True)\
                  .then_inc(g("gamma"), 1)

            @block.vector
            def _(dve):
                link = Chain(dve, g("dve_chain"))
                for n, w in enumerate((f1, f2)):
                    dve.wait_ge(g("ternary", n), 16)
                    dve.tensor_reduce(gam[:, n:n + 1], w[:, :, :], XY, ALU.add, apply_absolute_value=True)\
                       .then_inc(g("sums"), 1)
                dve.wait_ge(g("gamma"), 1)
                link(dve.tensor_scalar(gam[:, :], b.pst[:, 0, 0:2], 1.0 / (FF2 * D), EPS, ALU.mult, ALU.add))
                link(dve.reciprocal(gam[:, :], gam[:, :]))
                for n, w in enumerate((f1, f2)):
                    link(dve.tensor_scalar(w[:, :, :], w[:, :, :], gam[:, n:n + 1], ROUND, ALU.mult, ALU.add))
                    link(dve.tensor_scalar(w[:, :, :], w[:, :, :], -ROUND, 1.0, ALU.add, ALU.min))
                    link(dve.tensor_scalar(w[:, :, :], w[:, :, :], -1.0, None, ALU.max))
                dve.wait_ge(g("loaded"), total)
                dve.tensor_copy(b.causal[:, :], causal32[:, :])
                dve.tensor_copy(b.causalT[:, :], causalT32[:, :])
                dve.tensor_scalar(b.smask[:, :, :], sm8[:, :, :], -NEG, NEG, ALU.mult, ALU.add)
                dve.tensor_scalar(b.smaskT[:, :], smT8[:, :], -NEG, NEG, ALU.mult, ALU.add)
                dve.tensor_reduce(valid[:, :], sm8[:, :, :], X, ALU.max)

        region(nc, begin)

        def turn(i):
            def body(g, block):
                @block.sync
                def _(sp):
                    for s in range(SB):
                        load_context(sp, g, b, i, s)

                @block.gpsimd
                def _(pool):
                    link = Chain(pool, g("pool_chain"))
                    for L in ("L2a", "L2x", "L2f"):
                        for s in range(SB):
                            if L in b.heads:
                                split_k(pool, link, g, b, s, b.heads[L])
                        for s in range(SB):
                            norm_pool(pool, g, b, s, L)

                def pe_program(pe, s):
                    norm_pe(pe, g, b, s, "in", 3)
                    yield from causal_pe(pe, g, b, s, "in")
                    yield from context_pe(pe, g, b, s, "L2x")
                    norm_pe(pe, g, b, s, "L2a", 3)
                    yield from cross_pe(pe, g, b, s, "L2x", "L2a")
                    yield from heads_pe(pe, g, b, s, b.heads["L2x"])
                    norm_pe(pe, g, b, s, "L2x", 3)
                    yield from ternary_pe(pe, g, b, s, "L2x")

                @block.tensor
                def _(pe):
                    side_by_side([pe_program(pe, s) for s in range(SB)])

                def act_program(act, s):
                    norm_act(act, g, b, s, "in", 3)
                    yield
                    yield from causal_act(act, g, b, s)
                    yield from context_act(act, g, b, s, "L2x")
                    norm_act(act, g, b, s, "L2a", 3)
                    yield
                    yield from cross_act(act, g, b, s, "L2x")
                    yield from heads_act(act, g, b, s, b.heads["L2x"])
                    norm_act(act, g, b, s, "L2x", 3)
                    yield
                    yield from ternary_act(act, g, b, s)

                @block.scalar
                def _(act):
                    side_by_side([act_program(act, s) for s in range(SB)])

                def dve_program(dve, link, s):
                    take_in(dve, g, b, s, i)
                    yield
                    yield from causal_dve(dve, link, g, b, s)
                    norm_dve(dve, link, g, b, s, "L2a", 1)
                    yield
                    yield from cross_dve(dve, link, g, b, s, "L2x")
                    yield from heads_dve(dve, link, g, b, s, b.heads["L2x"], 1e-9)
                    norm_dve(dve, link, g, b, s, "L2x", 1, valid=valid)
                    yield
                    add_bias(dve, link, b, s, row_b2[:, :])
                    yield
                    norm_dve(dve, link, g, b, s, "L2f", 0, biased=True)
                    yield
                    put_back(dve, g, b, s, i, "L2f")

                @block.vector
                def _(dve):
                    link = Chain(dve, g("dve_chain"))
                    side_by_side([dve_program(dve, link, s) for s in range(SB)])

            return body

        with nc.Fori(0, NB // SB) as i:
            region(nc, turn(i))


def phase_third(nc, b, out):
    b.phase = "third"
    with ExitStack() as ctx:
        b.experts_in = ctx.enter_context(nc.semaphore("experts_in"))
        sb = lambda n, shape, dt=F32: ctx.enter_context(nc.sbuf_tensor(n, shape, dt))
        d = b.dram
        pair = pairs_of(b, sb)
        common_buffers(b, pair)
        heads_buffers(b, pair, SEQ)
        quarter = lambda a: [PT[:, a, :].rearrange("p (c n) -> p c n", c=2) for PT in b.PT]
        b.rc, b.rs = quarter(3), b.r
        b.t3, b.z3, b.a3, b.he = (quarter(a) for a in range(4))
        b.th = pair("th", [P, TILES * NE])
        b.raw = pair("raw", [P, TILES * NE])
        b.lg = pair("lg", [P, TILES, NE])
        b.m8 = pair("m8", [P, TILES, 8])
        b.i8 = pair("i8", [P, TILES, 8], U32)
        b.f8 = pair("f8", [P, TILES, 8])
        b.sel = pair("sel", [P, TILES, NE])
        b.gw = pair("gw", [P, TILES, NE])
        b.gT = pair("gT", [NE, SEQ])
        w3 = {n: sb("w3a_" + n, [P, DC, D]) for n in ("q", "q_rot", "k", "k_rot")}
        w3["v"] = sb("w3a_v", [P, DC, D])
        w3o = sb("w3o", [P, HC, D])
        b.rope_bias = {n: sb("rb_" + n, [P, DC]) for n in ("q", "q_rot", "k", "k_rot")}
        b.cos, b.sin = sb("cos", [P, SEQ]), sb("sin", [P, SEQ])
        b.v_bias, row_o = {"L3a": sb("v_bias", [P, D])}, sb("row_o3", [P, D])
        b.w1e, b.w3e = sb("w1e", [P, UNITS3, DC, FF3]), sb("w3e", [P, UNITS3, DC, FF3])
        b.w2e = sb("w2e", [P, UNITS3, D])
        b.b1e_half, b.b3e, b.b2e = sb("b1e", [P, UNITS3]), sb("b3e", [P, UNITS3]), sb("b2e", [NE, D])
        b.gate_w, b.expert_bias = sb("gate_w", [P, DC, NE]), sb("expert_bias", [P, NE])
        b.iota, b.sb2_twice = sb("iota", [P, NE]), sb("sb2", [1, 2 * D])
        b.w, b.wo = {"L3a": w3}, {"L3a": w3o}
        b.heads = {"L3a": Heads("L3a", [(0, P), (P, P)], DH, (1, 1, 1))}

        def begin(g, block):
            pairs = [(w3[n][:, :, :], chunked(d["w3" + n])) for n in w3]
            pairs += [(b.rope_bias[n][:, :], d["rb_" + n]) for n in b.rope_bias]
            pairs += [(w3o[:, :, :], chunked(d["w3o"])), (b.cos[:, :], d["cos"]), (b.sin[:, :], d["sin"]),
                      (b.v_bias["L3a"][:, :], d["row_v3"].partition_broadcast(P)),
                      (row_o[:, :], d["row_o3"].partition_broadcast(P)),
                      (b.b1e_half[:, :], d["b1e"]), (b.b3e[:, :], d["b3e"]), (b.b2e[:, :], d["b2e"]),
                      (b.gate_w[:, :, :], chunked(d["gate_w"])),
                      (b.expert_bias[:, :], d["expert_bias"].partition_broadcast(P)),
                      (b.iota[:, :], d["iota"].partition_broadcast(P)),
                      (b.sb2_twice[:, :], d["sb2"])]
            rest, total = load(block, g, pairs)

            @block.scalar
            def _(act):
                for dst, src in rest:
                    act.dma_start(dst, src).then_inc(g("loaded"), 16)
                for dst, src in ((b.w1e[:, :, :, :], d["w1e"].rearrange("e (c p) f -> p e c f", p=P)),
                                 (b.w3e[:, :, :, :], d["w3e"].rearrange("e (c p) f -> p e c f", p=P)),
                                 (b.w2e[:, :, :], d["w2e"].rearrange("e p n -> p e n"))):
                    act.dma_start(dst, src).then_inc(b.experts_in, 16)

            @block.gpsimd
            def _(pool):
                clear_spares(pool, b)

            @block.vector
            def _(dve):
                dve.wait_ge(g("loaded"), total)
                dve.tensor_scalar(b.b1e_half[:, :], b.b1e_half[:, :], 0.5, None, ALU.mult)

        region(nc, begin)

        def turn(i):
            def body(g, block):
                @block.sync
                def _(sp):
                    for s in range(SB):
                        load_context(sp, g, b, i, s)
                    for s in range(SB):
                        sp.wait_ge(g("L3f_x", s), TILES)
                        sp.dma_start(out.rearrange("(i s) (t p) n -> i s p t n", s=SB, p=P)[i, s],
                                     b.x[s][:, :, :]).then_inc(g("stored", s), 16)
                    for s in range(SB):
                        sp.wait_ge(g("stored", s), 16)

                @block.gpsimd
                def _(pool):
                    link = Chain(pool, g("pool_chain"))
                    for L in ("L3a", "L3x", "L3f"):
                        for s in range(SB):
                            if L in b.heads:
                                split_k(pool, link, g, b, s, b.heads[L])
                        for s in range(SB):
                            norm_pool(pool, g, b, s, L)

                def pe_program(pe, s):
                    norm_pe(pe, g, b, s, "in", 3)
                    yield from rotary_pe(pe, g, b, s, "in")
                    norm_pe(pe, g, b, s, "L3a", 3)
                    yield from wide_pe(pe, g, b, s, "L3a")
                    norm_pe(pe, g, b, s, "L3x", 3)
                    yield from experts_pe(pe, g, b, s, "L3x")

                @block.tensor
                def _(pe):
                    side_by_side([pe_program(pe, s) for s in range(SB)])

                def act_program(act, s):
                    norm_act(act, g, b, s, "in", 3)
                    yield
                    for _ in range(6):
                        yield
                    yield from heads_act(act, g, b, s, b.heads["L3a"])
                    norm_act(act, g, b, s, "L3a", 3)
                    yield
                    yield from wide_act(act, g, b, s)
                    norm_act(act, g, b, s, "L3x", 3)
                    yield
                    yield from experts_act(act, g, b, s)

                @block.scalar
                def _(act):
                    side_by_side([act_program(act, s) for s in range(SB)])

                def dve_program(dve, link, s):
                    take_in(dve, g, b, s, i)
                    yield
                    yield from rotary_dve(dve, link, g, b, s)
                    add_bias(dve, link, b, s, row_o[:, :])
                    yield
                    norm_dve(dve, link, g, b, s, "L3a", 1, biased=True)
                    yield
                    yield from wide_dve(dve, link, g, b, s)
                    norm_dve(dve, link, g, b, s, "L3x", 1)
                    yield
                    yield from experts_dve(dve, link, g, b, s)
                    norm_dve(dve, link, g, b, s, "L3f", 0)
                    yield

                @block.vector
                def _(dve):
                    link = Chain(dve, g("dve_chain"))
                    side_by_side([dve_program(dve, link, s) for s in range(SB)])

            return body

        with nc.Fori(0, NB // SB) as i:
            region(nc, turn(i))


def program(nc, dram, out, phases=5):
    with ExitStack() as ctx:
        b = Buffers()
        b.dram = dram
        sb = lambda n, shape, dt=F32: ctx.enter_context(nc.sbuf_tensor(n, shape, dt))
        b.x_all = sb("x_all", [P, NB * TILES, D])
        b.ident, b.identb, b.ones = sb("ident", [P, P]), sb("identb", [P, P], BF16), sb("ones", [P, P])
        b.minus_half = sb("minus_half", [P, TILES])
        b.sel_q = sb("sel_q", [P, PARTS, P // DH, P], BF16)
        b.sel_k = sb("sel_k", [P, PARTS, P // DH, P], BF16)
        b.one16, b.onehot = sb("one16", [PARTS * NH, NH]), sb("onehot", [PARTS * NH, NH, P], BF16)
        b.pst = ctx.enter_context(nc.psum_tensor("banks", [P, 8, 512], F32))
        b.ps = [b.pst[:, 4 * s:4 * s + 4, :] for s in range(SB)]
        b.first_in = ctx.enter_context(nc.semaphore("first_in"))
        with ExitStack() as first:
            first_weights(nc, b, first)
            phase_state(nc, b)
            if phases > 1:
                phase_first(nc, b)
        if phases > 2:
            phase_quantised(nc, b)
        if phases > 3:
            phase_second(nc, b)
        if phases > 4:
            phase_third(nc, b, out)
        else:
            def show(g, block):
                @block.sync
                def _(sp):
                    sp.dma_start(out.rearrange("b (t p) n -> p (b t) n", p=P), b.x_all[:, :, :]).then_inc(g("shown"), 16)
                    sp.wait_ge(g("shown"), 16)
            region(nc, show)


def laid_out(a):
    f = np.float32
    rows = lambda v: v.reshape(1, -1)

    def slots(w):
        w = w.reshape(NH, DH, -1)
        return np.concatenate([w, np.zeros((NH, SLOT - DH, w.shape[2]), f)], 1).reshape(NH * SLOT, -1)

    def columns(v):
        return v.reshape(-1, P).T

    def half_swapped(w):
        w = w.reshape(*w.shape[:-1], NH, 2, DH // 2)
        return w[..., ::-1, :].reshape(*w.shape[:-3], NH * DH)

    p = np.arange(P)
    same = (p[:, None] // BLK == p[None, :] // BLK)
    spread = np.stack([same & (p[:, None] % BLK == i) for i in range(BLK)], 1).astype(f)
    collect = np.stack([same & (p[None, :] % BLK == i) for i in range(BLK)], 1).astype(f)
    causal = np.where(p[None, :] <= p[:, None], 0.0, NEG).astype(f)
    inv_freq = (f(1.0) / f(10000.0) ** (np.arange(0, DH, 2, dtype=f) / f(DH))).astype(f)
    angle = np.arange(SEQ, dtype=f)[:, None] * inv_freq[None, :]
    cos = np.concatenate([np.cos(angle), np.cos(angle)], 1).T
    sin = np.concatenate([-np.sin(angle), np.sin(angle)], 1).T
    x, ctx = a["x"], a["ctx_1024"]
    mask = a["mask_Bx16xSxS2_bk1"]
    smask = a["mask_SxS2_bk0"]
    w3, b3 = a["L3_attn_W_qkv"].reshape(D, 3, D), a["L3_attn_b_qkv"].reshape(3, D)
    sw = lambda n: a[f"L3_ffn_s{n}"].reshape(2, FF3, D)
    return {
        "x": x.reshape(TOKENS, D), "xT": x.reshape(TOKENS, D).T, "ctx": ctx, "ctxT": ctx.transpose(0, 2, 1),
        "mask": mask.transpose(0, 2, 1, 3), "maskT": mask.transpose(0, 3, 1, 2), "smask": smask, "smaskT": smask.T,
        "w0k": a["L0_attn_W_k"].T, "w0v": a["L0_attn_W_v"].T, "w0q": a["L0_attn_W_q"].T,
        "same_block": same.astype(f), "spread": spread, "collect": collect, "ident": np.eye(P, dtype=f),
        "causal": causal, "causalT": causal.T,
        "wsim": columns(a["L0_xattn_w_sim"]), "b_sim": rows(a["L0_xattn_b_sim"]), "wqv": a["L0_xattn_W_qv"],
        "row_qv": rows(a["L0_xattn_b_qv"]), "w0f": a["L0_ffn_W"].T, "row_f0": rows(a["L0_ffn_b"]),
        "ld": a["L0_ffn_lora_down"].T, "da": a["L0_ffn_down_aux"], "lu": a["L0_ffn_lora_up"].T,
        "ua": a["L0_ffn_up_aux"].T,
        "w1a": a["L1_attn_W_qkv"], "w1o": a["L1_attn_W_out"].T, "row_o1": rows(a["L1_attn_b_out"]),
        "w1xq": a["L1_xattn_Wq"], "w1xk": a["L1_xattn_Wk"], "w1xv": a["L1_xattn_Wv"],
        "w1xo": slots(a["L1_xattn_Wo"]), "b1xq": columns(a["L1_xattn_bq"]),
        "b1xk": columns(a["L1_xattn_bk"]), "row_v1": rows(a["L1_xattn_bv"]),
        "row_x1": rows(a["L1_xattn_bo"]),
        "w_up": a["L1_ffn_w_up"], "w_gate": a["L1_ffn_w_gate"], "w_down": a["L1_ffn_w_down"],
        "w2aq": a["L2_attn_Wq"], "w2ak": a["L2_attn_Wk"], "w2av": a["L2_attn_Wv"],
        "w2ao": a["L2_attn_Wo"], "w2xq": a["L2_xattn_Wq"].T, "w2xk": a["L2_xattn_Wk"].T,
        "w2xv": a["L2_xattn_Wv"].T, "w2xo": slots(a["L2_xattn_Wo"].T), "w2f1": a["L2_ffn_W1"].T,
        "w2f2": a["L2_ffn_W2"].T, "b2f1": columns(a["L2_ffn_b1"]), "row_b2": rows(a["L2_ffn_b2"]),
        "w3q": w3[:, 0], "w3k": w3[:, 1], "w3v": w3[:, 2], "w3q_rot": half_swapped(w3[:, 0]),
        "w3k_rot": half_swapped(w3[:, 1]), "rb_q": columns(b3[0]), "rb_k": columns(b3[1]),
        "rb_q_rot": columns(half_swapped(b3[0])), "rb_k_rot": columns(half_swapped(b3[1])),
        "row_v3": rows(b3[2]), "w3o": slots(a["L3_attn_W_out"]), "row_o3": rows(a["L3_attn_b_out"]),
        "cos": np.tile(cos, (P // DH, 1)), "sin": np.tile(sin, (P // DH, 1)),
        "gate_w": a["L3_ffn_gate_w"].T, "expert_bias": rows(a["L3_ffn_expert_bias"]),
        "w1e": np.concatenate([a["L3_ffn_w1"], sw("w1")]).transpose(0, 2, 1),
        "w3e": np.concatenate([a["L3_ffn_w3"], sw("w3")]).transpose(0, 2, 1),
        "w2e": np.concatenate([a["L3_ffn_w2"], a["L3_ffn_sw2"].reshape(D, 2, FF3).transpose(1, 0, 2)])
                 .transpose(0, 2, 1),
        "b1e": np.concatenate([a["L3_ffn_b1"], a["L3_ffn_sb1"].reshape(2, FF3)]).T,
        "b3e": np.concatenate([a["L3_ffn_b3"], a["L3_ffn_sb3"].reshape(2, FF3)]).T,
        "b2e": a["L3_ffn_b2"], "sb2": rows(np.tile(a["L3_ffn_sb2"], 2)),
        "iota": rows(np.arange(NE, dtype=f)),
    }


def kernel(**inputs):
    import concourse.bacc as bacc
    from concourse.bass_utils import run_bass_kernel_spmd

    nc = bacc.Bacc("TRN2", target_bir_lowering=False, num_devices=1)
    arrays, dram = {}, {}
    for name, a in laid_out({k: np.asarray(v) for k, v in inputs.items()}).items():
        a = np.ascontiguousarray(a)
        arrays["in_" + name] = a
        dram[name] = nc.dram_tensor("in_" + name, a.shape, mybir.dt.from_np(a.dtype), kind="ExternalInput").ap()
    out = nc.dram_tensor("out_x", (NB, SEQ, D), F32, kind="ExternalOutput").ap()
    program(nc, dram, out)
    r = run_bass_kernel_spmd(nc, [arrays], core_ids=[0])
    return r.results[0]["out_x"]
```
